# Optimizing a Trainium2 kernel written in Bass

```python
import numpy as np
import jax
import jax.numpy as jnp

def _softmax(x, axis=-1):
    return jax.nn.softmax(x, axis=axis)

def _gelu(x):
    return jax.nn.gelu(x, approximate=True)

def _silu(x):
    return jax.nn.silu(x)

def _sigmoid(x):
    return jax.nn.sigmoid(x)

def _layernorm(x, axis=-1, eps=1e-05):
    m = jnp.mean(x, axis=axis, keepdims=True)
    v = jnp.var(x, axis=axis, keepdims=True)
    return (x - m) / jnp.sqrt(v + eps)

def _scatter_add(tgt, idx, src, axis=0):
    return tgt.at[idx].add(src)

def _segment_sum(src, seg, n):
    return jax.ops.segment_sum(src, seg, n)
kernel_name = 'mk_xattn_ffn_d1_seqx_r4_5dd2bf'

def setup_inputs(seed: int=0):
    np.random.seed(seed)
    _w = jnp.asarray

    def _rec_inputs():
        import jax
        import jax.numpy as jnp
        _rk = jax.random.key(seed)
        x = 7.22e-05 + 1 * jax.random.normal(jax.random.fold_in(_rk, 1), (4, 1024, 256), jnp.float32)
        _lenS = 1024 - jax.random.randint(jax.random.fold_in(_rk, 7), (4,), 0, max(1, 1024 // 4) + 1, jnp.int32)
        _lenS2 = 154 - jax.random.randint(jax.random.fold_in(_rk, 8), (4,), 0, max(1, 154 // 4) + 1, jnp.int32)
        _ctx_1024P = jax.random.normal(jax.random.fold_in(_rk, 11), (4, 16, 256), jnp.float32)
        _ctx_1024c = jax.random.dirichlet(jax.random.fold_in(_rk, 511), 0.3 * jnp.ones((16,), jnp.float32), (4, 154))
        _ctx_1024t = jnp.einsum('bsk,bkd->bsd', _ctx_1024c, _ctx_1024P)
        _ctx_1024t = _ctx_1024t * jax.lax.rsqrt(jnp.mean(jnp.square(_ctx_1024t)) + 1e-12) * 0.953939
        ctx_1024 = 4.13588e-05 + 0.999923 * (_ctx_1024t + 0.3 * jax.random.normal(jax.random.fold_in(_rk, 611), (4, 154, 256), jnp.float32))
        return (x, ctx_1024)
    x, ctx_1024 = _rec_inputs()

    def _L0_xattn_setup():
        import jax, jax.numpy as jnp
        import numpy as np
        B, S, D, H = (4, 512, 256, 16)
        HD = D // H
        key = jax.random.key(seed)
        ks = jax.random.split(key, 11)
        s = 1.0 / np.sqrt(D)
        return {'query': jax.random.normal(ks[0], (B, S, D), jnp.float32), 'key': jax.random.normal(ks[1], (B, S, D), jnp.float32), 'value': jax.random.normal(ks[2], (B, S, D), jnp.float32), 'Wq': jax.random.normal(ks[3], (D, D), jnp.float32) * s, 'bq': jax.random.normal(ks[4], (D,), jnp.float32) * s, 'Wk': jax.random.normal(ks[5], (D, D), jnp.float32) * s, 'bk': jax.random.normal(ks[6], (D,), jnp.float32) * s, 'Wv': jax.random.normal(ks[7], (D, D), jnp.float32) * s, 'bv': jax.random.normal(ks[8], (D,), jnp.float32) * s, 'Wo': jax.random.normal(ks[9], (D, D), jnp.float32) * s, 'bo': jax.random.normal(ks[10], (D,), jnp.float32) * s}
    _L0_xattn_all = _L0_xattn_setup()
    _L0_xattn_in = {k: v for k, v in _L0_xattn_all.items() if k in ('Wq', 'bq', 'Wk', 'bk', 'Wv', 'bv', 'Wo', 'bo')}
    del _L0_xattn_all

    def _L0_ffn_setup():
        import jax, jax.numpy as jnp
        import numpy as np
        D_MODEL = 256
        N_EXPERTS = 8
        TOP_K = 2
        key = jax.random.key(seed)
        k1, k2, k3, k4 = jax.random.split(key, 4)
        B, S, D, E = (4, 512, D_MODEL, N_EXPERTS)
        dff = 4 * D
        lim = float(np.sqrt(6.0 / (D + dff)))
        return {'x': jax.random.normal(k1, (B, S, D), dtype=jnp.float32), 'router_w': jax.random.normal(k2, (D, E), dtype=jnp.float32) * (1.0 / np.sqrt(D)), 'router_b': jnp.zeros((E,), dtype=jnp.float32), 'expert_up': jax.random.uniform(k3, (E, dff, D), dtype=jnp.float32, minval=-lim, maxval=lim), 'expert_down': jax.random.uniform(k4, (E, D, dff), dtype=jnp.float32, minval=-lim, maxval=lim)}
    _L0_ffn_all = _L0_ffn_setup()
    _L0_ffn_in = {k: v for k, v in _L0_ffn_all.items() if k in ('router_w', 'router_b', 'expert_up', 'expert_down')}
    del _L0_ffn_all
    return {'x': x, 'ctx_1024': ctx_1024, 'L0_xattn_Wq': _L0_xattn_in['Wq'], 'L0_xattn_bq': _L0_xattn_in['bq'], 'L0_xattn_Wk': _L0_xattn_in['Wk'], 'L0_xattn_bk': _L0_xattn_in['bk'], 'L0_xattn_Wv': _L0_xattn_in['Wv'], 'L0_xattn_bv': _L0_xattn_in['bv'], 'L0_xattn_Wo': _L0_xattn_in['Wo'], 'L0_xattn_bo': _L0_xattn_in['bo'], 'L0_ffn_router_w': _L0_ffn_in['router_w'], 'L0_ffn_router_b': _L0_ffn_in['router_b'], 'L0_ffn_expert_up': _L0_ffn_in['expert_up'], 'L0_ffn_expert_down': _L0_ffn_in['expert_down']}

def reference(x, ctx_1024, L0_xattn_Wq, L0_xattn_bq, L0_xattn_Wk, L0_xattn_bk, L0_xattn_Wv, L0_xattn_bv, L0_xattn_Wo, L0_xattn_bo, L0_ffn_router_w, L0_ffn_router_b, L0_ffn_expert_up, L0_ffn_expert_down):
    import jax
    import jax.numpy as jnp

    def _L0_xattn_ref(query, key, value, Wq, bq, Wk, bk, Wv, bv, Wo, bo):
        import jax, jax.numpy as jnp
        import numpy as np
        B, S, D, H = (4, 512, 256, 16)
        HD = D // H
        b = query.shape[0]
        q = (query @ Wq.T + bq).reshape(b, -1, H, HD).transpose(0, 2, 1, 3)
        k = (key @ Wk.T + bk).reshape(b, -1, H, HD).transpose(0, 2, 1, 3)
        v = (value @ Wv.T + bv).reshape(b, -1, H, HD).transpose(0, 2, 1, 3)
        scores = jnp.einsum('bhqd,bhkd->bhqk', q, k) / jnp.sqrt(jnp.float32(HD))
        attn = jax.nn.softmax(scores, axis=-1)
        out = jnp.einsum('bhqk,bhkd->bhqd', attn, v)
        out = out.transpose(0, 2, 1, 3).reshape(b, -1, D)
        return out @ Wo.T + bo

    def _L0_ffn_ref(x, router_w, router_b, expert_up, expert_down):
        import jax, jax.numpy as jnp
        import numpy as np
        D_MODEL = 256
        N_EXPERTS = 8
        TOP_K = 2
        B, S, D = x.shape
        E = expert_up.shape[0]
        x_flat = x.reshape(-1, D)
        logits = x_flat @ router_w + router_b
        probs = jax.nn.softmax(logits, axis=-1)
        top_w, top_idx = jax.lax.top_k(probs, TOP_K)
        comb = jnp.sum(top_w[..., None] * jax.nn.one_hot(top_idx, E, dtype=x.dtype), axis=1)
        output = jnp.zeros_like(x_flat)
        for e in range(E):
            h = jax.nn.gelu(x_flat @ expert_up[e].T, approximate=False)
            out_e = h @ expert_down[e].T
            output = output + comb[:, e:e + 1] * out_e
        return output.reshape(B, S, D)
    x = x + _L0_xattn_ref(_layernorm(x, axis=-1), ctx_1024, ctx_1024, L0_xattn_Wq, L0_xattn_bq, L0_xattn_Wk, L0_xattn_bk, L0_xattn_Wv, L0_xattn_bv, L0_xattn_Wo, L0_xattn_bo)
    x = x + _L0_ffn_ref(_layernorm(x, axis=-1), L0_ffn_router_w, L0_ffn_router_b, L0_ffn_expert_up, L0_ffn_expert_down)
    return x

_drawn_inputs = setup_inputs


def setup_inputs(seed=0):
    import zlib

    import numpy as np

    out = dict(_drawn_inputs(seed))
    spreads = {'L0_ffn_router_b': (0.0, 0.267)}
    factors = {'L0_xattn_bq': 3.347, 'L0_xattn_bk': 8.0}
    for name, (base, spread) in spreads.items():
        noise = np.random.default_rng([zlib.crc32(name.encode()), seed]).standard_normal(out[name].shape)
        drawn = base * np.exp(spread * noise) if base else spread * noise
        out[name] = jnp.asarray(drawn.astype(out[name].dtype))
    for name, factor in factors.items():
        out[name] = (out[name] * factor).astype(out[name].dtype)
    return out
```

```python
from contextlib import ExitStack

import concourse.bass as bass
from concourse import mybir

P = 128
B, S, D = 4, 1024, 256
SK = 154
H, HD = 16, 16
E, F = 8, 1024
DC = D // P
TOKENS = B * S
TILES = TOKENS // P
PAIRS = TILES // 2
BATCH_TILES = S // P
BATCH_PAIRS = BATCH_TILES // 2
EPS = 1e-5

HALF = H // DC * SK
COLS = H * SK
CHUNKS = -(-COLS // P)
PADDED = CHUNKS * P
GROUPS = [(c, o, n) for c in range(DC) for o, n in ((0, 3), (3, 3), (6, 2))]
SLOTS = 3
TURNS = CHUNKS // 4
VH = HD + 1
VCOLS = 3 * 2 * VH
KREST = SK - P

DOWN_AT = DC * F
EW = DOWN_AT + F // P * D
LIST = TOKENS
BLOCKS = 2 * TOKENS // P + E - 1
STEPS = (BLOCKS + 1) // 2 * 2
LIST_ROWS = E * LIST + 8 * P
NOBODY = 2.0 * TOKENS
EARLY = 4

C_ID, C_TRI, C_HM, C_DESC, C_BASE, C_TOK, C_J, C_M = 0, 128, 256, 264, 272, 280, 288, 288 + STEPS
C_ALL = C_M + 32
SELW = 282

F32 = mybir.dt.float32
F16 = mybir.dt.float16
BF16 = mybir.dt.bfloat16
I32 = mybir.dt.int32
ALU = mybir.AluOpType
ACT = mybir.ActivationFunctionType
AX = mybir.AxisListType

LN1_STEPS = 3
ROUTE_STEPS = 24
V_STEPS = 10


def bass_xattn_moe(nc, x, ctxT, wqT, bq, wkT, bk, wvT, bv, woT, bo, wr, br, upT, dnT, cst_in, sel_in, out):
    with ExitStack() as ctx:
        def sb(name, shape, dt=F32):
            return ctx.enter_context(nc.sbuf_tensor(name, shape, dt))

        def sem(name):
            return ctx.enter_context(nc.semaphore(name))

        v_dram = nc.dram_tensor("v_dram", [B, P, CHUNKS * VCOLS], BF16, kind="Internal").ap()
        n2_dram = nc.dram_tensor("n2_dram", [TOKENS, D], F32, kind="Internal").ap()
        list_dram = nc.dram_tensor("list_dram", [LIST_ROWS, 2], F32, kind="Internal").ap()

        x_tiles = x.rearrange("b (n p) d -> (b n) p d", p=P)
        out_rows = out.rearrange("b s d -> (b s) d")

        W = sb("W", [P, E * EW])
        tmp = W[:, EARLY * EW:(EARLY + 1) * EW]
        ctx_sb = tmp[:, 0:DC * B * SK].rearrange("p (c b k) -> p c b k", c=DC, b=B)
        kT = tmp[:, 1232:1232 + DC * B * SK].rearrange("p (c b k) -> p c b k", c=DC, b=B)
        sel_f = tmp[:, 2464:2464 + 4 * SELW].rearrange("p (a x) -> p a x", a=4)
        KB = W[:, (EARLY + 1) * EW:(EARLY + 1) * EW + B * COLS]
        tmp2 = W[:, (EARLY + 1) * EW + B * COLS:E * EW]
        wk_sb = tmp2[:, 0:512].rearrange("p (c n) -> p c n", c=DC)
        wv_sb = tmp2[:, 512:1024].rearrange("p (c n) -> p c n", c=DC)
        v_st = tmp2[:, 1024:1024 + CHUNKS * VCOLS // 2].bitcast(BF16)

        cst = sb("cst", [P, C_ALL])
        ident = cst[:, C_ID:C_ID + P]
        tri = sb("tri", [P, P], BF16)
        ones = sb("ones", [P, P], BF16)
        sel = sb("sel", [P, 4, SELW], BF16)
        wq_sb = sb("wq_sb", [P, DC, D])
        wo_sb = sb("wo_sb", [P, DC, D])
        wr_sb = sb("wr_sb", [P, DC, E])
        bq_sb = sb("bq_sb", [P, DC])
        bk_sb = sb("bk_sb", [P, DC])
        br_sb = sb("br_sb", [E, 1])
        bo_bc = sb("bo_bc", [P, D])
        bv_bc = sb("bv_bc", [P, D])
        v_f = sb("v_f", [P, D])
        v_r = sb("v_r", [P, D])
        vp = [sb("vp0", [P, 3, H, VH], BF16), sb("vp1", [KREST, 3, H, VH], BF16)]
        half_pow = sb("half_pow", [P, 2])
        eps = sb("eps", [P, 2])
        gate = sb("gate", [P, 2])

        xt = sb("xt", [P, 2, D])
        xn = sb("xn", [P, 2, D])
        xnT = sb("xnT", [P, 2, DC, P])
        qT = sb("qT", [P, DC, 2 * P])
        st1 = sb("st1", [P, 2, 6])
        mv1 = sb("mv1", [P, 2, 2])
        rs1 = sb("rs1", [P, 2])
        mx = sb("mx", [P, H])
        SX = sb("SX", [P, 2, PADDED])
        hi = sb("hi", [P, PADDED], F16)
        lo = sb("lo", [P, PADDED], F16)
        Vc = sb("Vc", [P, 2, CHUNKS * VCOLS], BF16)
        rden = sb("rden", [P, H])
        attn = sb("attn", [P, D])
        atT = sb("atT", [P, DC, P])
        xr = sb("xr", [P, 2, D])
        x2 = sb("x2", [P, 2, D])
        st2 = sb("st2", [P, 6])
        mv2 = sb("mv2", [P, 2])
        rs2 = sb("rs2", [P, 2])
        n2 = sb("n2", [P, 2, D])
        n2T = sb("n2T", [P, DC, 2 * P])
        lgT = sb("lgT", [E, 2 * P])
        Lg = sb("Lg", [P, BATCH_TILES * E])

        T8 = BATCH_TILES
        rt = sb("rt", [P, 8, T8, E])
        rs = sb("rs", [P, 8, T8])
        Mb = sb("Mb", [P, T8, E], BF16)
        cnt = sb("cnt", [P, E])
        tok = sb("tok", [P, T8])
        ent = sb("ent", [P, T8, 2, 2])
        pos = sb("pos", [P, 2, T8], I32)

        meta = sb("meta", [1, 4, STEPS])
        blk = sb("blk", [1, 4, E])
        exw = sb("exw", [1, STEPS], I32)
        off = sb("off", [1, STEPS], I32)
        lst = sb("lst", [P, 2, 2])
        idg = sb("idg", [P, 2, 1], I32)
        ids = sb("ids", [P, 2, 1], I32)
        xg = hi[:, 0:4 * D].bitcast(F32).rearrange("p (s d) -> p s d", s=2)
        xgT = hi[:, 4 * D:8 * D].bitcast(F32).rearrange("p (s c k) -> p s c k", s=2, c=DC)
        hh = SX[:, :, 0:F]
        hT = SX[:, :, F:2 * F]
        y = lo[:, 0:4 * D].bitcast(F32).rearrange("p (s d) -> p s d", s=2)

        banks = ctx.enter_context(nc.psum_tensor("banks", [P, 8, 512], F32))
        SC = [banks[:, s, :] for s in range(SLOTS)]
        PT = [banks[:, 3 + s, :] for s in range(2)]
        O = banks[:, 5, :]
        TR = banks[:, 6, :]
        PJ = banks[:, 7, :]
        UP = [[banks[:, 2 * s + u, :] for u in range(2)] for s in range(2)]
        HTp = [banks[:, 4 + s, :] for s in range(2)]
        XTp = banks[:, 6, :]
        Y = banks[:, 7, :]

        cst_in_s = sem("constants_loaded")
        ctx_in = sem("context_and_wk_loaded")
        wv_in = sem("wv_loaded")
        wts_in = sem("attention_weights_loaded")
        experts_in = sem("experts_loaded")
        init_done = sem("constants_made")
        k_ps = sem("k_in_psum")
        kT_done = sem("kT_done")
        KB_done = sem("KB_done")
        v_ps = sem("v_in_psum")
        v_step = sem("value_parts_step")
        vsel_ps = sem("chunk_values_in_psum")
        vst_a = sem("chunk_values_by_act")
        vst_d = sem("chunk_values_by_dve")
        v_stored = sem("chunk_values_stored")
        list_set = sem("list_filler_made")
        list_init = sem("lists_filled")
        x_loaded = sem("x_loaded")
        ln1_step = sem("ln1_step")
        ln1_rstd = sem("ln1_rstd")
        tr_full, tr_empty = sem("turned_in_psum"), sem("turned_taken")
        pj_full, pj_empty = sem("projected_in_psum"), sem("projected_taken")
        s_full, s_max, s_empty = sem("scores_in_psum"), sem("score_max"), sem("scores_taken")
        exp_done = sem("exp_done")
        pt_full, hi_done, pt_empty = sem("probs_turned"), sem("hi_done"), sem("lo_done")
        vc_loaded = [sem("vc_loaded0"), sem("vc_loaded1")]
        pv_done = sem("pv_done")
        rden_done, attn_done = sem("denominators"), sem("attn_done")
        xr_loaded = [sem("residual_loaded0"), sem("residual_loaded1")]
        xr_ready = sem("residual_ready")
        ln2_step, ln2_rstd, n2_done = sem("ln2_step"), sem("ln2_rstd"), sem("n2_done")
        x2_stored, n2_stored = sem("x2_stored"), sem("n2_stored")
        lg_done = sem("logits_ready")
        rt_exp = sem("router_exp")
        rt_step = sem("routing_step")
        scattered = sem("lists_scattered")
        meta_step = sem("block_table_step")
        gate_step = sem("gate_step")
        lst_loaded = [sem("rows_loaded0"), sem("rows_loaded1")]
        ids_ready = sem("ids_ready")
        gathered = [sem("gathered0"), sem("gathered1")]
        xt_full, xt_empty = sem("tokens_turned"), sem("tokens_taken")
        up_full, gelu_done = sem("up_in_psum"), sem("gelu_done")
        ht_full, ht_dve, ht_act = sem("hidden_turned"), sem("hidden_taken_dve"), sem("hidden_taken_act")
        y_full, y_done = sem("down_in_psum"), sem("y_done")
        added = sem("rows_added")

        META_STEPS = 11

        def tr_use(i, pos_, last=False):
            return 2 + 5 * i + pos_ - (1 if last else 0)

        def pj_use(i, b, pos_, last=False):
            return 2 + 5 * i + b + pos_ - (1 if last else 0)

        block = ctx.enter_context(nc.Block())

        @block.sync
        def _(sp):
            nc.sync.sem_inc(x2_stored, 16)
            nc.sync.sem_inc(n2_stored, 16)
            sp.dma_start(ctx_sb, ctxT.rearrange("(c p) b k -> p c b k", p=P)).then_inc(ctx_in, 16)
            sp.dma_start(wk_sb, wkT.rearrange("(c p) n -> p c n", p=P)).then_inc(ctx_in, 16)
            sp.dma_start(bk_sb[:], bk).then_inc(ctx_in, 16)
            sp.dma_start(cst[:], cst_in).then_inc(cst_in_s, 16)
            sp.dma_start(sel_f, sel_in).then_inc(cst_in_s, 16)
            sp.dma_start(wv_sb, wvT.rearrange("(c p) n -> p c n", p=P)).then_inc(wv_in, 16)
            sp.dma_start(bv_bc[:], bv.unsqueeze(0).broadcast_to([P, D])).then_inc(wv_in, 16)

            def load_x(p):
                if not isinstance(p, int) or p > 0:
                    sp.wait_ge(ln1_step, LN1_STEPS * p)
                sp.dma_start(xt[:], x_tiles[bass.ds(p * 2, 2)].rearrange("t p d -> p t d")).then_inc(x_loaded, 16)

            load_x(0)
            sp.dma_start(wq_sb[:], wqT.rearrange("(c p) n -> p c n", p=P)).then_inc(wts_in, 16)
            sp.dma_start(wo_sb[:], woT.rearrange("(c p) n -> p c n", p=P)).then_inc(wts_in, 16)
            sp.dma_start(wr_sb[:], wr.rearrange("(c p) n -> p c n", p=P)).then_inc(wts_in, 16)
            sp.dma_start(bq_sb[:], bq).then_inc(wts_in, 16)
            sp.dma_start(br_sb[:], br).then_inc(wts_in, 16)
            sp.dma_start(bo_bc[:], bo.unsqueeze(0).broadcast_to([P, D])).then_inc(wts_in, 16)

            for b in range(B):
                sp.wait_ge(vst_a, 2 * (b + 1))
                sp.wait_ge(vst_d, 2 * (b + 1))
                if b > 0:
                    sp.wait_ge(v_stored, 16 * b)
                sp.dma_start(v_dram[b], v_st).then_inc(v_stored, 16)
            sp.wait_ge(v_stored, 16 * B)

            def load_vc(k, par, kpair, first=False):
                if not first:
                    sp.wait_ge(pv_done, TURNS * (k - 1))
                sp.dma_start(Vc[:, par, :], v_dram[bass.ds(k // BATCH_TILES, 1)].rearrange("o p n -> p (o n)")).then_inc(vc_loaded[par], 16)

            def load_xr(m, par, first=False):
                if not first:
                    sp.wait_ge(ln2_step, 2 * (m - 1))
                sp.dma_start(xr[:, par, :], x_tiles[bass.ds(m, 1)].rearrange("o p d -> p (o d)")).then_inc(xr_loaded[par], 16)

            def store(m, par):
                sp.wait_ge(n2_done, m + 1)
                sp.wait_ge(x2_stored, 16 * m + 16)
                sp.wait_ge(n2_stored, 16 * m + 16)
                sp.dma_start(out_rows[bass.ds(m * P, P)], x2[:, par, :]).then_inc(x2_stored, 16)
                sp.dma_start(n2_dram[bass.ds(m * P, P)], n2[:, par, :]).then_inc(n2_stored, 16)

            load_x(1)
            for par in range(2):
                load_vc(par, par, 0, first=True)
                load_xr(par, par, first=True)

            def body(i, more=True, next_x=True):
                m = i * 2
                for par in range(2):
                    if par == 0 and next_x:
                        load_x(i + 2)
                    store(m + par, par)
                    if more:
                        load_xr(m + par + 2, par)
                        load_vc(m + par + 2, par, 0)

            with sp.Fori(0, PAIRS - 2) as i:
                body(i)
            body(PAIRS - 2, next_x=False)
            body(PAIRS - 1, more=False, next_x=False)

            sp.wait_ge(s_full, 6 * TILES)
            for e in range(EARLY, E):
                sp.dma_start(W[:, e * EW:e * EW + DOWN_AT].rearrange("p (c f) -> p c f", c=DC), upT[e].rearrange("(c p) f -> p c f", p=P)).then_inc(experts_in, 16)
                sp.dma_start(W[:, e * EW + DOWN_AT:(e + 1) * EW].rearrange("p (k d) -> p k d", d=D), dnT[e].rearrange("(k p) d -> p k d", p=P)).then_inc(experts_in, 16)

            sp.wait_ge(meta_step, META_STEPS)
            sp.wait_ge(scattered, 16 * 2 * TILES)

            def load_rows(t, par, first=False):
                v = sp.value_load(off[0:1, bass.ds(t, 1)], min_val=0, max_val=LIST_ROWS - P)
                if not first:
                    sp.wait_ge(y_done, t - 1)
                sp.dma_start(lst[:, par, :], list_dram[bass.ds(v, P)]).then_inc(lst_loaded[par], 16)

            load_rows(0, 0, first=True)
            load_rows(1, 1, first=True)
            with sp.Fori(1, STEPS // 2) as s:
                load_rows(s * 2, 0)
                load_rows(s * 2 + 1, 1)
            sp.wait_ge(x2_stored, 16 * (TILES + 1))
            sp.wait_ge(n2_stored, 16 * (TILES + 1))
            sp.wait_ge(v_stored, 16 * B)
            sp.wait_ge(added, 16 * STEPS)

        @block.gpsimd
        def _(pool):
            nc.gpsimd.memset(half_pow[:], -0.5).then_inc(init_done, 1)
            nc.gpsimd.memset(eps[:], EPS).then_inc(init_done, 1)
            nc.gpsimd.memset(gate[:], 0.0).then_inc(init_done, 1)
            filler = SX[:, 1, 0:2 * LIST_ROWS // P].rearrange("p (n a) -> p n a", a=2)
            nc.gpsimd.memset(filler[:, :, 0], NOBODY).then_inc(list_set, 1)
            nc.gpsimd.memset(filler[:, :, 1], 0.0).then_inc(list_set, 1)
            pool.wait_ge(list_set, 2)
            pool.dma_start(list_dram.rearrange("(p n) a -> p n a", p=P), filler).then_inc(list_init, 16)
            pool.wait_ge(list_init, 16)
            nc.gpsimd.memset(SX[:, 1, COLS:PADDED], 0.0).then_inc(init_done, 1)
            nc.gpsimd.memset(SX[:, 0, COLS:PADDED], 0.0).then_inc(init_done, 1)
            pool.wait_ge(init_done, 5)
            pool.wait_ge(wts_in, 96)

            def gate_op(nth):
                pool.wait_ge(gate_step, nth)
                nc.gpsimd.tensor_tensor(gate[:, 1:2], gate[:, 0:1], gate[:, 0:1], ALU.add).then_inc(gate_step, 1)

            def rstd1(p):
                pool.wait_ge(ln1_step, LN1_STEPS * p + 2)
                nc.gpsimd.tensor_tensor(rs1[:], mv1[:, :, 1], eps[:], ALU.add).then_inc(ln1_rstd, 1)
                pool.wait_ge(ln1_rstd, 2 * p + 1)
                nc.gpsimd.tensor_tensor(rs1[:], rs1[:], half_pow[:], ALU.pow).then_inc(ln1_rstd, 1)

            def residual(m, par, nth):
                pool.wait_ge(xr_loaded[par], 16 * (nth + 1))
                nc.gpsimd.tensor_tensor(xr[:, par, :], xr[:, par, :], bo_bc[:], ALU.add).then_inc(xr_ready, 1)

            def rstd2(m):
                pool.wait_ge(ln2_step, 2 * m + 2)
                nc.gpsimd.tensor_tensor(rs2[:, 0:1], mv2[:, 1:2], eps[:, 0:1], ALU.add).then_inc(ln2_rstd, 1)
                pool.wait_ge(ln2_rstd, 2 * m + 1)
                nc.gpsimd.tensor_tensor(rs2[:, 1:2], rs2[:, 0:1], half_pow[:, 0:1], ALU.pow).then_inc(ln2_rstd, 1)

            def scatter(b):
                pool.wait_ge(rt_step, ROUTE_STEPS * (b + 1))
                gate_op(b)
                for t in range(T8):
                    for k in range(2):
                        pool.indirect_dma_start(
                            out=list_dram, out_offset=bass.IndirectOffsetOnAxis(ap=pos[:, k, t:t + 1], axis=0),
                            in_=ent[:, t, k, :], in_offset=None).then_inc(scattered, 16)

            rstd1(0)
            rstd1(1)

            def body(i, next_x=True):
                for par in range(2):
                    residual(i * 2 + par, par, i)
                    rstd2_at = i * 2 + par
                    if par == 1 and next_x:
                        rstd1(i + 2)
                    rstd2(rstd2_at)

            with pool.Fori(0, B - 1) as b:
                with pool.Fori(0, BATCH_PAIRS) as j:
                    body(b * BATCH_PAIRS + j)
                scatter(b)
            with pool.Fori(0, BATCH_PAIRS - 2) as j:
                body((B - 1) * BATCH_PAIRS + j)
            body(PAIRS - 2, next_x=False)
            body(PAIRS - 1, next_x=False)
            scatter(B - 1)

            pool.wait_ge(n2_stored, 16 * (TILES + 1))
            pool.wait_ge(x2_stored, 16 * (TILES + 1))
            pool.wait_ge(pv_done, TURNS * TILES)

            def gather(t, par, first=False):
                pool.wait_ge(ids_ready, 2 * (t + 1))
                if not first:
                    pool.wait_ge(xt_full, t - 1)
                gate_op(B + t + (0 if first else t - 1))
                pool.indirect_dma_start(
                    out=xg[:, par, :], out_offset=None, in_=n2_dram,
                    in_offset=bass.IndirectOffsetOnAxis(ap=idg[:, par, :], axis=0)).then_inc(gathered[par], 16)

            def add_rows(t, par):
                pool.wait_ge(y_done, t + 1)
                if not isinstance(t, int) or t > 0:
                    pool.wait_ge(added, 16 * t)
                gate_op(B + min(t + 2, STEPS) + t if isinstance(t, int) else B + 2 * t + 2)
                pool.indirect_dma_start(
                    out=out_rows, out_offset=bass.IndirectOffsetOnAxis(ap=ids[:, par, :], axis=0),
                    in_=y[:, par, :], in_offset=None, bounds_check=TOKENS - 1, oob_is_err=False,
                    compute_op=ALU.add).then_inc(added, 16)

            gather(0, 0, first=True)
            gather(1, 1, first=True)
            with pool.Fori(0, STEPS // 2 - 1) as s:
                for par in range(2):
                    add_rows(s * 2 + par, par)
                    gather(s * 2 + par + 2, par)
            add_rows(STEPS - 2, 0)
            add_rows(STEPS - 1, 1)

        @block.tensor
        def _(pe):
            mm = nc.tensor.matmul
            pe.wait_ge(ctx_in, 48)
            for f in range(DC):
                for h in range(2):
                    for c in range(DC):
                        last = mm(banks[:, 2 * f + h, 0:2 * SK], wk_sb[:, c, f * P:(f + 1) * P],
                                  ctx_sb[:, c, 2 * h:2 * h + 2, :], start=c == 0, stop=c == DC - 1)
                    last.then_inc(k_ps, 1)
            pe.wait_ge(wv_in, 32)
            for b in range(B):
                for kb, n in ((0, P), (1, KREST)):
                    for c in range(DC):
                        last = mm(banks[0:n, 4 + b, kb * D:(kb + 1) * D], ctx_sb[:, c, b, kb * P:kb * P + n],
                                  wv_sb[:, c, :], start=c == 0, stop=c == DC - 1)
                    last.then_inc(v_ps, 1)
            for b in range(B):
                pe.wait_ge(v_step, V_STEPS * (b + 1))
                if b == 0:
                    pe.wait_ge(kT_done, 4)
                else:
                    pe.wait_ge(vst_a, 2 * b)
                    pe.wait_ge(vst_d, 2 * b)
                for c in range(CHUNKS):
                    h0, k0 = divmod(P * c, SK)
                    for slot in range(2):
                        h = min(h0 + slot, H - 1)
                        o = banks[:, c // 5, (c % 5) * VCOLS:(c % 5 + 1) * VCOLS].rearrange(
                            "p (a s v) -> p a s v", a=3, s=2)[:, :, slot, :]
                        for kb, n in ((0, P), (1, KREST)):
                            last = mm(o, sel[0:n, 2 * kb + slot, k0:k0 + P], vp[kb][:, :, h, :],
                                      start=kb == 0 and slot == 0 and c % 5 == 0, stop=kb == 1, skip_group_check=True)
                    if c % 5 == 4:
                        last.then_inc(vsel_ps, 1)

            def turn_x(p, use):
                pe.wait_ge(ln1_step, LN1_STEPS * (p + 1))
                pe.wait_ge(tr_empty, use)
                for t in range(2):
                    for c in range(DC):
                        last = nc.tensor.transpose(TR[:, (2 * t + c) * P:(2 * t + c + 1) * P],
                                                   xn[:, t, c * P:(c + 1) * P], ident)
                last.then_inc(tr_full, 1)

            def project_q(tr, use):
                pe.wait_ge(tr_empty, tr + 1)
                pe.wait_ge(pj_empty, use)
                for f in range(DC):
                    for c in range(DC):
                        last = mm(PJ[:, f * 2 * P:(f + 1) * 2 * P], wq_sb[:, c, f * P:(f + 1) * P],
                                  xnT[:, :, c, :], start=c == 0, stop=c == DC - 1, skip_group_check=True)
                last.then_inc(pj_full, 1)

            def scores(n, par, batch, g, first=False):
                c, h, w = GROUPS[g]
                if not (first and g < SLOTS):
                    pe.wait_ge(s_empty, 6 * n + g - 2)
                mm(SC[g % SLOTS][:, 0:w * SK], qT[:, c, par * P:(par + 1) * P],
                   KB[:, bass.ds(batch * COLS + (c * HALF + h * SK), w * SK)],
                   start=True, stop=True).then_inc(s_full, 1)

            def turn_probs(k, par, j, first=False):
                pe.wait_ge(exp_done, 2 * k + (1 if (j + 1) * 4 * P <= HALF else 2))
                if not (first and j < 2):
                    pe.wait_ge(pt_empty, TURNS * k + j - 1)
                for c in range(4):
                    last = nc.tensor.transpose(PT[(par + j) % 2][:, c * P:(c + 1) * P],
                                               SX[:, par, (4 * j + c) * P:(4 * j + c + 1) * P], ident)
                last.then_inc(pt_full, 1)

            def weigh(k, par, j, nth):
                pe.wait_ge(pt_empty, TURNS * k + j + 1)
                if j == 0:
                    pe.wait_ge(vc_loaded[par], 16 * (nth + 1))
                    pe.wait_ge(attn_done, k)
                for c in range(4 * j, 4 * j + 4):
                    h0 = P * c // SK
                    w = VH if h0 == H - 1 else 2 * VH
                    for n, (probs, part) in enumerate(((hi, 0), (hi, 1), (hi, 2), (lo, 0), (lo, 1))):
                        at = c * VCOLS + part * 2 * VH
                        last = mm(O[:, h0 * VH:h0 * VH + w], probs[:, c * P:(c + 1) * P],
                                  Vc[:, par, at:at + w], start=c == 0 and n == 0,
                                  stop=c == CHUNKS - 1 and n == 4, skip_group_check=True)
                last.then_inc(pv_done, 1)

            def turn_attn(m, use):
                pe.wait_ge(attn_done, m + 1)
                pe.wait_ge(tr_empty, use)
                for c in range(DC):
                    last = nc.tensor.transpose(TR[:, c * P:(c + 1) * P], attn[:, c * P:(c + 1) * P], ident)
                last.then_inc(tr_full, 1)

            def project_out(tr, use):
                pe.wait_ge(tr_empty, tr + 1)
                pe.wait_ge(pj_empty, use)
                for c in range(DC):
                    last = mm(PJ[:, 0:D], atT[:, c, :], wo_sb[:, c, :], start=c == 0, stop=c == DC - 1)
                last.then_inc(pj_full, 1)

            def turn_n2(m, par, use):
                pe.wait_ge(n2_done, m + 1)
                pe.wait_ge(tr_empty, use)
                for c in range(DC):
                    last = nc.tensor.transpose(TR[:, c * P:(c + 1) * P], n2[:, par, c * P:(c + 1) * P], ident)
                last.then_inc(tr_full, 1)

            def logits(tr, use):
                pe.wait_ge(tr_empty, tr + 1)
                pe.wait_ge(pj_empty, use)
                for c in range(DC):
                    last = mm(PJ[0:E, 0:2 * P], wr_sb[:, c, :], n2T[:, c, :], start=c == 0, stop=c == DC - 1)
                last.then_inc(pj_full, 1)

            def turn_logits():
                for t in range(2):
                    last = nc.tensor.transpose(PJ[:, t * E:(t + 1) * E], lgT[:, t * P:(t + 1) * P], ident[0:E, 0:E])
                last.then_inc(pj_full, 1)

            def count_experts(b, use):
                pe.wait_ge(rt_step, ROUTE_STEPS * b + 17)
                pe.wait_ge(pj_empty, use)
                mm(PJ[:, 0:T8 * E], tri[:], Mb[:].rearrange("p t e -> p (t e)"), start=True, stop=False, skip_group_check=True)
                for t in range(T8):
                    last = mm(PJ[:, (t + 1) * E:(T8 + 1) * E].rearrange("p (t e) -> p t e", e=E), ones[:],
                              Mb[:, t, :].unsqueeze(1).broadcast_to([P, T8 - t, E]),
                              start=False, stop=t == T8 - 1, skip_group_check=True)
                last.then_inc(pj_full, 1)

            def tick(n, k, m, par, i, b, batch_n, first=False, has_s=True, has_x=True, last_pair=False):
                odd = par == 1
                if has_s:
                    scores(n, par, batch_n, 0, first)
                    scores(n, par, batch_n, 1, first)
                if m is not None:
                    turn_attn(m, tr_use(i, 2 * par, last_pair))
                if has_s:
                    scores(n, par, batch_n, 2, first)
                if k is not None:
                    turn_probs(k, 1 - par, 0, first=isinstance(k, int) and k == 0)
                if m is not None:
                    project_out(tr_use(i, 2 * par, last_pair), pj_use(i, b, par, last_pair))
                if has_s:
                    scores(n, par, batch_n, 3)
                nth = None
                if k is not None:
                    nth = i + par
                    turn_probs(k, 1 - par, 1, first=isinstance(k, int) and k == 0)
                    weigh(k, 1 - par, 0, nth)
                if has_s:
                    scores(n, par, batch_n, 4)
                if k is not None:
                    turn_probs(k, 1 - par, 2)
                    weigh(k, 1 - par, 1, nth)
                if has_s:
                    scores(n, par, batch_n, 5)
                if k is not None:
                    turn_probs(k, 1 - par, 3)
                    weigh(k, 1 - par, 2, nth)
                if m is not None:
                    turn_n2(m, par, tr_use(i, 2 * par + 1, last_pair))
                if k is not None:
                    turn_probs(k, 1 - par, 4)
                    weigh(k, 1 - par, 3, nth)
                if odd and m is not None:
                    logits(tr_use(i, 3, last_pair), pj_use(i, b, 2, last_pair))
                if odd and has_x:
                    turn_x(i + 2, tr_use(i, 4))
                if odd and m is not None:
                    pe.wait_ge(pj_empty, pj_use(i, b, 3, last_pair))
                if k is not None:
                    weigh(k, 1 - par, 4, nth)
                if odd and m is not None:
                    turn_logits()
                if odd and has_x:
                    project_q(tr_use(i, 4), pj_use(i, b, 4))

            def body(i, b, **kw):
                n = i * 2 + 2
                batch_n = (i + 1) // BATCH_PAIRS
                tick(n, n - 1, n - 2, 0, i, b, batch_n, **kw)
                if kw.get("has_s", True):
                    tick(n + 1, n, n - 1, 1, i, b, batch_n, **kw)
                else:
                    tick(n + 1, None, n - 1, 1, i, b, batch_n, **kw)

            pe.wait_ge(wts_in, 96)
            pe.wait_ge(cst_in_s, 32)
            turn_x(0, 0)
            project_q(0, 0)
            pe.wait_ge(pj_empty, 1)
            pe.wait_ge(KB_done, 16)
            pe.wait_ge(vst_a, 2 * B)
            pe.wait_ge(vst_d, 2 * B)
            pe.wait_ge(init_done, 5)
            for g in range(6):
                scores(0, 0, 0, g, first=True)
            for g in range(3):
                scores(1, 1, 0, g)
            turn_probs(0, 0, 0, first=True)
            scores(1, 1, 0, 3)
            turn_probs(0, 0, 1, first=True)
            weigh(0, 0, 0, 0)
            scores(1, 1, 0, 4)
            turn_probs(0, 0, 2)
            weigh(0, 0, 1, 0)
            scores(1, 1, 0, 5)
            turn_probs(0, 0, 3)
            weigh(0, 0, 2, 0)
            turn_probs(0, 0, 4)
            weigh(0, 0, 3, 0)
            turn_x(1, 1)
            weigh(0, 0, 4, 0)
            project_q(1, 1)
            with pe.Fori(0, B - 1) as b:
                with pe.Fori(0, BATCH_PAIRS) as j:
                    i = b * BATCH_PAIRS + j
                    pe.wait_ge(pj_empty, pj_use(i, b, 0))
                    body(i, b)
                count_experts(b, pj_use(b * BATCH_PAIRS + BATCH_PAIRS, b, 0))
            b = B - 1
            with pe.Fori(0, BATCH_PAIRS - 2) as j:
                i = b * BATCH_PAIRS + j
                pe.wait_ge(pj_empty, pj_use(i, b, 0))
                body(i, b)
            pe.wait_ge(pj_empty, pj_use(PAIRS - 2, b, 0))
            body(PAIRS - 2, b, has_x=False)
            body(PAIRS - 1, b, has_s=False, has_x=False, last_pair=True)
            count_experts(b, pj_use(PAIRS - 1, b, 4, True))

            pe.wait_ge(pj_empty, pj_use(PAIRS - 1, b, 4, True) + 1)
            pe.wait_ge(meta_step, META_STEPS)
            pe.wait_ge(experts_in, 32 * E)

            def turn_tokens(t, par, nth):
                pe.wait_ge(gathered[par], 16 * (nth + 1))
                if not isinstance(t, int) or t > 0:
                    pe.wait_ge(xt_empty, t)
                for c in range(DC):
                    last = nc.tensor.transpose(XTp[:, c * P:(c + 1) * P], xg[:, par, c * P:(c + 1) * P], ident)
                last.then_inc(xt_full, 1)

            def up(t, par, first=False):
                v = pe.value_load(exw[0:1, bass.ds(t, 1)], min_val=0, max_val=(E - 1) * EW)
                pe.wait_ge(xt_empty, t + 1)
                if not first:
                    pe.wait_ge(gelu_done, 2 * (t - 1))
                for u in range(2):
                    for c in range(DC):
                        last = mm(UP[par][u], xgT[:, par, c, :], W[:, bass.ds(v + (c * F + u * 512), 512)],
                                  start=c == 0, stop=c == DC - 1)
                    last.then_inc(up_full, 1)
                return v

            def turn_hidden(t, par):
                for u in range(2):
                    pe.wait_ge(gelu_done, 2 * t + u + 1)
                    if not isinstance(t, int) or t > 0:
                        pe.wait_ge(ht_dve if u == 0 else ht_act, t)
                    for c in range(4):
                        k = 4 * u + c
                        last = nc.tensor.transpose(HTp[u][:, c * P:(c + 1) * P], hh[:, par, k * P:(k + 1) * P], ident)
                    last.then_inc(ht_full, 1)

            def down(t, par):
                v = pe.value_load(exw[0:1, bass.ds(t, 1)], min_val=0, max_val=(E - 1) * EW)
                for k in range(F // P):
                    if k == 0:
                        pe.wait_ge(ht_dve, t + 1)
                        if not isinstance(t, int) or t > 0:
                            pe.wait_ge(y_done, t)
                    if k == 4:
                        pe.wait_ge(ht_act, t + 1)
                    last = mm(Y[:, 0:D], hT[:, par, k * P:(k + 1) * P], W[:, bass.ds(v + (DOWN_AT + k * D), D)],
                              start=k == 0, stop=k == F // P - 1)
                last.then_inc(y_full, 1)

            turn_tokens(0, 0, 0)
            up(0, 0, first=True)

            def step(t, par, nth_next, first=False):
                turn_tokens(t + 1, 1 - par, nth_next)
                turn_hidden(t, par)
                up(t + 1, 1 - par, first)
                down(t, par)

            step(0, 0, 0, first=True)
            with pe.Fori(0, STEPS // 2 - 1) as s:
                step(s * 2 + 1, 1, s + 1)
                step(s * 2 + 2, 0, s + 1)
            turn_hidden(STEPS - 1, 1)
            down(STEPS - 1, 1)

        @block.scalar
        def _(act):
            A = nc.scalar.activation
            for e in range(EARLY):
                act.dma_start(W[:, e * EW:e * EW + DOWN_AT].rearrange("p (c f) -> p c f", c=DC), upT[e].rearrange("(c p) f -> p c f", p=P)).then_inc(experts_in, 16)
                act.dma_start(W[:, e * EW + DOWN_AT:(e + 1) * EW].rearrange("p (k d) -> p k d", d=D), dnT[e].rearrange("(k p) d -> p k d", p=P)).then_inc(experts_in, 16)
            act.wait_ge(ctx_in, 48)
            for f in range(DC):
                for h in range(2):
                    act.wait_ge(k_ps, 2 * f + h + 1)
                    A(kT[:, f, 2 * h:2 * h + 2, :], banks[:, 2 * f + h, 0:2 * SK].rearrange("p (b k) -> p b k", b=2), ACT.Identity,
                      bias=bk_sb[:, f:f + 1]).then_inc(kT_done, 1)
            for b in range(B):
                for g in range(2):
                    act.wait_ge(vsel_ps, 4 * b + g + 1)
                    if b > 0:
                        act.wait_ge(v_stored, 16 * b)
                    A(v_st[:, g * 5 * VCOLS:(g + 1) * 5 * VCOLS], banks[:, g, 0:5 * VCOLS], ACT.Copy).then_inc(vst_a, 1)

            act.wait_ge(wts_in, 96)

            def take_xnT(tr, prev_q):
                act.wait_ge(tr_full, tr + 1)
                if prev_q is not None:
                    act.wait_ge(pj_full, prev_q + 1)
                A(xnT[:], TR[:].rearrange("p (t c k) -> p t c k", t=2, c=DC), ACT.Copy).then_inc(tr_empty, 1)

            def take_q(pj):
                act.wait_ge(pj_full, pj + 1)
                A(qT[:, 0, :], PJ[:, 0:2 * P], ACT.Identity, bias=bq_sb[:, 0:1])
                A(qT[:, 1, :], PJ[:, 2 * P:4 * P], ACT.Identity, bias=bq_sb[:, 1:2]).then_inc(pj_empty, 1)

            def expo(n, par, half):
                act.wait_ge(s_empty, 6 * n + 3 * (half + 1))
                e = SX[:, par, half * HALF:(half + 1) * HALF]
                A(e, e, ACT.Exp).then_inc(exp_done, 1)

            def take_hi(k, par, j, first=False):
                act.wait_ge(pt_full, TURNS * k + j + 1)
                if not first:
                    act.wait_ge(pv_done, TURNS * (k - 1) + j + 1)
                A(hi[:, j * 4 * P:(j + 1) * 4 * P], PT[(par + j) % 2], ACT.Copy).then_inc(hi_done, 1)

            def take_atT(tr, prev_out):
                act.wait_ge(tr_full, tr + 1)
                if prev_out is not None:
                    act.wait_ge(pj_full, prev_out + 1)
                A(atT[:], TR[:, 0:D].rearrange("p (c k) -> p c k", c=DC), ACT.Copy).then_inc(tr_empty, 1)

            def take_n2T(tr, par, prev_lg):
                act.wait_ge(tr_full, tr + 1)
                if prev_lg is not None:
                    act.wait_ge(pj_full, prev_lg + 1)
                A(n2T[:, :, par * P:(par + 1) * P], TR[:, 0:D].rearrange("p (c k) -> p c k", c=DC), ACT.Copy).then_inc(tr_empty, 1)

            def take_lgT(pj):
                act.wait_ge(pj_full, pj + 1)
                A(lgT[:], PJ[0:E, 0:2 * P], ACT.Identity, bias=br_sb[:, 0:1]).then_inc(pj_empty, 1)

            def take_lg(pj, b, j):
                act.wait_ge(pj_full, pj + 1)
                act.wait_ge(rt_step, ROUTE_STEPS * b)
                A(Lg[:, bass.ds(j * 2 * E, 2 * E)], PJ[:, 0:2 * E], ACT.Copy).then_inc(pj_empty, 1)

            def router_exp(b):
                act.wait_ge(rt_step, ROUTE_STEPS * b + 2)
                A(rt[:, 1], rt[:, 0], ACT.Exp).then_inc(rt_exp, 1)

            def tick(n, k, m, par, i, b, j, has_s=True, has_x=True, last_pair=False):
                odd = par == 1
                first_k = isinstance(k, int) and k == 0
                if m is not None:
                    prev = pj_use(i, b, 0, last_pair) if odd else None
                    if not odd and not (isinstance(i, int) and i == 0):
                        prev = pj_use(i, b, 0, last_pair) - 1
                    take_atT(tr_use(i, 2 * par, last_pair), prev)
                if k is not None:
                    take_hi(k, 1 - par, 0, first_k)
                if has_s:
                    expo(n, par, 0)
                if k is not None:
                    for t in (1, 2, 3):
                        take_hi(k, 1 - par, t, first_k)
                if has_s:
                    expo(n, par, 1)
                if m is not None:
                    prev = None
                    if not (isinstance(i, int) and i == 0):
                        prev = pj_use(i, b, 0, last_pair) - 1
                    take_n2T(tr_use(i, 2 * par + 1, last_pair), par, prev)
                if k is not None:
                    take_hi(k, 1 - par, 4, first_k)
                if odd and m is not None:
                    take_lgT(pj_use(i, b, 2, last_pair))
                if odd and has_x:
                    take_xnT(tr_use(i, 4), pj_use(i, b, 0) - 1)
                if odd and m is not None:
                    take_lg(pj_use(i, b, 3, last_pair), b, j)
                if odd and has_x:
                    take_q(pj_use(i, b, 4))

            def body(i, b, j, **kw):
                n = i * 2 + 2
                tick(n, n - 1, n - 2, 0, i, b, j, **kw)
                tick(n + 1, n if kw.get("has_s", True) else None, n - 1, 1, i, b, j, **kw)

            take_xnT(0, None)
            take_q(0)
            expo(0, 0, 0)
            expo(0, 0, 1)
            take_hi(0, 0, 0, True)
            expo(1, 1, 0)
            for t in (1, 2, 3):
                take_hi(0, 0, t, True)
            expo(1, 1, 1)
            take_hi(0, 0, 4, True)
            take_xnT(1, 0)
            take_q(1)
            with act.Fori(0, B - 1) as b:
                with act.Fori(0, BATCH_PAIRS) as j:
                    body(b * BATCH_PAIRS + j, b, j)
                router_exp(b)
            b = B - 1
            with act.Fori(0, BATCH_PAIRS - 2) as j:
                body(b * BATCH_PAIRS + j, b, j)
            body(PAIRS - 2, b, BATCH_PAIRS - 2, has_x=False)
            body(PAIRS - 1, b, BATCH_PAIRS - 1, has_s=False, has_x=False, last_pair=True)
            router_exp(b)

            def take_xgT(t, par, first=False):
                act.wait_ge(xt_full, t + 1)
                if not first:
                    act.wait_ge(up_full, 2 * (t - 1))
                A(xgT[:, par], XTp[:, 0:D].rearrange("p (c k) -> p c k", c=DC), ACT.Copy).then_inc(xt_empty, 1)

            def gelu(t, par):
                for u in range(2):
                    act.wait_ge(up_full, 2 * t + u + 1)
                    if u == 0 and (not isinstance(t, int) or t > 1):
                        act.wait_ge(ht_full, 2 * (t - 1))
                    A(hh[:, par, u * 512:(u + 1) * 512], UP[par][u], ACT.Gelu).then_inc(gelu_done, 1)

            def take_hT(t, par):
                act.wait_ge(ht_full, 2 * t + 2)
                if not isinstance(t, int) or t > 1:
                    act.wait_ge(y_full, t - 1)
                A(hT[:, par, 4 * P:8 * P], HTp[1], ACT.Copy).then_inc(ht_act, 1)

            act.wait_ge(pv_done, TURNS * TILES)
            take_xgT(0, 0, True)
            gelu(0, 0)
            take_xgT(1, 1, True)
            take_hT(0, 0)
            gelu(1, 1)

            def step(t, par):
                take_xgT(t + 1, 1 - par)
                take_hT(t, par)
                gelu(t + 1, 1 - par)

            with act.Fori(0, STEPS // 2 - 1) as s:
                step(s * 2 + 1, 1)
                step(s * 2 + 2, 0)
            take_hT(STEPS - 1, 1)

        @block.vector
        def _(dve):
            V = nc.vector
            dve.wait_ge(cst_in_s, 32)
            V.memset(ones[:], 1.0)
            V.tensor_copy(tri[:], cst[:, C_TRI:C_TRI + P])
            V.tensor_copy(sel[:], sel_f)
            V.tensor_copy(tok[:], cst[:, C_TOK:C_TOK + T8])
            V.memset(cnt[:], 0.0)
            for v in vp:
                V.memset(v[:, 0, :, HD:VH], 1.0)
                V.memset(v[:, 1:3, :, HD:VH], 0.0)
            dve.wait_ge(kT_done, 4)
            KBv = KB.rearrange("p (b c h k) -> p b c h k", b=B, c=DC, k=SK)
            for f in range(DC):
                for h in range(H // DC):
                    V.tensor_scalar(KBv[:, :, f, h, :], kT[:, f], cst[:, C_HM + h:C_HM + h + 1], None, ALU.mult).then_inc(KB_done, 1)
            dve.wait_ge(wv_in, 32)
            for b in range(B):
                steps = V_STEPS * b

                def link(ins):
                    nonlocal steps
                    steps += 1
                    ins.then_inc(v_step, 1)
                    dve.wait_ge(v_step, steps)

                for kb, n in ((0, P), (1, KREST)):
                    dve.wait_ge(v_ps, 2 * b + 2)
                    if b > 0 and kb == 0:
                        dve.wait_ge(vsel_ps, 4 * b)
                    part = [vp[kb][0:n, a, :, 0:HD] for a in range(3)]
                    whole = v_f[0:n, :].rearrange("p (h d) -> p h d", h=H)
                    rest = v_r[0:n, :].rearrange("p (h d) -> p h d", h=H)
                    link(V.tensor_tensor(v_f[0:n, :], banks[0:n, 4 + b, kb * D:(kb + 1) * D], bv_bc[0:n, :], ALU.add))
                    link(V.tensor_copy(part[0], whole))
                    link(V.tensor_tensor(rest, whole, part[0], ALU.subtract))
                    link(V.tensor_copy(part[1], rest))
                    link(V.tensor_tensor(part[2], rest, part[1], ALU.subtract))
                for g in range(2, 4):
                    dve.wait_ge(vsel_ps, 4 * b + g + 1)
                    if b > 0:
                        dve.wait_ge(v_stored, 16 * b)
                    V.tensor_copy(v_st[:, g * 5 * VCOLS:(g + 1) * 5 * VCOLS], banks[:, g, 0:5 * VCOLS]).then_inc(vst_d, 1)

            dve.wait_ge(wts_in, 96)
            dve.wait_ge(init_done, 5)

            def ln1_stats(p):
                dve.wait_ge(x_loaded, 16 * p + 16)
                V.bn_stats(st1[:, 0, :], xt[:, 0, :])
                V.bn_stats(st1[:, 1, :], xt[:, 1, :]).then_inc(ln1_step, 1)

            def ln1_aggr(p, alone=False):
                if alone:
                    dve.wait_ge(ln1_step, LN1_STEPS * p + 1)
                V.bn_aggr(mv1[:, 0, :], st1[:, 0, :])
                V.bn_aggr(mv1[:, 1, :], st1[:, 1, :]).then_inc(ln1_step, 1)

            def ln1_apply(p, turned):
                dve.wait_ge(ln1_rstd, 2 * p + 2)
                dve.wait_ge(tr_full, turned)
                for t in range(2):
                    last = V.tensor_scalar(xn[:, t, :], xt[:, t, :], mv1[:, t, 0:1], rs1[:, t:t + 1], ALU.subtract, ALU.mult)
                last.then_inc(ln1_step, 1)

            def take_scores(n, par, g, first=False, stats=None, summed=None):
                c, h, w = GROUPS[g]
                at, h = c * HALF + h * SK, c * (H // DC) + h
                s = SC[g % SLOTS][:, 0:w * SK].rearrange("p (h k) -> p h k", k=SK)
                dve.wait_ge(s_full, 6 * n + g + 1)
                V.tensor_reduce(mx[:, h:h + w], s, AX.X, ALU.max).then_inc(s_max, 1)
                if stats:
                    stats()
                    dve.wait_ge(*summed)
                if g == 0 and not first:
                    dve.wait_ge(pt_full, TURNS * (n - 1))
                dve.wait_ge(s_max, 6 * n + g + 1)
                V.tensor_tensor(SX[:, par, at:at + w * SK].rearrange("p (h k) -> p h k", k=SK), s,
                                mx[:, h:h + w].unsqueeze(2).broadcast_to([P, w, SK]), ALU.subtract).then_inc(s_empty, 1)

            def take_lo(k, par, j, first=False):
                dve.wait_ge(hi_done, TURNS * k + j + 1)
                if not first:
                    dve.wait_ge(pv_done, TURNS * (k - 1) + j + 1)
                at = slice(j * 4 * P, (j + 1) * 4 * P)
                V.tensor_tensor(lo[:, at], PT[(par + j) % 2], hi[:, at], ALU.subtract).then_inc(pt_empty, 1)

            def normalise(k, turned):
                Ov = O[:, 0:H * VH].rearrange("p (h v) -> p h v", v=VH)
                dve.wait_ge(pv_done, TURNS * (k + 1))
                V.reciprocal(rden[:], Ov[:, :, HD]).then_inc(rden_done, 1)
                if turned is not None:
                    dve.wait_ge(tr_full, turned)
                dve.wait_ge(rden_done, k + 1)
                V.tensor_tensor(attn[:].rearrange("p (h d) -> p h d", h=H), Ov[:, :, 0:HD],
                                rden[:].unsqueeze(2).broadcast_to([P, H, HD]), ALU.mult).then_inc(attn_done, 1)

            def add_residual(m, par, pj):
                dve.wait_ge(pj_full, pj + 1)
                dve.wait_ge(xr_ready, m + 1)
                dve.wait_ge(x2_stored, 16 * m)
                V.tensor_tensor(x2[:, par, :], PJ[:, 0:D], xr[:, par, :], ALU.add).then_inc(pj_empty, 1)

            def ln2_stats(m, par, pj):
                dve.wait_ge(pj_empty, pj + 1)
                V.bn_stats(st2[:], x2[:, par, :]).then_inc(ln2_step, 1)

            def ln2_aggr(m, alone):
                if alone:
                    dve.wait_ge(ln2_step, 2 * m + 1)
                V.bn_aggr(mv2[:], st2[:]).then_inc(ln2_step, 1)

            def ln2_apply(m, par, turned):
                dve.wait_ge(ln2_rstd, 2 * m + 2)
                dve.wait_ge(tr_full, turned)
                dve.wait_ge(n2_stored, 16 * m)
                V.tensor_scalar(n2[:, par, :], x2[:, par, :], mv2[:, 0:1], rs2[:, 1:2], ALU.subtract, ALU.mult).then_inc(n2_done, 1)

            def tick(n, k, m, par, i, b, has_s=True, has_x=True, last_pair=False):
                odd = par == 1
                first_k = isinstance(k, int) and k == 0
                if has_s:
                    take_scores(n, par, 0)
                    if odd and has_x:
                        take_scores(n, par, 1, stats=lambda: ln1_stats(i + 2), summed=(ln1_step, LN1_STEPS * (i + 2) + 1))
                        ln1_aggr(i + 2)
                    else:
                        take_scores(n, par, 1)
                if has_s:
                    take_scores(n, par, 2)
                if k is not None:
                    take_lo(k, 1 - par, 0, first_k)
                pj = pj_use(i, b, par, last_pair)
                add_residual(m, par, pj)
                if has_s:
                    take_scores(n, par, 3, stats=lambda: ln2_stats(m, par, pj), summed=(ln2_step, 2 * m + 1))
                else:
                    ln2_stats(m, par, pj)
                ln2_aggr(m, not has_s)
                if k is not None:
                    take_lo(k, 1 - par, 1, first_k)
                if has_s:
                    take_scores(n, par, 4)
                if k is not None:
                    take_lo(k, 1 - par, 2, first_k)
                ln2_apply(m, par, tr_use(i, 0, last_pair))
                if odd and has_x:
                    ln1_apply(i + 2, tr_use(i, 0))
                if has_s:
                    take_scores(n, par, 5)
                if k is not None:
                    take_lo(k, 1 - par, 3, first_k)
                    take_lo(k, 1 - par, 4, first_k)
                    normalise(k, tr_use(i, 2 * par, last_pair) + 1)

            def body(i, b, **kw):
                n = i * 2 + 2
                tick(n, n - 1, n - 2, 0, i, b, **kw)
                tick(n + 1, n if kw.get("has_s", True) else None, n - 1, 1, i, b, **kw)

            def route(b, lg, count):
                steps = 0

                def link(ins):
                    nonlocal steps
                    steps += 1
                    ins.then_inc(rt_step, 1)
                    dve.wait_ge(rt_step, ROUTE_STEPS * b + steps)

                def over_e(v):
                    return v.unsqueeze(2).broadcast_to([P, T8, E])

                def over_t(v):
                    return v.unsqueeze(1).broadcast_to([P, T8, E])

                less, prob, pick, best, second, left, row = (rt[:, a] for a in range(7))
                top, total, inv, w1, first_at, w2 = (rs[:, a] for a in range(6))
                desc = cst[:, C_DESC:C_DESC + E]
                L = Lg[:].rearrange("p (t e) -> p t e", e=E)
                dve.wait_ge(pj_empty, lg + 1)
                link(V.tensor_reduce(top, L, AX.X, ALU.max))
                link(V.tensor_tensor(less, L, over_e(top), ALU.subtract))
                dve.wait_ge(rt_exp, b + 1)
                link(V.tensor_reduce(total, prob, AX.X, ALU.add))
                link(V.reciprocal(inv, total))
                link(V.tensor_tensor(prob, prob, over_e(inv), ALU.mult))
                for p_, w, one in ((prob, w1, best), (left, w2, second)):
                    link(V.tensor_reduce(w, p_, AX.X, ALU.max))
                    link(V.tensor_tensor(pick, p_, over_e(w), ALU.is_equal))
                    link(V.tensor_tensor(pick, pick, over_t(desc), ALU.mult))
                    link(V.tensor_reduce(first_at, pick, AX.X, ALU.max))
                    link(V.tensor_tensor(one, pick, over_e(first_at), ALU.is_equal))
                    if one is best:
                        link(V.scalar_tensor_tensor(left, best, -2.0, prob, ALU.mult, ALU.add))
                link(V.tensor_tensor(Mb[:], best, second, ALU.add))
                dve.wait_ge(pj_full, count + 1)
                link(V.tensor_tensor(row, PJ[:, 0:T8 * E].rearrange("p (t e) -> p t e", e=E), over_t(cnt[:]), ALU.add))
                V.tensor_tensor(cnt[:], cnt[:], PJ[:, T8 * E:(T8 + 1) * E], ALU.add).then_inc(pj_empty, 1)
                link(V.tensor_tensor(row, row, over_t(cst[:, C_BASE:C_BASE + E]), ALU.add))
                if not isinstance(b, int) or b > 0:
                    dve.wait_ge(scattered, 16 * 2 * T8 * b)
                for k, one in enumerate((best, second)):
                    link(V.tensor_tensor(pick, one, row, ALU.mult))
                    link(V.tensor_reduce(rs[:, 6 + k], pick, AX.X, ALU.add))
                V.tensor_copy(pos[:], rs[:, 6:8])
                for k, w in enumerate((w1, w2)):
                    V.tensor_copy(ent[:, :, k, 0], tok[:])
                    V.tensor_copy(ent[:, :, k, 1], w)
                link(V.tensor_scalar(tok[:], tok[:], float(S), None, ALU.add))
                assert steps == ROUTE_STEPS, steps

            ln1_stats(0)
            ln1_aggr(0, alone=True)
            ln1_apply(0, 0)
            for g in range(6):
                take_scores(0, 0, g, first=True)
            take_scores(1, 1, 0, first=True)
            take_scores(1, 1, 1)
            ln1_stats(1)
            ln1_aggr(1, alone=True)
            take_scores(1, 1, 2)
            take_lo(0, 0, 0, True)
            take_scores(1, 1, 3)
            take_lo(0, 0, 1, True)
            take_scores(1, 1, 4)
            take_lo(0, 0, 2, True)
            ln1_apply(1, 1)
            take_scores(1, 1, 5)
            take_lo(0, 0, 3, True)
            take_lo(0, 0, 4, True)
            normalise(0, None)
            with dve.Fori(0, B - 1) as b:
                with dve.Fori(0, BATCH_PAIRS) as j:
                    body(b * BATCH_PAIRS + j, b)
                route(b, pj_use(b * BATCH_PAIRS + BATCH_PAIRS - 1, b, 3), pj_use(b * BATCH_PAIRS + BATCH_PAIRS, b, 0))
            b = B - 1
            with dve.Fori(0, BATCH_PAIRS - 2) as j:
                body(b * BATCH_PAIRS + j, b)
            body(PAIRS - 2, b, has_x=False)
            body(PAIRS - 1, b, has_s=False, has_x=False, last_pair=True)
            route(b, pj_use(PAIRS - 1, b, 3, True), pj_use(PAIRS - 1, b, 4, True))

            steps = 0

            def link(ins):
                nonlocal steps
                steps += 1
                ins.then_inc(meta_step, 1)
                dve.wait_ge(meta_step, steps)

            row0 = SX[0:1, 0, :]
            past = row0[:, 0:STEPS * (E - 1)].rearrange("p (j e) -> p j e", e=E - 1)
            past_n = row0[:, 512:512 + STEPS * (E - 1)].rearrange("p (j e) -> p j e", e=E - 1)
            over = row0[:, 1024:1024 + E * 32].rearrange("p (e m) -> p e m", e=E)
            blocks, ends, unit = (blk[0:1, a, :] for a in range(3))
            expert, start, within = (meta[0:1, a, :] for a in range(3))
            js = cst[0:1, C_J:C_J + STEPS]
            V.memset(unit, 1.0)
            link(V.tensor_tensor(over, cnt[0:1, :].unsqueeze(2).broadcast_to([1, E, 32]),
                                 cst[0:1, C_M:C_M + 32].unsqueeze(1).broadcast_to([1, E, 32]), ALU.is_gt))
            link(V.tensor_reduce(blocks, over, AX.X, ALU.add))
            link(V.tensor_tensor_scan(ends, unit, blocks, 0.0, ALU.mult, ALU.add))
            link(V.tensor_tensor(past, js.unsqueeze(2).broadcast_to([1, STEPS, E - 1]),
                                 ends[:, 0:E - 1].unsqueeze(1).broadcast_to([1, STEPS, E - 1]), ALU.is_ge))
            link(V.tensor_reduce(expert, past, AX.X, ALU.add))
            link(V.tensor_tensor(past_n, past, blocks[:, 0:E - 1].unsqueeze(1).broadcast_to([1, STEPS, E - 1]), ALU.mult))
            link(V.tensor_reduce(start, past_n, AX.X, ALU.add))
            link(V.tensor_scalar(exw[:], expert, float(EW), None, ALU.mult))
            link(V.tensor_tensor(within, js, start, ALU.subtract))
            link(V.tensor_scalar(within, within, float(P), None, ALU.mult))
            link(V.scalar_tensor_tensor(off[:], expert, float(LIST), within, ALU.mult, ALU.add))
            assert steps == META_STEPS

            def take_rows(t, par, nth, first=False):
                dve.wait_ge(lst_loaded[par], 16 * (nth + 1))
                if not first:
                    dve.wait_ge(gathered[par], 16 * nth)
                    dve.wait_ge(added, 16 * (t - 1))
                V.tensor_scalar(idg[:, par, :], lst[:, par, 0:1], float(TOKENS - 1), None, ALU.min).then_inc(ids_ready, 1)
                V.tensor_copy(ids[:, par, :], lst[:, par, 0:1]).then_inc(ids_ready, 1)

            def take_hT(t, par):
                dve.wait_ge(ht_full, 2 * t + 1)
                if not isinstance(t, int) or t > 1:
                    dve.wait_ge(y_full, t - 1)
                V.tensor_copy(hT[:, par, 0:4 * P], HTp[0]).then_inc(ht_dve, 1)

            def take_y(t, par):
                dve.wait_ge(y_full, t + 1)
                if not isinstance(t, int) or t > 1:
                    dve.wait_ge(added, 16 * (t - 1))
                V.tensor_scalar(y[:, par, :], Y[:, 0:D], lst[:, par, 1:2], None, ALU.mult).then_inc(y_done, 1)

            take_rows(0, 0, 0, True)
            take_rows(1, 1, 0, True)
            for t in range(2):
                take_hT(t, t)
                take_y(t, t)
                take_rows(t + 2, t, 1)
            with dve.Fori(1, STEPS // 2 - 1) as s:
                for par in range(2):
                    take_hT(s * 2 + par, par)
                    take_y(s * 2 + par, par)
                    take_rows(s * 2 + par + 2, par, s + 1)
            for t in range(STEPS - 2, STEPS):
                take_hT(t, t % 2)
                take_y(t, t % 2)


def kernel(**inputs):
    import numpy as np
    import concourse.bacc as bacc
    from concourse.bass_utils import run_bass_kernel_spmd

    g = {k: np.asarray(v) for k, v in inputs.items()}
    cst = np.zeros((P, C_ALL), np.float32)
    p = np.arange(P)
    cst[:, C_ID:C_ID + P] = np.eye(P)
    cst[:, C_TRI:C_TRI + P] = p[:, None] < p[None, :]
    cst[:, C_HM:C_HM + H // DC] = (p[:, None] // HD == np.arange(H // DC)[None, :]) * HD ** -0.5
    cst[:, C_DESC:C_DESC + E] = E - np.arange(E)
    cst[:, C_BASE:C_BASE + E] = LIST * np.arange(E)
    cst[:, C_TOK:C_TOK + BATCH_TILES] = P * np.arange(BATCH_TILES)[None, :] + p[:, None]
    cst[:, C_J:C_J + STEPS] = np.arange(STEPS)
    cst[:, C_M:C_M + 32] = P * np.arange(32)
    xs = np.arange(SELW)
    sel = np.zeros((P, 4, SELW), np.float32)
    for kb in range(2):
        for slot in range(2):
            sel[:, 2 * kb + slot] = (kb * P + p)[:, None] == xs[None, :] - slot * SK
    sel[KREST:, 2:] = 0

    def T(a):
        return np.ascontiguousarray(np.swapaxes(a, -1, -2))

    def cols(v):
        return np.ascontiguousarray(v.reshape(DC, P).T)

    arrays = {
        "x": np.ascontiguousarray(g["x"]),
        "ctxT": np.ascontiguousarray(g["ctx_1024"].transpose(2, 0, 1)),
        "wqT": T(g["L0_xattn_Wq"]), "bq": cols(g["L0_xattn_bq"]),
        "wkT": T(g["L0_xattn_Wk"]), "bk": cols(g["L0_xattn_bk"]),
        "wvT": T(g["L0_xattn_Wv"]), "bv": np.ascontiguousarray(g["L0_xattn_bv"]),
        "woT": T(g["L0_xattn_Wo"]), "bo": np.ascontiguousarray(g["L0_xattn_bo"]),
        "wr": np.ascontiguousarray(g["L0_ffn_router_w"]), "br": g["L0_ffn_router_b"].reshape(E, 1).copy(),
        "upT": T(g["L0_ffn_expert_up"]), "dnT": T(g["L0_ffn_expert_down"]),
        "cst": cst, "sel": sel,
    }
    nc = bacc.Bacc("TRN2", target_bir_lowering=False, num_devices=1)
    args = [nc.dram_tensor(f"{k}_dram", a.shape, mybir.dt.from_np(a.dtype), kind="ExternalInput").ap() for k, a in arrays.items()]
    out = nc.dram_tensor("out_dram", (B, S, D), F32, kind="ExternalOutput").ap()
    bass_xattn_moe(nc, *args, out)
    r = run_bass_kernel_spmd(nc, [{f"{k}_dram": a for k, a in arrays.items()}], core_ids=[0])
    return r.results[0]["out_dram"]
```

```python
from contextlib import ExitStack

import concourse.bass as bass
from concourse import mybir

P = 128
B, S, D = 4, 1024, 256
SK = 154
H, HD = 16, 16
E, F = 8, 1024
DC = D // P
TOKENS = B * S
TILES = TOKENS // P
PAIRS = TILES // 2
BATCH_TILES = S // P
BATCH_PAIRS = BATCH_TILES // 2
EPS = 1e-5

HALF = H // DC * SK
COLS = H * SK
CHUNKS = -(-COLS // P)
PADDED = CHUNKS * P
GROUPS = [(c, o, n) for c in range(DC) for o, n in ((0, 3), (3, 3), (6, 2))]
SLOTS = 3
TURNS = CHUNKS // 4
VH = HD + 1
VCOLS = 3 * 2 * VH
KREST = SK - P

DOWN_AT = DC * F
EW = DOWN_AT + F // P * D
LIST = TOKENS
BLOCKS = 2 * TOKENS // P + E - 1
GROUP = 4
STEPS = -(-BLOCKS // GROUP) * GROUP
AHEAD = 3
LIST_ROWS = E * LIST + 8 * P
NOBODY = 2.0 * TOKENS
EARLY = 4

C_ID, C_TRI, C_HM, C_DESC, C_BASE, C_TOK, C_J, C_M = 0, 128, 256, 264, 272, 280, 288, 288 + STEPS
C_ALL = C_M + 32
SELW = 282

F32 = mybir.dt.float32
F16 = mybir.dt.float16
BF16 = mybir.dt.bfloat16
I32 = mybir.dt.int32
ALU = mybir.AluOpType
ACT = mybir.ActivationFunctionType
AX = mybir.AxisListType

LN1_STEPS = 3
ROUTE_STEPS = 24
V_STEPS = 10


def bass_xattn_moe(nc, x, ctxT, wqT, bq, wkT, bk, wvT, bv, woT, bo, wr, br, upT, dnT, cst_in, sel_in, out):
    with ExitStack() as ctx:
        def sb(name, shape, dt=F32):
            return ctx.enter_context(nc.sbuf_tensor(name, shape, dt))

        def sem(name):
            return ctx.enter_context(nc.semaphore(name))

        v_dram = nc.dram_tensor("v_dram", [B, P, CHUNKS * VCOLS], BF16, kind="Internal").ap()
        n2_dram = nc.dram_tensor("n2_dram", [TOKENS, D], F32, kind="Internal").ap()
        list_dram = nc.dram_tensor("list_dram", [LIST_ROWS, 2], F32, kind="Internal").ap()

        x_tiles = x.rearrange("b (n p) d -> (b n) p d", p=P)
        out_rows = out.rearrange("b s d -> (b s) d")

        W = sb("W", [P, E * EW])
        tmp = W[:, EARLY * EW:(EARLY + 1) * EW]
        ctx_sb = tmp[:, 0:DC * B * SK].rearrange("p (c b k) -> p c b k", c=DC, b=B)
        kT = tmp[:, 1232:1232 + DC * B * SK].rearrange("p (c b k) -> p c b k", c=DC, b=B)
        sel_f = tmp[:, 2464:2464 + 4 * SELW].rearrange("p (a x) -> p a x", a=4)
        KB = W[:, (EARLY + 1) * EW:(EARLY + 1) * EW + B * COLS]
        tmp2 = W[:, (EARLY + 1) * EW + B * COLS:E * EW]
        wk_sb = tmp2[:, 0:512].rearrange("p (c n) -> p c n", c=DC)
        wv_sb = tmp2[:, 512:1024].rearrange("p (c n) -> p c n", c=DC)
        v_st = tmp2[:, 1024:1024 + CHUNKS * VCOLS // 2].bitcast(BF16)

        cst = sb("cst", [P, C_ALL])
        ident = cst[:, C_ID:C_ID + P]
        tri = sb("tri", [P, P], BF16)
        ones = sb("ones", [P, P], BF16)
        sel = sb("sel", [P, 4, SELW], BF16)
        wq_sb = sb("wq_sb", [P, DC, D])
        wo_sb = sb("wo_sb", [P, DC, D])
        wr_sb = sb("wr_sb", [P, DC, E])
        bq_sb = sb("bq_sb", [P, DC])
        bk_sb = sb("bk_sb", [P, DC])
        br_sb = sb("br_sb", [E, 1])
        bo_bc = sb("bo_bc", [P, D])
        bv_bc = sb("bv_bc", [P, D])
        v_f = sb("v_f", [P, D])
        v_r = sb("v_r", [P, D])
        vp = [sb("vp0", [P, 3, H, VH], BF16), sb("vp1", [KREST, 3, H, VH], BF16)]
        half_pow = sb("half_pow", [P, 2])
        eps = sb("eps", [P, 2])
        gate = sb("gate", [P, 2])

        xt = sb("xt", [P, 2, D])
        xn = sb("xn", [P, 2, D])
        xnT = sb("xnT", [P, 2, DC, P])
        qT = sb("qT", [P, DC, 2 * P])
        st1 = sb("st1", [P, 2, 6])
        mv1 = sb("mv1", [P, 2, 2])
        rs1 = sb("rs1", [P, 2])
        mx = sb("mx", [P, H])
        SX = sb("SX", [P, 2, PADDED])
        hi = sb("hi", [P, PADDED], F16)
        lo = sb("lo", [P, PADDED], F16)
        Vc = sb("Vc", [P, 2, CHUNKS * VCOLS], BF16)
        rden = sb("rden", [P, H])
        attn = sb("attn", [P, D])
        atT = sb("atT", [P, DC, P])
        xr = sb("xr", [P, 2, D])
        x2 = sb("x2", [P, 2, D])
        st2 = sb("st2", [P, 6])
        mv2 = sb("mv2", [P, 2])
        rs2 = sb("rs2", [P, 2])
        n2 = sb("n2", [P, 2, D])
        n2T = sb("n2T", [P, DC, 2 * P])
        lgT = sb("lgT", [E, 2 * P])
        Lg = sb("Lg", [P, BATCH_TILES * E])

        T8 = BATCH_TILES
        rt = sb("rt", [P, 8, T8, E])
        rs = sb("rs", [P, 8, T8])
        Mb = sb("Mb", [P, T8, E], BF16)
        cnt = sb("cnt", [P, E])
        tok = sb("tok", [P, T8])
        ent = sb("ent", [P, T8, 2, 2])
        pos = sb("pos", [P, 2, T8], I32)

        meta = sb("meta", [1, 4, STEPS])
        blk = sb("blk", [1, 4, E])
        exw = sb("exw", [1, STEPS], I32)
        off = sb("off", [1, STEPS], I32)
        lst = sb("lst", [P, STEPS, 2])
        idg = sb("idg", [P, GROUP, 1], I32)
        ids = sb("ids", [P, 2, 1], I32)
        xg = Vc[:].rearrange("p s n -> p (s n)")[:, 0:GROUP * 2 * D].bitcast(F32).rearrange("p (s d) -> p s d", s=GROUP)
        xgT = hi[:, 4 * D:8 * D].bitcast(F32).rearrange("p (s c k) -> p s c k", s=2, c=DC)
        hh = SX[:, :, 0:F]
        hT = SX[:, :, F:2 * F]
        y = lo[:, 0:4 * D].bitcast(F32).rearrange("p (s d) -> p s d", s=2)

        banks = ctx.enter_context(nc.psum_tensor("banks", [P, 8, 512], F32))
        SC = [banks[:, s, :] for s in range(SLOTS)]
        PT = [banks[:, 3 + s, :] for s in range(2)]
        O = banks[:, 5, :]
        TR = banks[:, 6, :]
        PJ = banks[:, 7, :]
        UP = [[banks[:, 2 * s + u, :] for u in range(2)] for s in range(2)]
        HTp = [banks[:, 4 + s, :] for s in range(2)]
        XTp = banks[:, 6, :]
        Y = banks[:, 7, :]

        cst_in_s = sem("constants_loaded")
        ctx_in = sem("context_and_wk_loaded")
        wv_in = sem("wv_loaded")
        wts_in = sem("attention_weights_loaded")
        experts_in = sem("experts_loaded")
        init_done = sem("constants_made")
        k_ps = sem("k_in_psum")
        kT_done = sem("kT_done")
        KB_done = sem("KB_done")
        v_ps = sem("v_in_psum")
        v_step = sem("value_parts_step")
        vsel_ps = sem("chunk_values_in_psum")
        vst_a = sem("chunk_values_by_act")
        vst_d = sem("chunk_values_by_dve")
        v_stored = sem("chunk_values_stored")
        list_set = sem("list_filler_made")
        x_loaded = sem("x_loaded")
        ln1_step = sem("ln1_step")
        ln1_rstd = sem("ln1_rstd")
        tr_full, tr_empty = sem("turned_in_psum"), sem("turned_taken")
        pj_full, pj_empty = sem("projected_in_psum"), sem("projected_taken")
        s_full, s_max, s_empty = sem("scores_in_psum"), sem("score_max"), sem("scores_taken")
        exp_done = sem("exp_done")
        pt_full, hi_done, pt_empty = sem("probs_turned"), sem("hi_done"), sem("lo_done")
        vc_loaded = [sem("vc_loaded0"), sem("vc_loaded1")]
        pv_done = sem("pv_done")
        rden_done, attn_done = sem("denominators"), sem("attn_done")
        xr_loaded = [sem("residual_loaded0"), sem("residual_loaded1")]
        xr_ready = sem("residual_ready")
        ln2_step, ln2_rstd, n2_done = sem("ln2_step"), sem("ln2_rstd"), sem("n2_done")
        x2_stored, n2_stored = sem("x2_stored"), sem("n2_stored")
        lg_done = sem("logits_ready")
        rt_exp = sem("router_exp")
        rt_step = sem("routing_step")
        scattered = sem("lists_filled_and_scattered")
        meta_step = sem("block_table_step")
        gate_step = sem("gate_step")
        lst_loaded = sem("list_rows_loaded")
        idg_ready = sem("rows_to_gather")
        ids_ready = sem("rows_to_add")
        gathered = [sem(f"gathered{s}") for s in range(GROUP)]
        xt_full, xt_empty = sem("tokens_turned"), sem("tokens_taken")
        up_full, gelu_done = sem("up_in_psum"), sem("gelu_done")
        ht_full, ht_dve, ht_act = sem("hidden_turned"), sem("hidden_taken_dve"), sem("hidden_taken_act")
        y_full, y_done = sem("down_in_psum"), sem("y_done")
        added = sem("rows_added")

        META_STEPS = 11

        def tr_use(i, pos_, last=False):
            return 2 + 5 * i + pos_ - (1 if last else 0)

        def pj_use(i, b, pos_, last=False):
            return 2 + 5 * i + b + pos_ - (1 if last else 0)

        block = ctx.enter_context(nc.Block())

        @block.sync
        def _(sp):
            nc.sync.sem_inc(x2_stored, 32)
            nc.sync.sem_inc(n2_stored, 32)
            sp.dma_start(ctx_sb, ctxT.rearrange("(c p) b k -> p c b k", p=P)).then_inc(ctx_in, 16)
            sp.dma_start(wk_sb, wkT.rearrange("(c p) n -> p c n", p=P)).then_inc(ctx_in, 16)
            sp.dma_start(bk_sb[:], bk).then_inc(ctx_in, 16)
            sp.dma_start(cst[:], cst_in).then_inc(cst_in_s, 16)
            sp.dma_start(sel_f, sel_in).then_inc(cst_in_s, 16)
            sp.dma_start(wv_sb, wvT.rearrange("(c p) n -> p c n", p=P)).then_inc(wv_in, 16)
            sp.dma_start(bv_bc[:], bv.unsqueeze(0).broadcast_to([P, D])).then_inc(wv_in, 16)

            def load_x(p):
                if not isinstance(p, int) or p > 0:
                    sp.wait_ge(ln1_step, LN1_STEPS * p)
                sp.dma_start(xt[:], x_tiles[bass.ds(p * 2, 2)].rearrange("t p d -> p t d")).then_inc(x_loaded, 16)

            load_x(0)
            sp.dma_start(wq_sb[:], wqT.rearrange("(c p) n -> p c n", p=P)).then_inc(wts_in, 16)
            sp.dma_start(wo_sb[:], woT.rearrange("(c p) n -> p c n", p=P)).then_inc(wts_in, 16)
            sp.dma_start(wr_sb[:], wr.rearrange("(c p) n -> p c n", p=P)).then_inc(wts_in, 16)
            sp.dma_start(bq_sb[:], bq).then_inc(wts_in, 16)
            sp.dma_start(br_sb[:], br).then_inc(wts_in, 16)
            sp.dma_start(bo_bc[:], bo.unsqueeze(0).broadcast_to([P, D])).then_inc(wts_in, 16)

            for b in range(B):
                sp.wait_ge(vst_a, 2 * (b + 1))
                sp.wait_ge(vst_d, 2 * (b + 1))
                if b > 0:
                    sp.wait_ge(v_stored, 16 * b)
                sp.dma_start(v_dram[b], v_st).then_inc(v_stored, 16)
            sp.wait_ge(v_stored, 16 * B)

            def load_vc(k, par, kpair, first=False):
                if not first:
                    sp.wait_ge(pv_done, TURNS * (k - 1))
                sp.dma_start(Vc[:, par, :], v_dram[bass.ds(k // BATCH_TILES, 1)].rearrange("o p n -> p (o n)")).then_inc(vc_loaded[par], 16)

            def load_xr(m, par, first=False):
                if not first:
                    sp.wait_ge(ln2_step, 2 * (m - 1))
                sp.dma_start(xr[:, par, :], x_tiles[bass.ds(m, 1)].rearrange("o p d -> p (o d)")).then_inc(xr_loaded[par], 16)

            def store(m, par):
                sp.wait_ge(n2_done, m + 1)
                sp.wait_ge(x2_stored, 16 * m + 32)
                sp.wait_ge(n2_stored, 16 * m + 32)
                sp.dma_start(out_rows[bass.ds(m * P, P)], x2[:, par, :]).then_inc(x2_stored, 16)
                sp.dma_start(n2_dram[bass.ds(m * P, P)], n2[:, par, :]).then_inc(n2_stored, 16)

            load_x(1)
            for par in range(2):
                load_vc(par, par, 0, first=True)
                load_xr(par, par, first=True)

            def body(i, more=True, next_x=True):
                m = i * 2
                for par in range(2):
                    if par == 0 and next_x:
                        load_x(i + 2)
                    store(m + par, par)
                    if more:
                        load_xr(m + par + 2, par)
                        load_vc(m + par + 2, par, 0)

            with sp.Fori(0, PAIRS - 2) as i:
                body(i)
            body(PAIRS - 2, next_x=False)
            body(PAIRS - 1, more=False, next_x=False)

            sp.wait_ge(s_full, 6 * TILES)
            for e in range(EARLY, E):
                sp.dma_start(W[:, e * EW:e * EW + DOWN_AT].rearrange("p (c f) -> p c f", c=DC), upT[e].rearrange("(c p) f -> p c f", p=P)).then_inc(experts_in, 16)
                sp.dma_start(W[:, e * EW + DOWN_AT:(e + 1) * EW].rearrange("p (k d) -> p k d", d=D), dnT[e].rearrange("(k p) d -> p k d", p=P)).then_inc(experts_in, 16)

            sp.wait_ge(meta_step, META_STEPS)
            sp.wait_ge(scattered, 16 * 2 * TILES + 16)

            def load_rows(g):
                if not isinstance(g, int) or g > 0:
                    sp.wait_ge(idg_ready, GROUP * (g - 1) + 1)
                for j in range(GROUP):
                    t = g * GROUP + j
                    v = sp.value_load(off[0:1, bass.ds(t, 1)], min_val=0, max_val=LIST_ROWS - P)
                    sp.dma_start(lst[:, bass.ds(t, 1), :].rearrange("p o a -> p (o a)"), list_dram[bass.ds(v, P)]).then_inc(lst_loaded, 16)

            load_rows(0)
            with sp.Fori(1, STEPS // GROUP) as g:
                load_rows(g)
            sp.wait_ge(x2_stored, 16 * (TILES + 2))
            sp.wait_ge(n2_stored, 16 * (TILES + 2))
            sp.wait_ge(v_stored, 16 * B)
            sp.wait_ge(added, 16 * STEPS)

        @block.gpsimd
        def _(pool):
            nc.gpsimd.memset(half_pow[:], -0.5).then_inc(init_done, 1)
            nc.gpsimd.memset(eps[:], EPS).then_inc(init_done, 1)
            nc.gpsimd.memset(gate[:], 0.0).then_inc(init_done, 1)
            filler = SX[:, 1, 0:2 * LIST_ROWS // P].rearrange("p (n a) -> p n a", a=2)
            nc.gpsimd.sem_inc(gate_step, 1)
            nc.gpsimd.memset(filler[:, :, 0], NOBODY).then_inc(list_set, 1)
            nc.gpsimd.memset(filler[:, :, 1], 0.0).then_inc(list_set, 1)
            pool.wait_ge(list_set, 2)
            pool.dma_start(list_dram.rearrange("(p n) a -> p n a", p=P), filler).then_inc(scattered, 16)
            pool.wait_ge(scattered, 16)
            nc.gpsimd.memset(SX[:, 1, COLS:PADDED], 0.0).then_inc(init_done, 1)
            nc.gpsimd.memset(SX[:, 0, COLS:PADDED], 0.0).then_inc(init_done, 1)
            pool.wait_ge(init_done, 5)
            pool.wait_ge(wts_in, 96)

            def gate_op(nth):
                pool.wait_ge(gate_step, nth + 1)
                nc.gpsimd.tensor_tensor(gate[:, 1:2], gate[:, 0:1], gate[:, 0:1], ALU.add).then_inc(gate_step, 1)

            def rstd1(p):
                pool.wait_ge(ln1_step, LN1_STEPS * p + 2)
                nc.gpsimd.tensor_tensor(rs1[:], mv1[:, :, 1], eps[:], ALU.add).then_inc(ln1_rstd, 1)
                pool.wait_ge(ln1_rstd, 2 * p + 1)
                nc.gpsimd.tensor_tensor(rs1[:], rs1[:], half_pow[:], ALU.pow).then_inc(ln1_rstd, 1)

            def residual(m, par, nth):
                pool.wait_ge(xr_loaded[par], 16 * (nth + 1))
                nc.gpsimd.tensor_tensor(xr[:, par, :], xr[:, par, :], bo_bc[:], ALU.add).then_inc(xr_ready, 1)

            def rstd2(m):
                pool.wait_ge(ln2_step, 2 * m + 2)
                nc.gpsimd.tensor_tensor(rs2[:, 0:1], mv2[:, 1:2], eps[:, 0:1], ALU.add).then_inc(ln2_rstd, 1)
                pool.wait_ge(ln2_rstd, 2 * m + 1)
                nc.gpsimd.tensor_tensor(rs2[:, 1:2], rs2[:, 0:1], half_pow[:, 0:1], ALU.pow).then_inc(ln2_rstd, 1)

            def scatter(b):
                pool.wait_ge(rt_step, ROUTE_STEPS * (b + 1) + 1)
                gate_op(b)
                for t in range(T8):
                    for k in range(2):
                        pool.indirect_dma_start(
                            out=list_dram, out_offset=bass.IndirectOffsetOnAxis(ap=pos[:, k, t:t + 1], axis=0),
                            in_=ent[:, t, k, :], in_offset=None).then_inc(scattered, 16)

            rstd1(0)
            rstd1(1)

            def body(i, next_x=True):
                for par in range(2):
                    residual(i * 2 + par, par, i)
                    rstd2_at = i * 2 + par
                    if par == 1 and next_x:
                        rstd1(i + 2)
                    rstd2(rstd2_at)

            with pool.Fori(0, B - 1) as b:
                with pool.Fori(0, BATCH_PAIRS) as j:
                    body(b * BATCH_PAIRS + j)
                scatter(b)
            with pool.Fori(0, BATCH_PAIRS - 2) as j:
                body((B - 1) * BATCH_PAIRS + j)
            body(PAIRS - 2, next_x=False)
            body(PAIRS - 1, next_x=False)
            scatter(B - 1)

            pool.wait_ge(n2_stored, 16 * (TILES + 2))
            pool.wait_ge(x2_stored, 16 * (TILES + 2))
            pool.wait_ge(pv_done, TURNS * TILES)

            def gather(t, j, count):
                pool.wait_ge(idg_ready, t + 1)
                if not isinstance(t, int) or t >= GROUP:
                    pool.wait_ge(xt_full, t - GROUP + 1)
                gate_op(count)
                pool.indirect_dma_start(
                    out=xg[:, j, :], out_offset=None, in_=n2_dram,
                    in_offset=bass.IndirectOffsetOnAxis(ap=idg[:, j, :], axis=0)).then_inc(gathered[j], 16)

            def add_rows(t, j, count):
                pool.wait_ge(y_done, t + 1)
                pool.wait_ge(ids_ready, t + 1)
                if not isinstance(t, int) or t > 0:
                    pool.wait_ge(added, 16 * t)
                gate_op(count)
                pool.indirect_dma_start(
                    out=out_rows, out_offset=bass.IndirectOffsetOnAxis(ap=ids[:, j % 2, :], axis=0),
                    in_=y[:, j % 2, :], in_offset=None, bounds_check=TOKENS - 1, oob_is_err=False,
                    compute_op=ALU.add).then_inc(added, 16)

            for t in range(AHEAD):
                gather(t, t, B + t)

            def group(g):
                for j in range(GROUP):
                    t = g * GROUP + j
                    gather(t + AHEAD, (j + AHEAD) % GROUP, B + AHEAD + 2 * t)
                    add_rows(t, j, B + AHEAD + 2 * t + 1)

            group(0)
            with pool.Fori(1, STEPS // GROUP - 1) as g:
                group(g)
            t = STEPS - GROUP
            gather(t + AHEAD, AHEAD, B + AHEAD + 2 * t)
            for j in range(GROUP):
                add_rows(t + j, j, B + AHEAD + 2 * t + 1 + j)

        @block.tensor
        def _(pe):
            mm = nc.tensor.matmul
            pe.wait_ge(ctx_in, 48)
            for f in range(DC):
                for h in range(2):
                    for c in range(DC):
                        last = mm(banks[:, 2 * f + h, 0:2 * SK], wk_sb[:, c, f * P:(f + 1) * P],
                                  ctx_sb[:, c, 2 * h:2 * h + 2, :], start=c == 0, stop=c == DC - 1)
                    last.then_inc(k_ps, 1)
            pe.wait_ge(wv_in, 32)
            for b in range(B):
                for kb, n in ((0, P), (1, KREST)):
                    for c in range(DC):
                        last = mm(banks[0:n, 4 + b, kb * D:(kb + 1) * D], ctx_sb[:, c, b, kb * P:kb * P + n],
                                  wv_sb[:, c, :], start=c == 0, stop=c == DC - 1)
                    last.then_inc(v_ps, 1)
            for b in range(B):
                pe.wait_ge(v_step, V_STEPS * (b + 1))
                if b == 0:
                    pe.wait_ge(kT_done, 4)
                else:
                    pe.wait_ge(vst_a, 2 * b)
                    pe.wait_ge(vst_d, 2 * b)
                for c in range(CHUNKS):
                    h0, k0 = divmod(P * c, SK)
                    for slot in range(2):
                        h = min(h0 + slot, H - 1)
                        o = banks[:, c // 5, (c % 5) * VCOLS:(c % 5 + 1) * VCOLS].rearrange(
                            "p (a s v) -> p a s v", a=3, s=2)[:, :, slot, :]
                        for kb, n in ((0, P), (1, KREST)):
                            last = mm(o, sel[0:n, 2 * kb + slot, k0:k0 + P], vp[kb][:, :, h, :],
                                      start=kb == 0 and slot == 0 and c % 5 == 0, stop=kb == 1, skip_group_check=True)
                    if c % 5 == 4:
                        last.then_inc(vsel_ps, 1)

            def turn_x(p, use):
                pe.wait_ge(ln1_step, LN1_STEPS * (p + 1))
                pe.wait_ge(tr_empty, use)
                for t in range(2):
                    for c in range(DC):
                        last = nc.tensor.transpose(TR[:, (2 * t + c) * P:(2 * t + c + 1) * P],
                                                   xn[:, t, c * P:(c + 1) * P], ident)
                last.then_inc(tr_full, 1)

            def project_q(tr, use):
                pe.wait_ge(tr_empty, tr + 1)
                pe.wait_ge(pj_empty, use)
                for f in range(DC):
                    for c in range(DC):
                        last = mm(PJ[:, f * 2 * P:(f + 1) * 2 * P], wq_sb[:, c, f * P:(f + 1) * P],
                                  xnT[:, :, c, :], start=c == 0, stop=c == DC - 1, skip_group_check=True)
                last.then_inc(pj_full, 1)

            def scores(n, par, batch, g, first=False):
                c, h, w = GROUPS[g]
                if not (first and g < SLOTS):
                    pe.wait_ge(s_empty, 6 * n + g - 2)
                mm(SC[g % SLOTS][:, 0:w * SK], qT[:, c, par * P:(par + 1) * P],
                   KB[:, bass.ds(batch * COLS + (c * HALF + h * SK), w * SK)],
                   start=True, stop=True).then_inc(s_full, 1)

            def turn_probs(k, par, j, first=False):
                pe.wait_ge(exp_done, 2 * k + (1 if (j + 1) * 4 * P <= HALF else 2))
                if not (first and j < 2):
                    pe.wait_ge(pt_empty, TURNS * k + j - 1)
                for c in range(4):
                    last = nc.tensor.transpose(PT[(par + j) % 2][:, c * P:(c + 1) * P],
                                               SX[:, par, (4 * j + c) * P:(4 * j + c + 1) * P], ident)
                last.then_inc(pt_full, 1)

            def weigh(k, par, j, nth):
                pe.wait_ge(pt_empty, TURNS * k + j + 1)
                if j == 0:
                    pe.wait_ge(vc_loaded[par], 16 * (nth + 1))
                    pe.wait_ge(attn_done, k)
                for c in range(4 * j, 4 * j + 4):
                    h0 = P * c // SK
                    w = VH if h0 == H - 1 else 2 * VH
                    for n, (probs, part) in enumerate(((hi, 0), (hi, 1), (hi, 2), (lo, 0), (lo, 1))):
                        at = c * VCOLS + part * 2 * VH
                        last = mm(O[:, h0 * VH:h0 * VH + w], probs[:, c * P:(c + 1) * P],
                                  Vc[:, par, at:at + w], start=c == 0 and n == 0,
                                  stop=c == CHUNKS - 1 and n == 4, skip_group_check=True)
                last.then_inc(pv_done, 1)

            def turn_attn(m, use):
                pe.wait_ge(attn_done, m + 1)
                pe.wait_ge(tr_empty, use)
                for c in range(DC):
                    last = nc.tensor.transpose(TR[:, c * P:(c + 1) * P], attn[:, c * P:(c + 1) * P], ident)
                last.then_inc(tr_full, 1)

            def project_out(tr, use):
                pe.wait_ge(tr_empty, tr + 1)
                pe.wait_ge(pj_empty, use)
                for c in range(DC):
                    last = mm(PJ[:, 0:D], atT[:, c, :], wo_sb[:, c, :], start=c == 0, stop=c == DC - 1)
                last.then_inc(pj_full, 1)

            def turn_n2(m, par, use):
                pe.wait_ge(n2_done, m + 1)
                pe.wait_ge(tr_empty, use)
                for c in range(DC):
                    last = nc.tensor.transpose(TR[:, c * P:(c + 1) * P], n2[:, par, c * P:(c + 1) * P], ident)
                last.then_inc(tr_full, 1)

            def logits(tr, use):
                pe.wait_ge(tr_empty, tr + 1)
                pe.wait_ge(pj_empty, use)
                for c in range(DC):
                    last = mm(PJ[0:E, 0:2 * P], wr_sb[:, c, :], n2T[:, c, :], start=c == 0, stop=c == DC - 1)
                last.then_inc(pj_full, 1)

            def turn_logits():
                for t in range(2):
                    last = nc.tensor.transpose(PJ[:, t * E:(t + 1) * E], lgT[:, t * P:(t + 1) * P], ident[0:E, 0:E])
                last.then_inc(pj_full, 1)

            def count_experts(b, use):
                pe.wait_ge(rt_step, ROUTE_STEPS * b + 18)
                pe.wait_ge(pj_empty, use)
                mm(PJ[:, 0:T8 * E], tri[:], Mb[:].rearrange("p t e -> p (t e)"), start=True, stop=False, skip_group_check=True)
                for t in range(T8):
                    last = mm(PJ[:, (t + 1) * E:(T8 + 1) * E].rearrange("p (t e) -> p t e", e=E), ones[:],
                              Mb[:, t, :].unsqueeze(1).broadcast_to([P, T8 - t, E]),
                              start=False, stop=t == T8 - 1, skip_group_check=True)
                last.then_inc(pj_full, 1)

            def tick(n, k, m, par, i, b, batch_n, first=False, has_s=True, has_x=True, last_pair=False):
                odd = par == 1
                if has_s:
                    scores(n, par, batch_n, 0, first)
                    scores(n, par, batch_n, 1, first)
                if m is not None:
                    turn_attn(m, tr_use(i, 2 * par, last_pair))
                if has_s:
                    scores(n, par, batch_n, 2, first)
                if k is not None:
                    turn_probs(k, 1 - par, 0, first=isinstance(k, int) and k == 0)
                if m is not None:
                    project_out(tr_use(i, 2 * par, last_pair), pj_use(i, b, par, last_pair))
                if has_s:
                    scores(n, par, batch_n, 3)
                nth = None
                if k is not None:
                    nth = i + par
                    turn_probs(k, 1 - par, 1, first=isinstance(k, int) and k == 0)
                    weigh(k, 1 - par, 0, nth)
                if has_s:
                    scores(n, par, batch_n, 4)
                if k is not None:
                    turn_probs(k, 1 - par, 2)
                    weigh(k, 1 - par, 1, nth)
                if has_s:
                    scores(n, par, batch_n, 5)
                if k is not None:
                    turn_probs(k, 1 - par, 3)
                    weigh(k, 1 - par, 2, nth)
                if m is not None:
                    turn_n2(m, par, tr_use(i, 2 * par + 1, last_pair))
                if k is not None:
                    turn_probs(k, 1 - par, 4)
                    weigh(k, 1 - par, 3, nth)
                if odd and m is not None:
                    logits(tr_use(i, 3, last_pair), pj_use(i, b, 2, last_pair))
                if odd and has_x:
                    turn_x(i + 2, tr_use(i, 4))
                if odd and m is not None:
                    pe.wait_ge(pj_empty, pj_use(i, b, 3, last_pair))
                if k is not None:
                    weigh(k, 1 - par, 4, nth)
                if odd and m is not None:
                    turn_logits()
                if odd and has_x:
                    project_q(tr_use(i, 4), pj_use(i, b, 4))

            def body(i, b, **kw):
                n = i * 2 + 2
                batch_n = (i + 1) // BATCH_PAIRS
                tick(n, n - 1, n - 2, 0, i, b, batch_n, **kw)
                if kw.get("has_s", True):
                    tick(n + 1, n, n - 1, 1, i, b, batch_n, **kw)
                else:
                    tick(n + 1, None, n - 1, 1, i, b, batch_n, **kw)

            pe.wait_ge(wts_in, 96)
            pe.wait_ge(cst_in_s, 32)
            turn_x(0, 0)
            project_q(0, 0)
            pe.wait_ge(pj_empty, 1)
            pe.wait_ge(KB_done, 16)
            pe.wait_ge(vst_a, 2 * B)
            pe.wait_ge(vst_d, 2 * B)
            pe.wait_ge(init_done, 5)
            for g in range(6):
                scores(0, 0, 0, g, first=True)
            for g in range(3):
                scores(1, 1, 0, g)
            turn_probs(0, 0, 0, first=True)
            scores(1, 1, 0, 3)
            turn_probs(0, 0, 1, first=True)
            weigh(0, 0, 0, 0)
            scores(1, 1, 0, 4)
            turn_probs(0, 0, 2)
            weigh(0, 0, 1, 0)
            scores(1, 1, 0, 5)
            turn_probs(0, 0, 3)
            weigh(0, 0, 2, 0)
            turn_probs(0, 0, 4)
            weigh(0, 0, 3, 0)
            turn_x(1, 1)
            weigh(0, 0, 4, 0)
            project_q(1, 1)
            with pe.Fori(0, B - 1) as b:
                with pe.Fori(0, BATCH_PAIRS) as j:
                    i = b * BATCH_PAIRS + j
                    pe.wait_ge(pj_empty, pj_use(i, b, 0))
                    body(i, b)
                count_experts(b, pj_use(b * BATCH_PAIRS + BATCH_PAIRS, b, 0))
            b = B - 1
            with pe.Fori(0, BATCH_PAIRS - 2) as j:
                i = b * BATCH_PAIRS + j
                pe.wait_ge(pj_empty, pj_use(i, b, 0))
                body(i, b)
            pe.wait_ge(pj_empty, pj_use(PAIRS - 2, b, 0))
            body(PAIRS - 2, b, has_x=False)
            body(PAIRS - 1, b, has_s=False, has_x=False, last_pair=True)
            count_experts(b, pj_use(PAIRS - 1, b, 4, True))

            pe.wait_ge(pj_empty, pj_use(PAIRS - 1, b, 4, True) + 1)
            pe.wait_ge(meta_step, META_STEPS)
            pe.wait_ge(experts_in, 32 * E)

            def turn_tokens(t, j, g):
                pe.wait_ge(gathered[j], 16 * (g + 1))
                if not isinstance(t, int) or t > 0:
                    pe.wait_ge(xt_empty, t)
                for c in range(DC):
                    last = nc.tensor.transpose(XTp[:, c * P:(c + 1) * P], xg[:, j, c * P:(c + 1) * P], ident)
                last.then_inc(xt_full, 1)

            def up(t, par):
                v = pe.value_load(exw[0:1, bass.ds(t, 1)], min_val=0, max_val=(E - 1) * EW)
                pe.wait_ge(xt_empty, t + 1)
                if not isinstance(t, int) or t > 1:
                    pe.wait_ge(gelu_done, 2 * (t - 1))
                for u in range(2):
                    for c in range(DC):
                        last = mm(UP[par][u], xgT[:, par, c, :], W[:, bass.ds(v + (c * F + u * 512), 512)],
                                  start=c == 0, stop=c == DC - 1)
                    last.then_inc(up_full, 1)
                return v

            def turn_hidden(t, par):
                for u in range(2):
                    pe.wait_ge(gelu_done, 2 * t + u + 1)
                    if not isinstance(t, int) or t > 0:
                        pe.wait_ge(ht_dve if u == 0 else ht_act, t)
                    for c in range(4):
                        k = 4 * u + c
                        last = nc.tensor.transpose(HTp[u][:, c * P:(c + 1) * P], hh[:, par, k * P:(k + 1) * P], ident)
                    last.then_inc(ht_full, 1)

            def down(t, par):
                v = pe.value_load(exw[0:1, bass.ds(t, 1)], min_val=0, max_val=(E - 1) * EW)
                for k in range(F // P):
                    if k == 0:
                        pe.wait_ge(ht_dve, t + 1)
                        if not isinstance(t, int) or t > 0:
                            pe.wait_ge(y_done, t)
                    if k == 4:
                        pe.wait_ge(ht_act, t + 1)
                    last = mm(Y[:, 0:D], hT[:, par, k * P:(k + 1) * P], W[:, bass.ds(v + (DOWN_AT + k * D), D)],
                              start=k == 0, stop=k == F // P - 1)
                last.then_inc(y_full, 1)

            def step(t, j, g, turn=True, more=True):
                turn_hidden(t, j % 2)
                if more:
                    up(t + 1, (j + 1) % 2)
                if turn:
                    turn_tokens(t + 2, (j + 2) % GROUP, g + (j + 2) // GROUP)
                down(t, j % 2)

            turn_tokens(0, 0, 0)
            up(0, 0)
            turn_tokens(1, 1, 0)
            for j in range(GROUP):
                step(j, j, 0)
            with pe.Fori(1, STEPS // GROUP - 1) as g:
                for j in range(GROUP):
                    step(g * GROUP + j, j, g)
            for j in range(GROUP):
                step(STEPS - GROUP + j, j, STEPS // GROUP - 1, turn=j < GROUP - 2, more=j < GROUP - 1)

        @block.scalar
        def _(act):
            A = nc.scalar.activation
            for e in range(EARLY):
                act.dma_start(W[:, e * EW:e * EW + DOWN_AT].rearrange("p (c f) -> p c f", c=DC), upT[e].rearrange("(c p) f -> p c f", p=P)).then_inc(experts_in, 16)
                act.dma_start(W[:, e * EW + DOWN_AT:(e + 1) * EW].rearrange("p (k d) -> p k d", d=D), dnT[e].rearrange("(k p) d -> p k d", p=P)).then_inc(experts_in, 16)
            act.wait_ge(ctx_in, 48)
            for f in range(DC):
                for h in range(2):
                    act.wait_ge(k_ps, 2 * f + h + 1)
                    A(kT[:, f, 2 * h:2 * h + 2, :], banks[:, 2 * f + h, 0:2 * SK].rearrange("p (b k) -> p b k", b=2), ACT.Identity,
                      bias=bk_sb[:, f:f + 1]).then_inc(kT_done, 1)
            for b in range(B):
                for g in range(2):
                    act.wait_ge(vsel_ps, 4 * b + g + 1)
                    if b > 0:
                        act.wait_ge(v_stored, 16 * b)
                    A(v_st[:, g * 5 * VCOLS:(g + 1) * 5 * VCOLS], banks[:, g, 0:5 * VCOLS], ACT.Copy).then_inc(vst_a, 1)

            act.wait_ge(wts_in, 96)

            def take_xnT(tr, prev_q):
                act.wait_ge(tr_full, tr + 1)
                if prev_q is not None:
                    act.wait_ge(pj_full, prev_q + 1)
                A(xnT[:], TR[:].rearrange("p (t c k) -> p t c k", t=2, c=DC), ACT.Copy).then_inc(tr_empty, 1)

            def take_q(pj):
                act.wait_ge(pj_full, pj + 1)
                A(qT[:, 0, :], PJ[:, 0:2 * P], ACT.Identity, bias=bq_sb[:, 0:1])
                A(qT[:, 1, :], PJ[:, 2 * P:4 * P], ACT.Identity, bias=bq_sb[:, 1:2]).then_inc(pj_empty, 1)

            def expo(n, par, half):
                act.wait_ge(s_empty, 6 * n + 3 * (half + 1))
                e = SX[:, par, half * HALF:(half + 1) * HALF]
                A(e, e, ACT.Exp).then_inc(exp_done, 1)

            def take_hi(k, par, j, first=False):
                act.wait_ge(pt_full, TURNS * k + j + 1)
                if not first:
                    act.wait_ge(pv_done, TURNS * (k - 1) + j + 1)
                A(hi[:, j * 4 * P:(j + 1) * 4 * P], PT[(par + j) % 2], ACT.Copy).then_inc(hi_done, 1)

            def take_atT(tr, prev_out):
                act.wait_ge(tr_full, tr + 1)
                if prev_out is not None:
                    act.wait_ge(pj_full, prev_out + 1)
                A(atT[:], TR[:, 0:D].rearrange("p (c k) -> p c k", c=DC), ACT.Copy).then_inc(tr_empty, 1)

            def take_n2T(tr, par, prev_lg):
                act.wait_ge(tr_full, tr + 1)
                if prev_lg is not None:
                    act.wait_ge(pj_full, prev_lg + 1)
                A(n2T[:, :, par * P:(par + 1) * P], TR[:, 0:D].rearrange("p (c k) -> p c k", c=DC), ACT.Copy).then_inc(tr_empty, 1)

            def take_lgT(pj):
                act.wait_ge(pj_full, pj + 1)
                A(lgT[:], PJ[0:E, 0:2 * P], ACT.Identity, bias=br_sb[:, 0:1]).then_inc(pj_empty, 1)

            def take_lg(pj, b, j):
                act.wait_ge(pj_full, pj + 1)
                act.wait_ge(rt_step, ROUTE_STEPS * b + 1)
                A(Lg[:, bass.ds(j * 2 * E, 2 * E)], PJ[:, 0:2 * E], ACT.Copy).then_inc(pj_empty, 1)

            def router_exp(b):
                act.wait_ge(rt_step, ROUTE_STEPS * b + 3)
                A(rt[:, 1], rt[:, 0], ACT.Exp).then_inc(rt_exp, 1)

            def tick(n, k, m, par, i, b, j, has_s=True, has_x=True, last_pair=False):
                odd = par == 1
                first_k = isinstance(k, int) and k == 0
                if m is not None:
                    prev = pj_use(i, b, 0, last_pair) if odd else None
                    if not odd and not (isinstance(i, int) and i == 0):
                        prev = pj_use(i, b, 0, last_pair) - 1
                    take_atT(tr_use(i, 2 * par, last_pair), prev)
                if k is not None:
                    take_hi(k, 1 - par, 0, first_k)
                if has_s:
                    expo(n, par, 0)
                if k is not None:
                    for t in (1, 2, 3):
                        take_hi(k, 1 - par, t, first_k)
                if has_s:
                    expo(n, par, 1)
                if m is not None:
                    prev = None
                    if not (isinstance(i, int) and i == 0):
                        prev = pj_use(i, b, 0, last_pair) - 1
                    take_n2T(tr_use(i, 2 * par + 1, last_pair), par, prev)
                if k is not None:
                    take_hi(k, 1 - par, 4, first_k)
                if odd and m is not None:
                    take_lgT(pj_use(i, b, 2, last_pair))
                if odd and has_x:
                    take_xnT(tr_use(i, 4), pj_use(i, b, 0) - 1)
                if odd and m is not None:
                    take_lg(pj_use(i, b, 3, last_pair), b, j)
                if odd and has_x:
                    take_q(pj_use(i, b, 4))

            def body(i, b, j, **kw):
                n = i * 2 + 2
                tick(n, n - 1, n - 2, 0, i, b, j, **kw)
                tick(n + 1, n if kw.get("has_s", True) else None, n - 1, 1, i, b, j, **kw)

            take_xnT(0, None)
            take_q(0)
            expo(0, 0, 0)
            expo(0, 0, 1)
            take_hi(0, 0, 0, True)
            expo(1, 1, 0)
            for t in (1, 2, 3):
                take_hi(0, 0, t, True)
            expo(1, 1, 1)
            take_hi(0, 0, 4, True)
            take_xnT(1, 0)
            take_q(1)
            with act.Fori(0, B - 1) as b:
                with act.Fori(0, BATCH_PAIRS) as j:
                    body(b * BATCH_PAIRS + j, b, j)
                router_exp(b)
            b = B - 1
            with act.Fori(0, BATCH_PAIRS - 2) as j:
                body(b * BATCH_PAIRS + j, b, j)
            body(PAIRS - 2, b, BATCH_PAIRS - 2, has_x=False)
            body(PAIRS - 1, b, BATCH_PAIRS - 1, has_s=False, has_x=False, last_pair=True)
            router_exp(b)

            def take_xgT(t, par):
                act.wait_ge(xt_full, t + 1)
                if not isinstance(t, int) or t > 1:
                    act.wait_ge(up_full, 2 * (t - 1))
                A(xgT[:, par], XTp[:, 0:D].rearrange("p (c k) -> p c k", c=DC), ACT.Copy).then_inc(xt_empty, 1)

            def gelu(t, par):
                for u in range(2):
                    act.wait_ge(up_full, 2 * t + u + 1)
                    if u == 0 and (not isinstance(t, int) or t > 1):
                        act.wait_ge(ht_full, 2 * (t - 1))
                    A(hh[:, par, u * 512:(u + 1) * 512], UP[par][u], ACT.Gelu).then_inc(gelu_done, 1)

            def take_hT(t, par):
                act.wait_ge(ht_full, 2 * t + 2)
                if not isinstance(t, int) or t > 1:
                    act.wait_ge(y_full, t - 1)
                A(hT[:, par, 4 * P:8 * P], HTp[1], ACT.Copy).then_inc(ht_act, 1)

            act.wait_ge(pv_done, TURNS * TILES)
            take_xgT(0, 0)
            gelu(0, 0)
            take_xgT(1, 1)

            def step(t, par):
                take_hT(t, par)
                gelu(t + 1, 1 - par)
                take_xgT(t + 2, par)

            step(0, 0)
            step(1, 1)
            with act.Fori(1, STEPS // 2 - 1) as s:
                step(s * 2, 0)
                step(s * 2 + 1, 1)
            take_hT(STEPS - 2, 0)
            gelu(STEPS - 1, 1)
            take_hT(STEPS - 1, 1)

        @block.vector
        def _(dve):
            V = nc.vector
            V.sem_inc(rt_step, 1)
            dve.wait_ge(cst_in_s, 32)
            V.memset(ones[:], 1.0)
            V.tensor_copy(tri[:], cst[:, C_TRI:C_TRI + P])
            V.tensor_copy(sel[:], sel_f)
            V.tensor_copy(tok[:], cst[:, C_TOK:C_TOK + T8])
            V.memset(cnt[:], 0.0)
            for v in vp:
                V.memset(v[:, 0, :, HD:VH], 1.0)
                V.memset(v[:, 1:3, :, HD:VH], 0.0)
            dve.wait_ge(kT_done, 4)
            KBv = KB.rearrange("p (b c h k) -> p b c h k", b=B, c=DC, k=SK)
            for f in range(DC):
                for h in range(H // DC):
                    V.tensor_scalar(KBv[:, :, f, h, :], kT[:, f], cst[:, C_HM + h:C_HM + h + 1], None, ALU.mult).then_inc(KB_done, 1)
            dve.wait_ge(wv_in, 32)
            for b in range(B):
                steps = V_STEPS * b

                def link(ins):
                    nonlocal steps
                    steps += 1
                    ins.then_inc(v_step, 1)
                    dve.wait_ge(v_step, steps)

                for kb, n in ((0, P), (1, KREST)):
                    dve.wait_ge(v_ps, 2 * b + 2)
                    if b > 0 and kb == 0:
                        dve.wait_ge(vsel_ps, 4 * b)
                    part = [vp[kb][0:n, a, :, 0:HD] for a in range(3)]
                    whole = v_f[0:n, :].rearrange("p (h d) -> p h d", h=H)
                    rest = v_r[0:n, :].rearrange("p (h d) -> p h d", h=H)
                    link(V.tensor_tensor(v_f[0:n, :], banks[0:n, 4 + b, kb * D:(kb + 1) * D], bv_bc[0:n, :], ALU.add))
                    link(V.tensor_copy(part[0], whole))
                    link(V.tensor_tensor(rest, whole, part[0], ALU.subtract))
                    link(V.tensor_copy(part[1], rest))
                    link(V.tensor_tensor(part[2], rest, part[1], ALU.subtract))
                for g in range(2, 4):
                    dve.wait_ge(vsel_ps, 4 * b + g + 1)
                    if b > 0:
                        dve.wait_ge(v_stored, 16 * b)
                    V.tensor_copy(v_st[:, g * 5 * VCOLS:(g + 1) * 5 * VCOLS], banks[:, g, 0:5 * VCOLS]).then_inc(vst_d, 1)

            dve.wait_ge(wts_in, 96)
            dve.wait_ge(init_done, 5)

            def ln1_stats(p):
                dve.wait_ge(x_loaded, 16 * p + 16)
                V.bn_stats(st1[:, 0, :], xt[:, 0, :])
                V.bn_stats(st1[:, 1, :], xt[:, 1, :]).then_inc(ln1_step, 1)

            def ln1_aggr(p, alone=False):
                if alone:
                    dve.wait_ge(ln1_step, LN1_STEPS * p + 1)
                V.bn_aggr(mv1[:, 0, :], st1[:, 0, :])
                V.bn_aggr(mv1[:, 1, :], st1[:, 1, :]).then_inc(ln1_step, 1)

            def ln1_apply(p, turned):
                dve.wait_ge(ln1_rstd, 2 * p + 2)
                dve.wait_ge(tr_full, turned)
                for t in range(2):
                    last = V.tensor_scalar(xn[:, t, :], xt[:, t, :], mv1[:, t, 0:1], rs1[:, t:t + 1], ALU.subtract, ALU.mult)
                last.then_inc(ln1_step, 1)

            def take_scores(n, par, g, first=False, stats=None, summed=None):
                c, h, w = GROUPS[g]
                at, h = c * HALF + h * SK, c * (H // DC) + h
                s = SC[g % SLOTS][:, 0:w * SK].rearrange("p (h k) -> p h k", k=SK)
                dve.wait_ge(s_full, 6 * n + g + 1)
                V.tensor_reduce(mx[:, h:h + w], s, AX.X, ALU.max).then_inc(s_max, 1)
                if stats:
                    stats()
                    dve.wait_ge(*summed)
                if g == 0 and not first:
                    dve.wait_ge(pt_full, TURNS * (n - 1))
                dve.wait_ge(s_max, 6 * n + g + 1)
                V.tensor_tensor(SX[:, par, at:at + w * SK].rearrange("p (h k) -> p h k", k=SK), s,
                                mx[:, h:h + w].unsqueeze(2).broadcast_to([P, w, SK]), ALU.subtract).then_inc(s_empty, 1)

            def take_lo(k, par, j, first=False):
                dve.wait_ge(hi_done, TURNS * k + j + 1)
                if not first:
                    dve.wait_ge(pv_done, TURNS * (k - 1) + j + 1)
                at = slice(j * 4 * P, (j + 1) * 4 * P)
                V.tensor_tensor(lo[:, at], PT[(par + j) % 2], hi[:, at], ALU.subtract).then_inc(pt_empty, 1)

            def normalise(k, turned):
                Ov = O[:, 0:H * VH].rearrange("p (h v) -> p h v", v=VH)
                dve.wait_ge(pv_done, TURNS * (k + 1))
                V.reciprocal(rden[:], Ov[:, :, HD]).then_inc(rden_done, 1)
                if turned is not None:
                    dve.wait_ge(tr_full, turned)
                dve.wait_ge(rden_done, k + 1)
                V.tensor_tensor(attn[:].rearrange("p (h d) -> p h d", h=H), Ov[:, :, 0:HD],
                                rden[:].unsqueeze(2).broadcast_to([P, H, HD]), ALU.mult).then_inc(attn_done, 1)

            def add_residual(m, par, pj):
                dve.wait_ge(pj_full, pj + 1)
                dve.wait_ge(xr_ready, m + 1)
                dve.wait_ge(x2_stored, 16 * m + 16)
                V.tensor_tensor(x2[:, par, :], PJ[:, 0:D], xr[:, par, :], ALU.add).then_inc(pj_empty, 1)

            def ln2_stats(m, par, pj):
                dve.wait_ge(pj_empty, pj + 1)
                V.bn_stats(st2[:], x2[:, par, :]).then_inc(ln2_step, 1)

            def ln2_aggr(m, alone):
                if alone:
                    dve.wait_ge(ln2_step, 2 * m + 1)
                V.bn_aggr(mv2[:], st2[:]).then_inc(ln2_step, 1)

            def ln2_apply(m, par, turned):
                dve.wait_ge(ln2_rstd, 2 * m + 2)
                dve.wait_ge(tr_full, turned)
                dve.wait_ge(n2_stored, 16 * m + 16)
                V.tensor_scalar(n2[:, par, :], x2[:, par, :], mv2[:, 0:1], rs2[:, 1:2], ALU.subtract, ALU.mult).then_inc(n2_done, 1)

            def tick(n, k, m, par, i, b, has_s=True, has_x=True, last_pair=False):
                odd = par == 1
                first_k = isinstance(k, int) and k == 0
                if has_s:
                    take_scores(n, par, 0)
                    if odd and has_x:
                        take_scores(n, par, 1, stats=lambda: ln1_stats(i + 2), summed=(ln1_step, LN1_STEPS * (i + 2) + 1))
                        ln1_aggr(i + 2)
                    else:
                        take_scores(n, par, 1)
                if has_s:
                    take_scores(n, par, 2)
                if k is not None:
                    take_lo(k, 1 - par, 0, first_k)
                pj = pj_use(i, b, par, last_pair)
                add_residual(m, par, pj)
                if has_s:
                    take_scores(n, par, 3, stats=lambda: ln2_stats(m, par, pj), summed=(ln2_step, 2 * m + 1))
                else:
                    ln2_stats(m, par, pj)
                ln2_aggr(m, not has_s)
                if k is not None:
                    take_lo(k, 1 - par, 1, first_k)
                if has_s:
                    take_scores(n, par, 4)
                if k is not None:
                    take_lo(k, 1 - par, 2, first_k)
                ln2_apply(m, par, tr_use(i, 0, last_pair))
                if odd and has_x:
                    ln1_apply(i + 2, tr_use(i, 0))
                if has_s:
                    take_scores(n, par, 5)
                if k is not None:
                    take_lo(k, 1 - par, 3, first_k)
                    take_lo(k, 1 - par, 4, first_k)
                    normalise(k, tr_use(i, 2 * par, last_pair) + 1)

            def body(i, b, **kw):
                n = i * 2 + 2
                tick(n, n - 1, n - 2, 0, i, b, **kw)
                tick(n + 1, n if kw.get("has_s", True) else None, n - 1, 1, i, b, **kw)

            def route(b, lg, count):
                steps = 0

                def link(ins):
                    nonlocal steps
                    steps += 1
                    ins.then_inc(rt_step, 1)
                    dve.wait_ge(rt_step, ROUTE_STEPS * b + steps + 1)

                def over_e(v):
                    return v.unsqueeze(2).broadcast_to([P, T8, E])

                def over_t(v):
                    return v.unsqueeze(1).broadcast_to([P, T8, E])

                less, prob, pick, best, second, left, row = (rt[:, a] for a in range(7))
                top, total, inv, w1, first_at, w2 = (rs[:, a] for a in range(6))
                desc = cst[:, C_DESC:C_DESC + E]
                L = Lg[:].rearrange("p (t e) -> p t e", e=E)
                dve.wait_ge(pj_empty, lg + 1)
                link(V.tensor_reduce(top, L, AX.X, ALU.max))
                link(V.tensor_tensor(less, L, over_e(top), ALU.subtract))
                dve.wait_ge(rt_exp, b + 1)
                link(V.tensor_reduce(total, prob, AX.X, ALU.add))
                link(V.reciprocal(inv, total))
                link(V.tensor_tensor(prob, prob, over_e(inv), ALU.mult))
                for p_, w, one in ((prob, w1, best), (left, w2, second)):
                    link(V.tensor_reduce(w, p_, AX.X, ALU.max))
                    link(V.tensor_tensor(pick, p_, over_e(w), ALU.is_equal))
                    link(V.tensor_tensor(pick, pick, over_t(desc), ALU.mult))
                    link(V.tensor_reduce(first_at, pick, AX.X, ALU.max))
                    link(V.tensor_tensor(one, pick, over_e(first_at), ALU.is_equal))
                    if one is best:
                        link(V.scalar_tensor_tensor(left, best, -2.0, prob, ALU.mult, ALU.add))
                link(V.tensor_tensor(Mb[:], best, second, ALU.add))
                dve.wait_ge(pj_full, count + 1)
                link(V.tensor_tensor(row, PJ[:, 0:T8 * E].rearrange("p (t e) -> p t e", e=E), over_t(cnt[:]), ALU.add))
                V.tensor_tensor(cnt[:], cnt[:], PJ[:, T8 * E:(T8 + 1) * E], ALU.add).then_inc(pj_empty, 1)
                link(V.tensor_tensor(row, row, over_t(cst[:, C_BASE:C_BASE + E]), ALU.add))
                dve.wait_ge(scattered, 16 * 2 * T8 * b + 16)
                for k, one in enumerate((best, second)):
                    link(V.tensor_tensor(pick, one, row, ALU.mult))
                    link(V.tensor_reduce(rs[:, 6 + k], pick, AX.X, ALU.add))
                V.tensor_copy(pos[:], rs[:, 6:8])
                for k, w in enumerate((w1, w2)):
                    V.tensor_copy(ent[:, :, k, 0], tok[:])
                    V.tensor_copy(ent[:, :, k, 1], w)
                link(V.tensor_scalar(tok[:], tok[:], float(S), None, ALU.add))
                assert steps == ROUTE_STEPS, steps

            ln1_stats(0)
            ln1_aggr(0, alone=True)
            ln1_apply(0, 0)
            for g in range(6):
                take_scores(0, 0, g, first=True)
            take_scores(1, 1, 0, first=True)
            take_scores(1, 1, 1)
            ln1_stats(1)
            ln1_aggr(1, alone=True)
            take_scores(1, 1, 2)
            take_lo(0, 0, 0, True)
            take_scores(1, 1, 3)
            take_lo(0, 0, 1, True)
            take_scores(1, 1, 4)
            take_lo(0, 0, 2, True)
            ln1_apply(1, 1)
            take_scores(1, 1, 5)
            take_lo(0, 0, 3, True)
            take_lo(0, 0, 4, True)
            normalise(0, None)
            with dve.Fori(0, B - 1) as b:
                with dve.Fori(0, BATCH_PAIRS) as j:
                    body(b * BATCH_PAIRS + j, b)
                route(b, pj_use(b * BATCH_PAIRS + BATCH_PAIRS - 1, b, 3), pj_use(b * BATCH_PAIRS + BATCH_PAIRS, b, 0))
            b = B - 1
            with dve.Fori(0, BATCH_PAIRS - 2) as j:
                body(b * BATCH_PAIRS + j, b)
            body(PAIRS - 2, b, has_x=False)
            body(PAIRS - 1, b, has_s=False, has_x=False, last_pair=True)
            route(b, pj_use(PAIRS - 1, b, 3, True), pj_use(PAIRS - 1, b, 4, True))

            steps = 0

            def link(ins):
                nonlocal steps
                steps += 1
                ins.then_inc(meta_step, 1)
                dve.wait_ge(meta_step, steps)

            row0 = SX[0:1, 0, :]
            past = row0[:, 0:STEPS * (E - 1)].rearrange("p (j e) -> p j e", e=E - 1)
            past_n = row0[:, 512:512 + STEPS * (E - 1)].rearrange("p (j e) -> p j e", e=E - 1)
            over = row0[:, 1024:1024 + E * 32].rearrange("p (e m) -> p e m", e=E)
            blocks, ends, unit = (blk[0:1, a, :] for a in range(3))
            expert, start, within = (meta[0:1, a, :] for a in range(3))
            js = cst[0:1, C_J:C_J + STEPS]
            V.memset(unit, 1.0)
            link(V.tensor_tensor(over, cnt[0:1, :].unsqueeze(2).broadcast_to([1, E, 32]),
                                 cst[0:1, C_M:C_M + 32].unsqueeze(1).broadcast_to([1, E, 32]), ALU.is_gt))
            link(V.tensor_reduce(blocks, over, AX.X, ALU.add))
            link(V.tensor_tensor_scan(ends, unit, blocks, 0.0, ALU.mult, ALU.add))
            link(V.tensor_tensor(past, js.unsqueeze(2).broadcast_to([1, STEPS, E - 1]),
                                 ends[:, 0:E - 1].unsqueeze(1).broadcast_to([1, STEPS, E - 1]), ALU.is_ge))
            link(V.tensor_reduce(expert, past, AX.X, ALU.add))
            link(V.tensor_tensor(past_n, past, blocks[:, 0:E - 1].unsqueeze(1).broadcast_to([1, STEPS, E - 1]), ALU.mult))
            link(V.tensor_reduce(start, past_n, AX.X, ALU.add))
            link(V.tensor_scalar(exw[:], expert, float(EW), None, ALU.mult))
            link(V.tensor_tensor(within, js, start, ALU.subtract))
            link(V.tensor_scalar(within, within, float(P), None, ALU.mult))
            link(V.scalar_tensor_tensor(off[:], expert, float(LIST), within, ALU.mult, ALU.add))
            assert steps == META_STEPS

            def rows_to_gather(t, j, g):
                dve.wait_ge(lst_loaded, 16 * GROUP * (g + 1))
                if not isinstance(g, int) or g > 0:
                    dve.wait_ge(gathered[j], 16 * g)
                V.tensor_scalar(idg[:, j, :], lst[:, bass.ds(t, 1), 0], float(TOKENS - 1), None, ALU.min).then_inc(idg_ready, 1)

            def rows_to_add(t, par):
                if not isinstance(t, int) or t > 1:
                    dve.wait_ge(added, 16 * (t - 1))
                V.tensor_scalar(ids[:, par, :], lst[:, bass.ds(t, 1), 0], 0.0, None, ALU.max).then_inc(ids_ready, 1)

            def take_hT(t, par):
                dve.wait_ge(ht_full, 2 * t + 1)
                if not isinstance(t, int) or t > 1:
                    dve.wait_ge(y_full, t - 1)
                V.tensor_copy(hT[:, par, 0:4 * P], HTp[0]).then_inc(ht_dve, 1)

            def take_y(t, par):
                dve.wait_ge(y_full, t + 1)
                if not isinstance(t, int) or t > 1:
                    dve.wait_ge(added, 16 * (t - 1))
                V.tensor_scalar(y[:, par, :], Y[:, 0:D], lst[:, bass.ds(t, 1), 1], None, ALU.mult).then_inc(y_done, 1)

            for t in range(AHEAD):
                rows_to_gather(t, t, 0)

            def group(g, more=True):
                for j in range(GROUP):
                    t = g * GROUP + j
                    if more or j + AHEAD < GROUP:
                        rows_to_gather(t + AHEAD, (j + AHEAD) % GROUP, g + (j + AHEAD) // GROUP)
                    take_hT(t, j % 2)
                    rows_to_add(t, j % 2)
                    take_y(t, j % 2)

            group(0)
            with dve.Fori(1, STEPS // GROUP - 1) as g:
                group(g)
            group(STEPS // GROUP - 1, more=False)


def kernel(**inputs):
    import numpy as np
    import concourse.bacc as bacc
    from concourse.bass_utils import run_bass_kernel_spmd

    g = {k: np.asarray(v) for k, v in inputs.items()}
    cst = np.zeros((P, C_ALL), np.float32)
    p = np.arange(P)
    cst[:, C_ID:C_ID + P] = np.eye(P)
    cst[:, C_TRI:C_TRI + P] = p[:, None] < p[None, :]
    cst[:, C_HM:C_HM + H // DC] = (p[:, None] // HD == np.arange(H // DC)[None, :]) * HD ** -0.5
    cst[:, C_DESC:C_DESC + E] = E - np.arange(E)
    cst[:, C_BASE:C_BASE + E] = LIST * np.arange(E)
    cst[:, C_TOK:C_TOK + BATCH_TILES] = P * np.arange(BATCH_TILES)[None, :] + p[:, None]
    cst[:, C_J:C_J + STEPS] = np.arange(STEPS)
    cst[:, C_M:C_M + 32] = P * np.arange(32)
    xs = np.arange(SELW)
    sel = np.zeros((P, 4, SELW), np.float32)
    for kb in range(2):
        for slot in range(2):
            sel[:, 2 * kb + slot] = (kb * P + p)[:, None] == xs[None, :] - slot * SK
    sel[KREST:, 2:] = 0

    def T(a):
        return np.ascontiguousarray(np.swapaxes(a, -1, -2))

    def cols(v):
        return np.ascontiguousarray(v.reshape(DC, P).T)

    arrays = {
        "x": np.ascontiguousarray(g["x"]),
        "ctxT": np.ascontiguousarray(g["ctx_1024"].transpose(2, 0, 1)),
        "wqT": T(g["L0_xattn_Wq"]), "bq": cols(g["L0_xattn_bq"]),
        "wkT": T(g["L0_xattn_Wk"]), "bk": cols(g["L0_xattn_bk"]),
        "wvT": T(g["L0_xattn_Wv"]), "bv": np.ascontiguousarray(g["L0_xattn_bv"]),
        "woT": T(g["L0_xattn_Wo"]), "bo": np.ascontiguousarray(g["L0_xattn_bo"]),
        "wr": np.ascontiguousarray(g["L0_ffn_router_w"]), "br": g["L0_ffn_router_b"].reshape(E, 1).copy(),
        "upT": T(g["L0_ffn_expert_up"]), "dnT": T(g["L0_ffn_expert_down"]),
        "cst": cst, "sel": sel,
    }
    nc = bacc.Bacc("TRN2", target_bir_lowering=False, num_devices=1)
    args = [nc.dram_tensor(f"{k}_dram", a.shape, mybir.dt.from_np(a.dtype), kind="ExternalInput").ap() for k, a in arrays.items()]
    out = nc.dram_tensor("out_dram", (B, S, D), F32, kind="ExternalOutput").ap()
    bass_xattn_moe(nc, *args, out)
    r = run_bass_kernel_spmd(nc, [{f"{k}_dram": a for k, a in arrays.items()}], core_ids=[0])
    return r.results[0]["out_dram"]
```

```python
from contextlib import ExitStack

import concourse.bass as bass
from concourse import mybir

P = 128
B, S, D = 4, 1024, 256
SK = 154
H, HD = 16, 16
E, F = 8, 1024
DC = D // P
TOKENS = B * S
TILES = TOKENS // P
PAIRS = TILES // 2
BATCH_TILES = S // P
BATCH_PAIRS = BATCH_TILES // 2
EPS = 1e-5

HALF = H // DC * SK
COLS = H * SK
CHUNKS = -(-COLS // P)
PADDED = CHUNKS * P
GROUPS = [(c, o, n) for c in range(DC) for o, n in ((0, 3), (3, 3), (6, 2))]
SLOTS = 3
TURNS = CHUNKS // 4
VH = HD + 1
VCOLS = 3 * 2 * VH
KREST = SK - P

EW = DC * F + F // P * D
PIECE = 512
PIECES = EW // PIECE
HALF_EXPERT = EW // 2
W_SCALE, X_SCALE, H_SCALE = 64.0, 16.0, 4.0
LIST = TOKENS
BLOCKS = 2 * TOKENS // P + E - 1
GROUP = 4
FULL = (BLOCKS - 3) // GROUP
TABLE = -(-BLOCKS // GROUP) * GROUP
AHEAD = 3
assert FULL * GROUP + AHEAD == BLOCKS
LIST_ROWS = E * LIST + 8 * P
NOBODY = 2.0 * TOKENS
EARLY = 4

C_ID, C_TRI, C_HM, C_DESC, C_BASE, C_TOK, C_J, C_M = 0, 128, 256, 264, 272, 280, 288, 288 + TABLE
C_ALL = C_M + 32
SELW = 282

F32 = mybir.dt.float32
F16 = mybir.dt.float16
BF16 = mybir.dt.bfloat16
I32 = mybir.dt.int32
ALU = mybir.AluOpType
ACT = mybir.ActivationFunctionType
AX = mybir.AxisListType

LN1_STEPS = 3
ROUTE_STEPS = 24
ROUTE_AT = (0, 2, 5, 11, 17)


def bank_uses():
    turned, projected = {(-1, "x"): 0}, {(-1, "q"): 0}
    for p in range(PAIRS + 3):
        late, mid, more = 0 <= p - 2 < PAIRS, 0 <= p - 1 < PAIRS, p + 1 < PAIRS
        for what, there in (("at0", mid), ("n2", late), ("x", more), ("at1", mid)):
            if there:
                turned[p, what] = len(turned)
        projected[p, "first"] = first = len([k for k in projected if k[1] != "first"])
        batch_before = p > 3 and (p - 2) % BATCH_PAIRS == 0
        for what, there in (("count", batch_before), ("out0", mid), ("lg", late), ("lgt", late), ("q", more), ("out1", mid)):
            if there:
                projected[p, what] = first
                first += 1
    return turned, projected


TR_USE, PJ_USE = bank_uses()
FIRST_BODY, LAST_BODY = 2, PAIRS - 3


def tr_use(p, what):
    if isinstance(p, int):
        return TR_USE[p, what]
    return p * 4 + (TR_USE[FIRST_BODY, what] - 4 * FIRST_BODY)


def pj_use(p, b, what):
    if isinstance(p, int):
        return PJ_USE[p, what]
    return p * 5 + b + (PJ_USE[FIRST_BODY, what] - 5 * FIRST_BODY)


def pj_first(p, b, counts):
    return pj_use(p, b, "first") - (1 if counts and not isinstance(p, int) else 0)


def tile_there(t):
    return not isinstance(t, int) or 0 <= t < TILES


def pair_there(p):
    return not isinstance(p, int) or 0 <= p < PAIRS


def bass_xattn_moe(nc, x, ctxT, wqT, bq, wkT, bk, wvT, bv, woT, bo, wr, br, experts, cst_in, sel_in_dram, out):
    with ExitStack() as ctx:
        def sb(name, shape, dt=F32):
            return ctx.enter_context(nc.sbuf_tensor(name, shape, dt))

        def sem(name):
            return ctx.enter_context(nc.semaphore(name))

        n2_dram = nc.dram_tensor("n2_dram", [TOKENS, D], F32, kind="Internal").ap()
        list_dram = nc.dram_tensor("list_dram", [LIST_ROWS, 2], F32, kind="Internal").ap()

        x_tiles = x.rearrange("b (n p) d -> (b n) p d", p=P)
        out_rows = out.rearrange("b s d -> (b s) d")

        W = sb("W", [P, E * EW])
        W16 = W[:].bitcast(F16)
        Vall = W[:, EARLY * EW:EARLY * EW + B * CHUNKS * VCOLS // 2].bitcast(BF16)
        KB = W[:, (EARLY + 1) * EW:(EARLY + 1) * EW + B * COLS]
        rest = W[:, (EARLY + 1) * EW + B * COLS:E * EW]
        wk_sb = rest[:, 0:512].rearrange("p (c n) -> p c n", c=DC)
        wv_sb = rest[:, 512:1024].rearrange("p (c n) -> p c n", c=DC)
        qT = rest[:, 1024:1536].rearrange("p (c t k) -> p c t k", c=DC, t=2)
        q_odd = rest[:, 1536:1792].rearrange("p (c k) -> p c k", c=DC)
        cst = sb("cst", [P, C_ALL])
        ident = cst[:, C_ID:C_ID + P]
        tri = sb("tri", [P, P], BF16)
        ones = sb("ones", [P, P], BF16)
        sel = sb("sel", [P, 4, SELW], BF16)
        wq_sb = sb("wq_sb", [P, DC, D])
        wo_sb = sb("wo_sb", [P, DC, D])
        wr_sb = sb("wr_sb", [P, DC, E])
        bq_sb = sb("bq_sb", [P, DC])
        bk_sb = sb("bk_sb", [P, DC])
        br_sb = sb("br_sb", [E, 1])
        bo_bc = sb("bo_bc", [P, D])
        bv_bc = sb("bv_bc", [P, D])
        vp_flat = sb("vp", [P, 2 * B * 3 * H * VH], BF16)
        vp = vp_flat[:].rearrange("p (w b a h v) -> p w b a h v", w=2, b=B, a=3, h=H)
        Vcur = vp_flat[:, 0:CHUNKS * VCOLS]
        bkm = sb("bkm", [P, H // DC])
        half_pow = sb("half_pow", [P, 2])
        eps = sb("eps", [P, 2])
        gate = sb("gate", [P, 2])
        w_scale = sb("w_scale", [P, 1])

        xt = sb("xt", [P, 2, D])
        xn = sb("xn", [P, 2, D])
        xnT = sb("xnT", [P, 2, DC, P])
        spare = sb("spare", [P, 1])
        st1 = sb("st1", [P, 2, 6])
        mv1 = sb("mv1", [P, 2, 2])
        rs1 = sb("rs1", [P, 2])
        mx = sb("mx", [P, H])
        SX = sb("SX", [P, 2, PADDED])
        hi = sb("hi", [P, PADDED], F16)
        lo = sb("lo", [P, PADDED], F16)
        early = SX[:].rearrange("p s n -> p (s n)")
        ctx_sb = early[:, 0:DC * B * SK].rearrange("p (c b k) -> p c b k", c=DC, b=B)
        sel_f = early[:, 1232:1232 + 4 * SELW].rearrange("p (a x) -> p a x", a=4)
        v_f = hi[:, 0:8 * D].bitcast(F32).rearrange("p (s x) -> p s x", s=2)
        v_r = lo[:, 0:8 * D].bitcast(F32).rearrange("p (s x) -> p s x", s=2)
        filler = early[:, 3600:3600 + 2 * LIST_ROWS // P].rearrange("p (n a) -> p n a", a=2)
        rden = sb("rden", [P, H])
        attn = sb("attn", [P, D])
        atT = sb("atT", [P, DC, P])
        xr = sb("xr", [P, 2, D])
        x2 = sb("x2", [P, 2, D])
        st2 = sb("st2", [P, 6])
        mv2 = sb("mv2", [P, 2])
        rs2 = sb("rs2", [P, 2])
        n2 = sb("n2", [P, 2, D])
        n2T = sb("n2T", [P, DC, 2 * P])
        lgT = sb("lgT", [E, 2 * P])
        Lg = sb("Lg", [P, BATCH_TILES * E])

        T8 = BATCH_TILES
        rt = sb("rt", [P, 8, T8, E])
        rs = sb("rs", [P, 8, T8])
        Mb = sb("Mb", [P, T8, E], BF16)
        cnt = sb("cnt", [P, E])
        tok = sb("tok", [P, T8])
        ent = sb("ent", [P, T8, 2, 2])
        pos = sb("pos", [P, 2, T8], I32)

        meta = sb("meta", [1, 4, TABLE])
        blk = sb("blk", [1, 4, E])
        exw = sb("exw", [1, TABLE], I32)
        off = sb("off", [1, TABLE], I32)
        lst = sb("lst", [P, TABLE, 2])
        idg = sb("idg", [P, GROUP, 1], I32)
        ids = sb("ids", [P, 2, 1], I32)
        xg = hi[:, 0:GROUP * 2 * D].bitcast(F32).rearrange("p (s d) -> p s d", s=GROUP)
        xgT = lo[:, 4 * D:8 * D].rearrange("p (s a c k) -> p s a c k", s=2, a=2, c=DC)
        early_piece = rest[:, 0:2 * PIECE].rearrange("p (s x) -> p s x", s=2)
        scaled_piece = rest[:, 1792:1792 + PIECE]
        late_half = [SX[:, 0, 0:HALF_EXPERT], SX[:, 1, 0:HALF_EXPERT],
                     vp_flat[:, 0:2 * HALF_EXPERT].bitcast(F32)]
        hh = SX[:, :, 0:F]
        hT = [SX[:, t, F:2 * F].bitcast(F16).rearrange("p (a k) -> p a k", a=2) for t in range(2)]
        y = lo[:, 0:4 * D].bitcast(F32).rearrange("p (s d) -> p s d", s=2)

        banks = ctx.enter_context(nc.psum_tensor("banks", [P, 8, 512], F32))
        SC = [banks[:, s, :] for s in range(SLOTS)]
        PT = [banks[:, 3 + s, :] for s in range(2)]
        O = banks[:, 5, :]
        TR = banks[:, 6, :]
        PJ = banks[:, 7, :]
        UP = [[banks[:, 2 * s + u, :] for u in range(2)] for s in range(2)]
        HTp = [banks[:, 4 + s, :] for s in range(2)]
        XTp = banks[:, 6, :]
        Y = banks[:, 7, :]

        cst_in_s = sem("constants_loaded")
        ctx_in = sem("context_and_wk_loaded")
        wv_in = sem("wv_loaded")
        wq_in, wts_in = sem("wq_loaded"), sem("attention_weights_loaded")
        piece_in = [sem("piece_loaded0"), sem("piece_loaded1")]
        piece_step = sem("piece_step")
        half_in = [sem(f"half_expert_loaded{slot}") for slot in range(3)]
        half_hi, half_lo = sem("half_expert_first_part"), sem("half_expert_second_part")
        init_done = sem("constants_made")
        k_ps = sem("k_in_psum")
        bias_done = sem("key_biases_masked")
        KB_act, KB_dve = sem("keys_by_act"), sem("keys_by_dve")
        v_ps = sem("v_in_psum")
        v_add, v_sub, v_last = sem("values_whole"), sem("values_less_first_part"), sem("third_parts")
        v_p0, v_p1 = sem("first_parts"), sem("second_parts")
        sel_in, sel_made = sem("row_picks_loaded"), sem("row_picks_made")
        vsel_ps = sem("chunk_values_in_psum")
        vst_a = sem("chunk_values_by_act")
        vst_d = sem("chunk_values_by_dve")
        list_set = sem("list_filler_made")
        x_loaded = sem("x_loaded")
        ln1_step = sem("ln1_step")
        ln1_rstd = sem("ln1_rstd")
        q_ready = sem("second_tile_queries")
        tr_full, tr_empty = sem("turned_in_psum"), sem("turned_taken")
        pj_full, pj_empty = sem("projected_in_psum"), sem("projected_taken")
        s_full, s_max = sem("scores_in_psum"), sem("score_max")
        exp_done = sem("exp_done")
        pt_full, hi_done, pt_empty = sem("probs_turned"), sem("hi_done"), sem("lo_done")
        values_in = [sem(f"values_in_place{j}") for j in range(TURNS)]
        pv_done = sem("pv_done")
        rden_done, attn_done = sem("denominators"), sem("attn_done")
        xr_loaded = [sem("residual_loaded0"), sem("residual_loaded1")]
        xr_ready = sem("residual_ready")
        ln2_step, ln2_rstd, n2_done = sem("ln2_step"), sem("ln2_rstd"), sem("n2_done")
        x2_stored, n2_stored = sem("x2_stored"), sem("n2_stored")
        lg_done = sem("logits_ready")
        rt_exp = sem("router_exp")
        rt_step = sem("routing_step")
        scattered = sem("lists_filled_and_scattered")
        meta_step = sem("block_table_step")
        gate_step = sem("gate_step")
        lst_loaded = sem("list_rows_loaded")
        idg_ready = sem("rows_to_gather")
        ids_ready = sem("rows_to_add")
        gathered = [sem(f"gathered{s}") for s in range(GROUP)]
        xt_full, xt_hi, xt_lo = sem("tokens_turned"), sem("tokens_first_part"), sem("tokens_second_part")
        up_full, gelu_done = sem("up_in_psum"), sem("gelu_done")
        ht_full, ht_hi, ht_lo = sem("hidden_turned"), sem("hidden_first_part"), sem("hidden_second_part")
        y_full, y_done = sem("down_in_psum"), sem("y_done")
        added = sem("rows_added")

        META_STEPS = 11

        block = ctx.enter_context(nc.Block())

        def piece_parts(i):
            return W16[:, bass.ds(i * (2 * PIECE), PIECE)], W16[:, bass.ds(i * (2 * PIECE) + PIECE, PIECE)]

        HALVES = [(e, h) for e in (*range(EARLY + 1, E), EARLY) for h in range(2)]

        def half_parts(u):
            e, h = HALVES[u]
            at = (2 * e + h) * 2 * HALF_EXPERT
            both = W16[:, at:at + 2 * HALF_EXPERT].rearrange("p (q a x) -> p q a x", a=2, x=PIECE)
            return both[:, :, 0, :], both[:, :, 1, :]

        HALF_SLOT = (0, 1, 2, 0, 1, 2, 0, 1)
        HALF_NTH = [HALF_SLOT[:u].count(slot) for u, slot in enumerate(HALF_SLOT)]

        def in_pieces(v):
            return v.rearrange("p (q x) -> p q x", x=PIECE)

        KBv = KB.rearrange("p (b c h k) -> p b c h k", b=B, c=DC, k=SK)
        Vallv = Vall.rearrange("p (b x) -> p b x", b=B)

        def keys_in_psum(f):
            return banks[:, 2 * f:2 * f + 2, 0:2 * SK].rearrange("p h (b k) -> p h b k", b=2)

        def part(b, a):
            return vp[:, :, b, a, :, 0:HD]

        def heads(v):
            return v.rearrange("p (w h d) -> p w h d", w=2, h=H)

        @block.sync
        def _(sp):
            nc.sync.sem_inc(x2_stored, 32)
            nc.sync.sem_inc(n2_stored, 32)
            sp.dma_start(ctx_sb, ctxT.rearrange("(c p) b k -> p c b k", p=P)).then_inc(ctx_in, 16)
            sp.dma_start(wk_sb, wkT.rearrange("(c p) n -> p c n", p=P)).then_inc(ctx_in, 16)
            sp.dma_start(bk_sb[:], bk).then_inc(ctx_in, 16)
            sp.dma_start(cst[:], cst_in).then_inc(cst_in_s, 16)

            def load_x(p):
                if not pair_there(p):
                    return
                if not isinstance(p, int) or p > 0:
                    sp.wait_ge(ln1_step, LN1_STEPS * p)
                sp.dma_start(xt[:], x_tiles[bass.ds(p * 2, 2)].rearrange("t p d -> p t d")).then_inc(x_loaded, 16)

            load_x(0)
            sp.dma_start(wq_sb[:], wqT.rearrange("(c p) n -> p c n", p=P)).then_inc(wq_in, 16)
            sp.dma_start(bq_sb[:], bq).then_inc(wq_in, 16)
            sp.dma_start(wv_sb, wvT.rearrange("(c p) n -> p c n", p=P)).then_inc(wv_in, 16)
            sp.dma_start(bv_bc[:], bv.unsqueeze(0).broadcast_to([P, D])).then_inc(wv_in, 16)
            sp.dma_start(sel_f, sel_in_dram).then_inc(sel_in, 16)
            sp.dma_start(wo_sb[:], woT.rearrange("(c p) n -> p c n", p=P)).then_inc(wts_in, 16)
            sp.dma_start(wr_sb[:], wr.rearrange("(c p) n -> p c n", p=P)).then_inc(wts_in, 16)
            sp.dma_start(br_sb[:], br).then_inc(wts_in, 16)
            sp.dma_start(bo_bc[:], bo.unsqueeze(0).broadcast_to([P, D])).then_inc(wts_in, 16)

            def load_xr(m, par):
                if not tile_there(m):
                    return
                if not isinstance(m, int) or m > 1:
                    sp.wait_ge(ln2_step, 2 * m - 3)
                sp.dma_start(xr[:, par, :], x_tiles[bass.ds(m, 1)].rearrange("o p d -> p (o d)")).then_inc(xr_loaded[par], 16)

            def store(m, par):
                if not tile_there(m):
                    return
                sp.wait_ge(n2_done, m + 1)
                sp.wait_ge(x2_stored, 16 * m + 32)
                sp.wait_ge(n2_stored, 16 * m + 32)
                sp.dma_start(out_rows[bass.ds(m * P, P)], x2[:, par, :]).then_inc(x2_stored, 16)
                sp.dma_start(n2_dram[bass.ds(m * P, P)], n2[:, par, :]).then_inc(n2_stored, 16)

            def put_values(b, pieces):
                for j in pieces:
                    at = 4 * j * VCOLS
                    if b > 0:
                        sp.wait_ge(pv_done, TURNS * (b * BATCH_TILES - 1) + j + 1)
                    sp.dma_start(Vcur[:, at:at + 4 * VCOLS], Vallv[:, b, at:at + 4 * VCOLS]).then_inc(values_in[j], 16)

            load_x(1)
            sp.wait_ge(v_ps, 2 * B)
            sp.wait_ge(vst_a, CHUNKS // 2)
            sp.wait_ge(vst_d, CHUNKS // 2)
            put_values(0, range(TURNS))

            def load_piece(i, slot):
                if isinstance(i, int) and not 0 <= i < EARLY * PIECES:
                    return
                if not isinstance(i, int) or i > 1:
                    sp.wait_ge(piece_step, 3 * i - 3)
                sp.dma_start(early_piece[:, slot, :], experts[:, bass.ds(i * PIECE, PIECE)]).then_inc(piece_in[slot], 16)

            def body(p):
                first = isinstance(p, int) and 0 < p < PAIRS and p % BATCH_PAIRS == 0
                store(p * 2 - 3, 1)
                load_xr(p * 2 - 1, 1)
                if first:
                    put_values(p // BATCH_PAIRS, range(3))
                load_x(p + 2)
                store(p * 2 - 2, 0)
                load_piece(p * 2, 0)
                load_xr(p * 2, 0)
                if first:
                    put_values(p // BATCH_PAIRS, range(3, TURNS))
                load_piece(p * 2 + 1, 1)

            for p in range(FIRST_BODY):
                body(p)
            with sp.Fori(FIRST_BODY, BATCH_PAIRS) as p:
                body(p)
            for b in range(1, B - 1):
                body(b * BATCH_PAIRS)
                with sp.Fori(b * BATCH_PAIRS + 1, (b + 1) * BATCH_PAIRS) as p:
                    body(p)
            def load_half(u):
                e, h = HALVES[u]
                slot = HALF_SLOT[u]
                if HALF_NTH[u] > 0:
                    before = max(i for i in range(u) if HALF_SLOT[i] == slot)
                    sp.wait_ge(half_lo, before + 1)
                elif slot < 2:
                    sp.wait_ge(pt_full, TURNS * (TILES - 1 + slot))
                else:
                    sp.wait_ge(pv_done, TURNS * TILES)
                at = (2 * e + h) * HALF_EXPERT
                sp.dma_start(late_half[slot], experts[:, at:at + HALF_EXPERT]).then_inc(half_in[slot], 16)

            for p in range((B - 1) * BATCH_PAIRS, PAIRS + 2):
                if p == PAIRS:
                    load_half(0)
                if p == PAIRS + 1:
                    load_half(1)
                    load_half(2)
                body(p)
            for u in range(3, len(HALVES)):
                load_half(u)

            sp.wait_ge(meta_step, META_STEPS)

            def load_rows(g):
                if not isinstance(g, int) or g > 0:
                    sp.wait_ge(idg_ready, GROUP * (g - 1) + 1)
                starts = [sp.value_load(off[0:1, bass.ds(g * GROUP + j, 1)], min_val=0, max_val=LIST_ROWS - P) for j in range(GROUP)]
                if isinstance(g, int) and g == 0:
                    sp.wait_ge(scattered, 16 * 2 * TILES + 16)
                for j, v in enumerate(starts):
                    t = g * GROUP + j
                    sp.dma_start(lst[:, bass.ds(t, 1), :].rearrange("p o a -> p (o a)"), list_dram[bass.ds(v, P)]).then_inc(lst_loaded, 16)

            load_rows(0)
            with sp.Fori(1, TABLE // GROUP) as g:
                load_rows(g)
            sp.wait_ge(x2_stored, 16 * (TILES + 2))
            sp.wait_ge(n2_stored, 16 * (TILES + 2))
            sp.wait_ge(added, 16 * BLOCKS)

        @block.gpsimd
        def _(pool):
            nc.gpsimd.memset(half_pow[:], -0.5).then_inc(init_done, 1)
            nc.gpsimd.memset(eps[:], EPS).then_inc(init_done, 1)
            nc.gpsimd.memset(w_scale[:], W_SCALE)
            nc.gpsimd.memset(gate[:], 0.0).then_inc(init_done, 1)
            nc.gpsimd.sem_inc(gate_step, 1)
            nc.gpsimd.memset(filler[:, :, 0], NOBODY).then_inc(list_set, 1)
            nc.gpsimd.memset(filler[:, :, 1], 0.0).then_inc(list_set, 1)
            pool.wait_ge(list_set, 2)
            pool.dma_start(list_dram.rearrange("(p n) a -> p n a", p=P), filler).then_inc(scattered, 16)
            pool.wait_ge(scattered, 16)
            pool.wait_ge(init_done, 3)

            def gate_op(nth):
                pool.wait_ge(gate_step, nth + 1)
                nc.gpsimd.tensor_tensor(gate[:, 1:2], gate[:, 0:1], gate[:, 0:1], ALU.add).then_inc(gate_step, 1)

            def rstd1(p):
                pool.wait_ge(ln1_step, LN1_STEPS * p + 2)
                nc.gpsimd.tensor_tensor(rs1[:], mv1[:, :, 1], eps[:], ALU.add).then_inc(ln1_rstd, 1)
                pool.wait_ge(ln1_rstd, 2 * p + 1)
                nc.gpsimd.tensor_tensor(rs1[:], rs1[:], half_pow[:], ALU.pow).then_inc(ln1_rstd, 1)

            def residual(m, par, nth):
                pool.wait_ge(xr_loaded[par], 16 * (nth + 1))
                nc.gpsimd.tensor_tensor(xr[:, par, :], xr[:, par, :], bo_bc[:], ALU.add).then_inc(xr_ready, 1)

            def rstd2(m):
                pool.wait_ge(ln2_step, 2 * m + 2)
                nc.gpsimd.tensor_tensor(rs2[:, 0:1], mv2[:, 1:2], eps[:, 0:1], ALU.add).then_inc(ln2_rstd, 1)
                pool.wait_ge(ln2_rstd, 2 * m + 1)
                nc.gpsimd.tensor_tensor(rs2[:, 1:2], rs2[:, 0:1], half_pow[:, 0:1], ALU.pow).then_inc(ln2_rstd, 1)

            def scatter(b, part):
                pool.wait_ge(rt_step, ROUTE_STEPS * (b + 1) + 1)
                gate_op(b * 4 + part)
                for t in range(part * T8 // 4, (part + 1) * T8 // 4):
                    for k in range(2):
                        pool.indirect_dma_start(
                            out=list_dram, out_offset=bass.IndirectOffsetOnAxis(ap=pos[:, k, t:t + 1], axis=0),
                            in_=ent[:, t, k, :], in_offset=None).then_inc(scattered, 16)

            def take_piece(i, slot, nth):
                if isinstance(i, int) and not 0 <= i < EARLY * PIECES:
                    return
                G = nc.gpsimd.tensor_tensor
                first, second = piece_parts(i)
                scale = w_scale[:].broadcast_to([P, PIECE])
                if not isinstance(i, int) or i > 0:
                    pool.wait_ge(piece_step, 3 * i)
                pool.wait_ge(piece_in[slot], 16 * (nth + 1))
                G(scaled_piece, early_piece[:, slot, :], scale, ALU.mult).then_inc(piece_step, 1)
                G(first, early_piece[:, slot, :], scale, ALU.mult).then_inc(piece_step, 1)
                pool.wait_ge(piece_step, 3 * i + 2)
                G(second, scaled_piece, first, ALU.subtract).then_inc(piece_step, 1)

            rstd1(0)
            pool.wait_ge(sel_made, 1)
            pool.wait_ge(v_ps, 2 * B)
            nc.gpsimd.memset(SX[:, 1, COLS:PADDED], 0.0).then_inc(init_done, 1)
            nc.gpsimd.memset(SX[:, 0, COLS:PADDED], 0.0).then_inc(init_done, 1)
            pool.wait_ge(init_done, 5)
            pool.wait_ge(wts_in, 64)

            def body(p, routed=None, parts=()):
                for par in range(2):
                    m = p * 2 - 2 + par
                    if par == 0 and pair_there(p + 1):
                        rstd1(p + 1)
                    if tile_there(m):
                        residual(m, par, p - 1)
                    if parts:
                        scatter(routed, parts[par])
                    if tile_there(m):
                        rstd2(m)
                    take_piece(p * 2 - 2 + par, par, p - 1)

            for p in range(FIRST_BODY):
                body(p)
            with pool.Fori(FIRST_BODY, FIRST_BODY + BATCH_PAIRS) as p:
                body(p)
            with pool.Fori(1, B - 1) as b:
                p = b * BATCH_PAIRS + FIRST_BODY
                body(p, b - 1, (0, 1))
                body(p + 1, b - 1, (2, 3))
                with pool.Fori(2, BATCH_PAIRS) as j:
                    body(p + j)
            body(LAST_BODY + 1, B - 2, (0, 1))
            body(LAST_BODY + 2, B - 2, (2, 3))
            body(LAST_BODY + 3)
            for part in range(4):
                scatter(B - 1, part)

            pool.wait_ge(n2_stored, 16 * (TILES + 2))
            pool.wait_ge(x2_stored, 16 * (TILES + 2))
            pool.wait_ge(pv_done, TURNS * TILES)

            def gather(t, j, count):
                pool.wait_ge(idg_ready, t + 1)
                if not isinstance(t, int) or t >= GROUP:
                    pool.wait_ge(xt_full, t - GROUP + 1)
                gate_op(count)
                pool.indirect_dma_start(
                    out=xg[:, j, :], out_offset=None, in_=n2_dram,
                    in_offset=bass.IndirectOffsetOnAxis(ap=idg[:, j, :], axis=0)).then_inc(gathered[j], 16)

            def add_rows(t, j, count):
                pool.wait_ge(y_done, t + 1)
                pool.wait_ge(ids_ready, t + 1)
                if not isinstance(t, int) or t > 0:
                    pool.wait_ge(added, 16 * t)
                gate_op(count)
                pool.indirect_dma_start(
                    out=out_rows, out_offset=bass.IndirectOffsetOnAxis(ap=ids[:, j % 2, :], axis=0),
                    in_=y[:, j % 2, :], in_offset=None, bounds_check=TOKENS - 1, oob_is_err=False,
                    compute_op=ALU.add).then_inc(added, 16)

            for t in range(AHEAD):
                gather(t, t, 4 * B + t)

            def group(g):
                for j in range(GROUP):
                    t = g * GROUP + j
                    gather(t + AHEAD, (j + AHEAD) % GROUP, 4 * B + AHEAD + 2 * t)
                    add_rows(t, j, 4 * B + AHEAD + 2 * t + 1)

            group(0)
            with pool.Fori(1, FULL) as g:
                group(g)
            for t in range(FULL * GROUP, BLOCKS):
                add_rows(t, t % GROUP, 4 * B + t + BLOCKS)

        @block.tensor
        def _(pe):
            mm = nc.tensor.matmul
            pe.wait_ge(ctx_in, 48)
            for f in range(DC):
                for h in range(2):
                    for c in range(DC):
                        last = mm(banks[:, 2 * f + h, 0:2 * SK], wk_sb[:, c, f * P:(f + 1) * P],
                                  ctx_sb[:, c, 2 * h:2 * h + 2, :], start=c == 0, stop=c == DC - 1)
                    last.then_inc(k_ps, 1)
            def values(b):
                for kb in range(2):
                    for c in range(DC):
                        last = mm(banks[:, 4 + b, kb * D:(kb + 1) * D], ctx_sb[:, c, b, kb * KREST:kb * KREST + P],
                                  wv_sb[:, c, :], start=c == 0, stop=c == DC - 1)
                    last.then_inc(v_ps, 1)

            def pick_values():
                pe.wait_ge(v_last, B)
                pe.wait_ge(sel_made, 1)
                pe.wait_ge(KB_act, H // 2)
                pe.wait_ge(KB_dve, H // 2)
                for c in range(CHUNKS):
                    if c >= 4:
                        pe.wait_ge(vst_a if c % 2 == 0 else vst_d, c // 2 - 1)
                    h0, k0 = divmod(P * c, SK)
                    for slot in range(2):
                        h = min(h0 + slot, H - 1)
                        o = banks[:, c % 4, 0:B * VCOLS].rearrange("p (b a s v) -> p b a s v", b=B, a=3, s=2)[:, :, :, slot, :]
                        for kb in range(2):
                            last = mm(o, sel[:, 2 * kb + slot, k0:k0 + P], vp[:, kb, :, :, h, :],
                                      start=kb == 0 and slot == 0, stop=kb == 1, skip_group_check=True)
                    last.then_inc(vsel_ps, 1)

            def turn_x(p, use):
                pe.wait_ge(ln1_step, LN1_STEPS * (p + 1))
                pe.wait_ge(tr_empty, use)
                for t in range(2):
                    for c in range(DC):
                        last = nc.tensor.transpose(TR[:, (2 * t + c) * P:(2 * t + c + 1) * P],
                                                   xn[:, t, c * P:(c + 1) * P], ident)
                last.then_inc(tr_full, 1)

            def project_q(tr, use):
                pe.wait_ge(tr_empty, tr + 1)
                pe.wait_ge(pj_empty, use)
                for f in range(DC):
                    for c in range(DC):
                        last = mm(PJ[:, f * 2 * P:(f + 1) * 2 * P], wq_sb[:, c, f * P:(f + 1) * P],
                                  xnT[:, :, c, :], start=c == 0, stop=c == DC - 1, skip_group_check=True)
                last.then_inc(pj_full, 1)

            def scores(n, p, par, g):
                if not tile_there(n):
                    return
                c, h, w = GROUPS[g]
                if n is not 0 or g >= SLOTS:
                    pe.wait_ge(exp_done, 6 * n + g - 2)
                mm(SC[g % SLOTS][:, 0:w * SK], qT[:, c, par, :],
                   KB[:, bass.ds((p // BATCH_PAIRS) * COLS + (c * HALF + h * SK), w * SK)],
                   start=True, stop=True).then_inc(s_full, 1)

            def turn_probs(k, par, j):
                if not tile_there(k):
                    return
                heads = min(-(-(j + 1) * 4 * P // SK), H)
                groups = min(g + 1 for g, (c, o, n) in enumerate(GROUPS) if c * (H // DC) + o + n >= heads)
                pe.wait_ge(exp_done, 6 * k + groups)
                if not isinstance(k, int) or k > 0 or j > 1:
                    pe.wait_ge(pt_empty, TURNS * k + j - 1)
                for c in range(4):
                    last = nc.tensor.transpose(PT[(par + j) % 2][:, c * P:(c + 1) * P],
                                               SX[:, par, (4 * j + c) * P:(4 * j + c + 1) * P], ident)
                last.then_inc(pt_full, 1)

            def weigh(k, par, pair, j):
                if not tile_there(k):
                    return
                if not isinstance(pair, int) or pair % BATCH_PAIRS == 0:
                    pe.wait_ge(values_in[j], (pair // BATCH_PAIRS) * 16 + 16)
                pe.wait_ge(pt_empty, TURNS * k + j + 1)
                if j == 0 and (not isinstance(k, int) or k > 0):
                    pe.wait_ge(attn_done, k)
                for c in range(4 * j, 4 * j + 4):
                    h0 = P * c // SK
                    w = VH if h0 == H - 1 else 2 * VH
                    for n, (probs, part) in enumerate(((hi, 0), (hi, 1), (hi, 2), (lo, 0), (lo, 1))):
                        at = c * VCOLS + part * 2 * VH
                        last = mm(O[:, h0 * VH:h0 * VH + w], probs[:, c * P:(c + 1) * P],
                                  Vcur[:, at:at + w], start=c == 0 and n == 0,
                                  stop=c == CHUNKS - 1 and n == 4, skip_group_check=True)
                last.then_inc(pv_done, 1)

            def turn_attn(m, use):
                pe.wait_ge(attn_done, m + 1)
                pe.wait_ge(tr_empty, use)
                for c in range(DC):
                    last = nc.tensor.transpose(TR[:, c * P:(c + 1) * P], attn[:, c * P:(c + 1) * P], ident)
                last.then_inc(tr_full, 1)

            def project_out(tr, use):
                pe.wait_ge(tr_empty, tr + 1)
                pe.wait_ge(pj_empty, use)
                for c in range(DC):
                    last = mm(PJ[:, 0:D], atT[:, c, :], wo_sb[:, c, :], start=c == 0, stop=c == DC - 1)
                last.then_inc(pj_full, 1)

            def turn_n2(p, use):
                pe.wait_ge(n2_done, 2 * p + 2)
                pe.wait_ge(tr_empty, use)
                for par in range(2):
                    for c in range(DC):
                        last = nc.tensor.transpose(TR[:, (2 * par + c) * P:(2 * par + c + 1) * P], n2[:, par, c * P:(c + 1) * P], ident)
                last.then_inc(tr_full, 1)

            def logits(tr, use):
                pe.wait_ge(tr_empty, tr + 1)
                pe.wait_ge(pj_empty, use)
                for c in range(DC):
                    last = mm(PJ[0:E, 0:2 * P], wr_sb[:, c, :], n2T[:, c, :], start=c == 0, stop=c == DC - 1)
                last.then_inc(pj_full, 1)

            def turn_logits():
                for t in range(2):
                    last = nc.tensor.transpose(PJ[:, t * E:(t + 1) * E], lgT[:, t * P:(t + 1) * P], ident[0:E, 0:E])
                last.then_inc(pj_full, 1)

            def count_experts(b, use):
                pe.wait_ge(rt_step, ROUTE_STEPS * b + 18)
                pe.wait_ge(pj_empty, use)
                mm(PJ[:, 0:T8 * E], tri[:], Mb[:].rearrange("p t e -> p (t e)"), start=True, stop=False, skip_group_check=True)
                for t in range(T8):
                    last = mm(PJ[:, (t + 1) * E:(T8 + 1) * E].rearrange("p (t e) -> p t e", e=E), ones[:],
                              Mb[:, t, :].unsqueeze(1).broadcast_to([P, T8 - t, E]),
                              start=False, stop=t == T8 - 1, skip_group_check=True)
                last.then_inc(pj_full, 1)

            def tick(p, par, b, counts=False):
                n = p * 2 + par
                k, m = n - 1, n - 2
                k_pair, m_pair = (p if par else p - 1), p - 1
                late, mid, more = pair_there(p - 2), tile_there(m), pair_there(p + 1)
                for g in range(6):
                    scores(n, p, par, g)
                    if g == 4 and mid:
                        project_out(tr_use(p, f"at{par}"), pj_use(p, b, f"out{par}"))
                    if g < TURNS:
                        turn_probs(k, 1 - par, g)
                    if g == 1 and par == 1 and late:
                        pe.wait_ge(pj_empty, pj_use(p, b, "lgt"))
                    if g < 2:
                        weigh(m, par, m_pair, g + 3)
                    elif g < TURNS:
                        weigh(k, 1 - par, k_pair, g - 2)
                    if g == 1 and counts:
                        count_experts(b - 1, pj_first(p, b, counts))
                    if g == 2 and mid:
                        turn_attn(m, tr_use(p, f"at{par}"))
                    if g == 3 and par == 0 and late:
                        turn_n2(p - 2, tr_use(p, "n2"))
                    if g == 5 and par == 0 and late:
                        logits(tr_use(p, "n2"), pj_use(p, b, "lg"))
                    if g == 0 and par == 1 and more:
                        turn_x(p + 1, tr_use(p, "x"))
                    if g == 1 and par == 1 and late:
                        turn_logits()
                    if g == 2 and par == 1 and more:
                        project_q(tr_use(p, "x"), pj_use(p, b, "q"))

            def body(p, b, counts=False):
                if pair_there(p):
                    pe.wait_ge(pj_empty, pj_first(p, b, counts) - (1 if p is not 0 else 0))
                tick(p, 0, b, counts)
                if pair_there(p):
                    pe.wait_ge(q_ready, p + 1)
                tick(p, 1, b)

            pe.wait_ge(wv_in, 32)
            values(0)
            values(1)
            pe.wait_ge(cst_in_s, 16)
            turn_x(0, 0)
            pe.wait_ge(wq_in, 32)
            project_q(0, 0)
            pe.wait_ge(tr_empty, 1)
            values(2)
            pe.wait_ge(pj_empty, 1)
            values(3)
            pe.wait_ge(wts_in, 64)
            pick_values()
            pe.wait_ge(pj_empty, 1)
            pe.wait_ge(vst_a, CHUNKS // 2)
            pe.wait_ge(vst_d, CHUNKS // 2)
            pe.wait_ge(init_done, 5)
            for p in range(FIRST_BODY):
                body(p, 0)
            with pe.Fori(FIRST_BODY, FIRST_BODY + BATCH_PAIRS - 1) as p:
                body(p, 0)
            with pe.Fori(0, B - 2) as b:
                p = b * BATCH_PAIRS + (FIRST_BODY + BATCH_PAIRS - 1)
                body(p, b)
                body(p + 1, b + 1, counts=True)
                with pe.Fori(2, BATCH_PAIRS) as j:
                    body(p + j, b + 1)
            for p in range(LAST_BODY, PAIRS + 2):
                body(p, (p - 2) // BATCH_PAIRS, counts=p == LAST_BODY + 1)
            count_experts(B - 1, pj_use(PAIRS + 2, B, "count"))

            pe.wait_ge(pj_empty, pj_use(PAIRS + 2, B, "count") + 1)
            pe.wait_ge(meta_step, META_STEPS)
            pe.wait_ge(piece_step, 3 * EARLY * PIECES)
            pe.wait_ge(half_lo, len(HALVES))

            PRODUCTS = ((0, 0), (0, 1), (1, 0))

            def turn_tokens(t, j, g):
                pe.wait_ge(gathered[j], 16 * (g + 1))
                if not isinstance(t, int) or t > 0:
                    pe.wait_ge(xt_lo, t)
                for c in range(DC):
                    last = nc.tensor.transpose(XTp[:, c * P:(c + 1) * P], xg[:, j, c * P:(c + 1) * P], ident)
                last.then_inc(xt_full, 1)

            def up(t, par):
                v = pe.value_load(exw[0:1, bass.ds(t, 1)], min_val=0, max_val=(E - 1) * 2 * EW)
                pe.wait_ge(xt_lo, t + 1)
                if not isinstance(t, int) or t > 1:
                    pe.wait_ge(gelu_done, 2 * (t - 1))
                for u in range(2):
                    for c in range(DC):
                        at = (2 * c + u) * 2 * PIECE
                        for n, (xa, wa) in enumerate(PRODUCTS):
                            last = mm(UP[par][u], xgT[:, par, xa, c, :], W16[:, bass.ds(v + (at + wa * PIECE), PIECE)],
                                      start=c == 0 and n == 0, stop=c == DC - 1 and n == 2)
                    last.then_inc(up_full, 1)
                return v

            def turn_hidden(t, par):
                for u in range(2):
                    pe.wait_ge(gelu_done, 2 * t + u + 1)
                    if not isinstance(t, int) or t > 0:
                        pe.wait_ge(ht_lo, 2 * t + u - 1)
                    for c in range(4):
                        k = 4 * u + c
                        last = nc.tensor.transpose(HTp[u][:, c * P:(c + 1) * P], hh[:, par, k * P:(k + 1) * P], ident)
                    last.then_inc(ht_full, 1)

            def down(t, par):
                v = pe.value_load(exw[0:1, bass.ds(t, 1)], min_val=0, max_val=(E - 1) * 2 * EW)
                for k in range(F // P):
                    if k == 0:
                        pe.wait_ge(ht_lo, 2 * t + 1)
                        if not isinstance(t, int) or t > 0:
                            pe.wait_ge(y_done, t)
                    if k == 4:
                        pe.wait_ge(ht_lo, 2 * t + 2)
                    at = (4 + k // 2) * 2 * PIECE + k % 2 * D
                    for n, (ha, wa) in enumerate(PRODUCTS):
                        last = mm(Y[:, 0:D], hT[par][:, ha, k * P:(k + 1) * P], W16[:, bass.ds(v + (at + wa * PIECE), D)],
                                  start=k == 0 and n == 0, stop=k == F // P - 1 and n == 2)
                last.then_inc(y_full, 1)

            def step(t, j, g, turn=True, more=True):
                turn_hidden(t, j % 2)
                if more:
                    up(t + 1, (j + 1) % 2)
                if turn:
                    turn_tokens(t + 2, (j + 2) % GROUP, g + (j + 2) // GROUP)
                down(t, j % 2)

            turn_tokens(0, 0, 0)
            up(0, 0)
            turn_tokens(1, 1, 0)
            for j in range(GROUP):
                step(j, j, 0)
            with pe.Fori(1, FULL) as g:
                for j in range(GROUP):
                    step(g * GROUP + j, j, g)
            for t in range(FULL * GROUP, BLOCKS):
                step(t, t % GROUP, FULL, turn=t + 2 < BLOCKS, more=t + 1 < BLOCKS)

        @block.scalar
        def _(act):
            A = nc.scalar.activation
            def take_xnT(tr, before):
                act.wait_ge(tr_full, tr + 1)
                if before is not None:
                    act.wait_ge(pj_full, before)
                A(xnT[:], TR[:].rearrange("p (t c k) -> p t c k", t=2, c=DC), ACT.Copy).then_inc(tr_empty, 1)

            def take_q(p, pj):
                act.wait_ge(pj_full, pj + 1)
                for f in range(DC):
                    A(qT[:, f, 0, :], PJ[:, f * 2 * P:f * 2 * P + P], ACT.Identity, bias=bq_sb[:, f:f + 1])
                    last = A(q_odd[:, f, :], PJ[:, f * 2 * P + P:(f + 1) * 2 * P], ACT.Identity, bias=bq_sb[:, f:f + 1])
                last.then_inc(pj_empty, 1)

            def take_q_odd(p, made):
                act.wait_ge(pj_empty, made)
                if not isinstance(p, int) or p > 0:
                    act.wait_ge(s_full, 12 * p)
                A(qT[:, :, 1, :], q_odd, ACT.Copy).then_inc(q_ready, 1)

            def expo(n, par, g):
                if not tile_there(n):
                    return
                c, o, w = GROUPS[g]
                act.wait_ge(s_max, 6 * n + g + 1)
                for h in range(w):
                    head = c * (H // DC) + o + h
                    last = A(SX[:, par, head * SK:(head + 1) * SK], SC[g % SLOTS][:, h * SK:(h + 1) * SK], ACT.Exp,
                             bias=mx[:, head:head + 1], scale=-1.0)
                last.then_inc(exp_done, 1)

            def take_hi(k, par, j):
                if not tile_there(k):
                    return
                act.wait_ge(pt_full, TURNS * k + j + 1)
                if not isinstance(k, int) or k > 0:
                    act.wait_ge(pv_done, TURNS * (k - 1) + j + 1)
                A(hi[:, j * 4 * P:(j + 1) * 4 * P], PT[(par + j) % 2], ACT.Copy).then_inc(hi_done, 1)

            def take_atT(tr, before):
                act.wait_ge(tr_full, tr + 1)
                act.wait_ge(pj_full, before)
                A(atT[:], TR[:, 0:D].rearrange("p (c k) -> p c k", c=DC), ACT.Copy).then_inc(tr_empty, 1)

            def take_n2T(tr, before):
                act.wait_ge(tr_full, tr + 1)
                act.wait_ge(pj_full, before)
                A(n2T[:].rearrange("p c (t k) -> p t c k", t=2), TR[:].rearrange("p (t c k) -> p t c k", t=2, c=DC), ACT.Copy).then_inc(tr_empty, 1)

            def take_lgT(pj):
                act.wait_ge(pj_full, pj + 1)
                A(lgT[:], PJ[0:E, 0:2 * P], ACT.Identity, bias=br_sb[:, 0:1]).then_inc(pj_empty, 1)

            def take_lg(pj, b, j):
                act.wait_ge(pj_full, pj + 1)
                act.wait_ge(rt_step, ROUTE_STEPS * b + 1)
                A(Lg[:, bass.ds(j * 2 * E, 2 * E)], PJ[:, 0:2 * E], ACT.Copy).then_inc(pj_empty, 1)

            def router_exp(b):
                act.wait_ge(rt_step, ROUTE_STEPS * b + 3)
                A(rt[:, 1], rt[:, 0], ACT.Exp).then_inc(rt_exp, 1)

            def tick(p, par, b, j, routes=False, counts=False):
                n = p * 2 + par
                k, m = n - 1, n - 2
                late, mid, more = pair_there(p - 2), tile_there(m), pair_there(p + 1)
                before = pj_first(p, b, counts)
                if par == 0 and pair_there(p):
                    take_q_odd(p, before if isinstance(p, int) else before - 1)
                for g in range(6):
                    if g == 3 and mid:
                        take_atT(tr_use(p, f"at{par}"), pj_use(p, b, "out0") + 1 if par else before)
                    if g == 3 and routes:
                        router_exp(b)
                    if g == 3 and par == 1 and more:
                        take_q(p + 1, pj_use(p, b, "q"))
                    if g < TURNS:
                        take_hi(k, 1 - par, g)
                    if g == 1 and par == 1 and late:
                        take_lg(pj_use(p, b, "lgt"), b, j)
                    expo(n, par, g)
                    if g == 5 and par == 0 and late:
                        take_lgT(pj_use(p, b, "lg"))
                    if g == 3 and par == 0 and late:
                        take_n2T(tr_use(p, "n2"), before)
                    if g == 0 and par == 1 and more:
                        take_xnT(tr_use(p, "x"), before)

            def body(p, b, j, routes=False, counts=False):
                for par in range(2):
                    tick(p, par, b, j, routes and par == 1, counts)

            def first_part(u):
                if u == 0:
                    act.wait_ge(s_full, 6 * TILES)
                if u == 4:
                    act.wait_ge(piece_step, 3 * EARLY * PIECES)
                if u == 6:
                    act.wait_ge(pv_done, TURNS * TILES)
                act.wait_ge(half_in[HALF_SLOT[u]], 16 * (HALF_NTH[u] + 1))
                A(half_parts(u)[0], in_pieces(late_half[HALF_SLOT[u]]), ACT.Copy, scale=W_SCALE).then_inc(half_hi, 1)

            act.wait_ge(bias_done, 1)
            act.wait_ge(k_ps, 2)
            for h in range(H // DC):
                A(KBv[:, :, 0, h, :].rearrange("p (a b) k -> p a b k", a=2), keys_in_psum(0), ACT.Identity, bias=bkm[:, h:h + 1],
                  scale=cst[:, C_HM + h:C_HM + h + 1]).then_inc(KB_act, 1)
            take_xnT(0, None)
            act.wait_ge(wq_in, 32)
            take_q(0, 0)
            for b in range(B + 1):
                if b < B:
                    act.wait_ge(v_add, b + 1)
                    A(part(b, 0), heads(v_f[:, b % 2]), ACT.Copy).then_inc(v_p0, 1)
                if b > 0:
                    act.wait_ge(v_sub, b)
                    A(part(b - 1, 1), heads(v_r[:, (b - 1) % 2]), ACT.Copy).then_inc(v_p1, 1)
            act.wait_ge(wts_in, 64)
            for c in range(0, CHUNKS, 2):
                act.wait_ge(vsel_ps, c + 1)
                A(Vallv[:, :, c * VCOLS:(c + 1) * VCOLS], banks[:, c % 4, 0:B * VCOLS].rearrange("p (b x) -> p b x", b=B), ACT.Copy).then_inc(vst_a, 1)
            for p in range(FIRST_BODY):
                body(p, 0, 0)
            with act.Fori(0, BATCH_PAIRS - 1) as j:
                body(j + FIRST_BODY, 0, j)
            with act.Fori(0, B - 2) as b:
                p = b * BATCH_PAIRS + (FIRST_BODY + BATCH_PAIRS - 1)
                body(p, b, BATCH_PAIRS - 1, routes=True)
                body(p + 1, b + 1, 0, counts=True)
                with act.Fori(2, BATCH_PAIRS) as j:
                    body(p + j, b + 1, j - 1)
            for p in range(LAST_BODY, PAIRS + 2):
                body(p, (p - 2) // BATCH_PAIRS, (p - 2) % BATCH_PAIRS, routes=p in (LAST_BODY, PAIRS + 1), counts=p == LAST_BODY + 1)

            for u in range(len(HALVES)):
                first_part(u)

            def take_xgT(t, par):
                act.wait_ge(xt_full, t + 1)
                if not isinstance(t, int) or t > 1:
                    act.wait_ge(up_full, 2 * (t - 1))
                A(xgT[:, par, 0], XTp[:, 0:D].rearrange("p (c k) -> p c k", c=DC), ACT.Copy, scale=X_SCALE).then_inc(xt_hi, 1)

            def gelu(t, par):
                for u in range(2):
                    act.wait_ge(up_full, 2 * t + u + 1)
                    if u == 0 and (not isinstance(t, int) or t > 1):
                        act.wait_ge(ht_full, 2 * (t - 1))
                    A(hh[:, par, u * 512:(u + 1) * 512], UP[par][u], ACT.Gelu, scale=1 / (X_SCALE * W_SCALE)).then_inc(gelu_done, 1)

            def take_hT(t, par):
                for u in range(2):
                    act.wait_ge(ht_full, 2 * t + u + 1)
                    if u == 0 and (not isinstance(t, int) or t > 1):
                        act.wait_ge(y_full, t - 1)
                    A(hT[par][:, 0, u * 512:(u + 1) * 512], HTp[u], ACT.Copy, scale=H_SCALE).then_inc(ht_hi, 1)

            take_xgT(0, 0)
            gelu(0, 0)
            take_xgT(1, 1)

            def step(t, par):
                take_hT(t, par)
                gelu(t + 1, 1 - par)
                take_xgT(t + 2, par)

            step(0, 0)
            step(1, 1)
            with act.Fori(1, (BLOCKS - 3) // 2) as s:
                step(s * 2, 0)
                step(s * 2 + 1, 1)
            step(BLOCKS - 3, 0)
            take_hT(BLOCKS - 2, 1)
            gelu(BLOCKS - 1, 0)
            take_hT(BLOCKS - 1, 0)

        @block.vector
        def _(dve):
            V = nc.vector
            V.sem_inc(rt_step, 1)
            def ln1_stats(p, t):
                dve.wait_ge(x_loaded, 16 * p + 16)
                last = V.bn_stats(st1[:, t, :], xt[:, t, :])
                if t == 1:
                    last.then_inc(ln1_step, 1)

            def ln1_aggr(p):
                V.bn_aggr(mv1[:, 0, :], st1[:, 0, :])
                V.bn_aggr(mv1[:, 1, :], st1[:, 1, :]).then_inc(ln1_step, 1)

            def ln1_apply(p, turned):
                dve.wait_ge(ln1_rstd, 2 * p + 2)
                if turned is not None:
                    dve.wait_ge(tr_full, turned)
                for t in range(2):
                    last = V.tensor_scalar(xn[:, t, :], xt[:, t, :], mv1[:, t, 0:1], rs1[:, t:t + 1], ALU.subtract, ALU.mult)
                last.then_inc(ln1_step, 1)

            def take_max(n, g):
                if not tile_there(n):
                    return
                c, h, w = GROUPS[g]
                h = c * (H // DC) + h
                dve.wait_ge(s_full, 6 * n + g + 1)
                V.tensor_reduce(mx[:, h:h + w], SC[g % SLOTS][:, 0:w * SK].rearrange("p (h k) -> p h k", k=SK), AX.X, ALU.min).then_inc(s_max, 1)

            def take_lo(k, par, j):
                if not tile_there(k):
                    return
                dve.wait_ge(hi_done, TURNS * k + j + 1)
                if not isinstance(k, int) or k > 0:
                    dve.wait_ge(pv_done, TURNS * (k - 1) + j + 1)
                at = slice(j * 4 * P, (j + 1) * 4 * P)
                V.tensor_tensor(lo[:, at], PT[(par + j) % 2], hi[:, at], ALU.subtract).then_inc(pt_empty, 1)

            def normalise(k, turned):
                Ov = O[:, 0:H * VH].rearrange("p (h v) -> p h v", v=VH)
                dve.wait_ge(pv_done, TURNS * (k + 1))
                V.reciprocal(rden[:], Ov[:, :, HD]).then_inc(rden_done, 1)
                if turned is not None:
                    dve.wait_ge(tr_full, turned)
                dve.wait_ge(rden_done, k + 1)
                V.tensor_tensor(attn[:].rearrange("p (h d) -> p h d", h=H), Ov[:, :, 0:HD],
                                rden[:].unsqueeze(2).broadcast_to([P, H, HD]), ALU.mult).then_inc(attn_done, 1)

            def add_residual(m, par, pj):
                dve.wait_ge(pj_full, pj + 1)
                dve.wait_ge(xr_ready, m + 1)
                dve.wait_ge(x2_stored, 16 * m + 16)
                V.tensor_tensor(x2[:, par, :], PJ[:, 0:D], xr[:, par, :], ALU.add).then_inc(pj_empty, 1)

            def ln2_stats(m, par, pj):
                dve.wait_ge(pj_empty, pj + 1)
                V.bn_stats(st2[:], x2[:, par, :]).then_inc(ln2_step, 1)

            def ln2_aggr(m):
                V.bn_aggr(mv2[:], st2[:]).then_inc(ln2_step, 1)

            def ln2_apply(m, par, turned):
                dve.wait_ge(ln2_rstd, 2 * m + 2)
                if turned is not None:
                    dve.wait_ge(tr_full, turned)
                dve.wait_ge(n2_stored, 16 * m + 16)
                V.tensor_scalar(n2[:, par, :], x2[:, par, :], mv2[:, 0:1], rs2[:, 1:2], ALU.subtract, ALU.mult).then_inc(n2_done, 1)

            def tick(p, par, b, routes=False, counts=False):
                n = p * 2 + par
                k, m = n - 1, n - 2
                more, mid = par == 0 and pair_there(p + 1), tile_there(m)
                for g in range(6):
                    take_max(n, g)
                    if g == 1 and mid:
                        before = None if m is 0 else tr_use(p, "at0") + 1 if par else tr_use(p - 1, "at1") + 1
                        normalise(m, before)
                    if g == 4 and mid:
                        add_residual(m, par, pj_use(p, b, f"out{par}"))
                    if g == 5 and mid:
                        dve.wait_ge(ln2_step, 2 * m + 1)
                        sums_waited()
                        ln2_aggr(m)
                    if g < TURNS:
                        take_lo(k, 1 - par, g)
                    if g == 4 and mid:
                        ln2_stats(m, par, pj_use(p, b, f"out{par}"))
                    if g == 0 and tile_there(n - 3):
                        if par:
                            turned = tr_use(p, "n2") + 1 if pair_there(p - 2) else None
                        else:
                            turned = tr_use(p - 1, "n2") + 1 if pair_there(p - 3) else None
                        ln2_apply(n - 3, 1 - par, turned)
                    if g in (1, 2) and more:
                        ln1_stats(p + 1, g - 1)
                    if g == 3 and more:
                        dve.wait_ge(ln1_step, LN1_STEPS * (p + 1) + 1)
                        sums_waited()
                        ln1_aggr(p + 1)
                    if g == 5 and more:
                        ln1_apply(p + 1, tr_use(p - 1, "x") + 1)
                    if routes and g > 1:
                        route(b, g - 2, lg=pj_use(p, b, "lgt"))
                    if counts and g == 2:
                        route(b - 1, 4, count=pj_first(p, b, counts))

            def body(p, b, routes=False, counts=False):
                for par in range(2):
                    tick(p, par, b, routes and par == 1, counts and par == 0)

            def second_part(u):
                dve.wait_ge(half_hi, u + 1)
                first, second = half_parts(u)
                V.scalar_tensor_tensor(second, in_pieces(late_half[HALF_SLOT[u]]), W_SCALE, first, ALU.mult, ALU.subtract).then_inc(half_lo, 1)

            def route(b, part, lg=None, count=None):
                steps = ROUTE_AT[part]

                def link(ins):
                    nonlocal steps
                    steps += 1
                    ins.then_inc(rt_step, 1)
                    dve.wait_ge(rt_step, ROUTE_STEPS * b + steps + 1)

                def over_e(v):
                    return v.unsqueeze(2).broadcast_to([P, T8, E])

                def over_t(v):
                    return v.unsqueeze(1).broadcast_to([P, T8, E])

                less, prob, pick, best, second, left, row = (rt[:, a] for a in range(7))
                top, total, inv, w1, first_at, w2 = (rs[:, a] for a in range(6))
                desc = cst[:, C_DESC:C_DESC + E]
                L = Lg[:].rearrange("p (t e) -> p t e", e=E)
                if part == 0:
                    dve.wait_ge(pj_empty, lg + 1)
                    link(V.tensor_reduce(top, L, AX.X, ALU.max))
                    link(V.tensor_tensor(less, L, over_e(top), ALU.subtract))
                if part == 1:
                    dve.wait_ge(rt_exp, b + 1)
                    link(V.tensor_reduce(total, prob, AX.X, ALU.add))
                    link(V.reciprocal(inv, total))
                    link(V.tensor_tensor(prob, prob, over_e(inv), ALU.mult))
                if part in (2, 3):
                    p_, w, one = ((prob, w1, best), (left, w2, second))[part - 2]
                    link(V.tensor_reduce(w, p_, AX.X, ALU.max))
                    link(V.tensor_tensor(pick, p_, over_e(w), ALU.is_equal))
                    link(V.tensor_tensor(pick, pick, over_t(desc), ALU.mult))
                    link(V.tensor_reduce(first_at, pick, AX.X, ALU.max))
                    link(V.tensor_tensor(one, pick, over_e(first_at), ALU.is_equal))
                    if part == 2:
                        link(V.scalar_tensor_tensor(left, best, -2.0, prob, ALU.mult, ALU.add))
                    else:
                        link(V.tensor_tensor(Mb[:], best, second, ALU.add))
                if part == 4:
                    dve.wait_ge(pj_full, count + 1)
                    link(V.tensor_tensor(row, PJ[:, 0:T8 * E].rearrange("p (t e) -> p t e", e=E), over_t(cnt[:]), ALU.add))
                    V.tensor_tensor(cnt[:], cnt[:], PJ[:, T8 * E:(T8 + 1) * E], ALU.add).then_inc(pj_empty, 1)
                    link(V.tensor_tensor(row, row, over_t(cst[:, C_BASE:C_BASE + E]), ALU.add))
                    dve.wait_ge(scattered, 16 * 2 * T8 * b + 16)
                    for k, one in enumerate((best, second)):
                        link(V.tensor_tensor(pick, one, row, ALU.mult))
                        link(V.tensor_reduce(rs[:, 6 + k], pick, AX.X, ALU.add))
                    V.tensor_copy(pos[:], rs[:, 6:8])
                    for k, w in enumerate((w1, w2)):
                        V.tensor_copy(ent[:, :, k, 0], tok[:])
                        V.tensor_copy(ent[:, :, k, 1], w)
                    link(V.tensor_scalar(tok[:], tok[:], float(S), None, ALU.add))
                assert steps == (ROUTE_AT + (ROUTE_STEPS,))[part + 1], steps

            def sums_waited():
                V.tensor_tensor(spare[:], eps[:, 0:1], eps[:, 0:1], ALU.add)

            V.memset(ones[:], 1.0)
            V.memset(cnt[:], 0.0)
            for w in range(2):
                V.memset(vp[:, w, :, 0, :, HD:VH], 1.0)
                V.memset(vp[:, w, :, 1, :, HD:VH], 0.0)
                V.memset(vp[:, w, :, 2, :, HD:VH], 0.0)
            dve.wait_ge(cst_in_s, 16)
            dve.wait_ge(ctx_in, 48)
            mask = cst[:, C_HM:C_HM + H // DC]
            V.tensor_scalar(bkm[:], mask, bk_sb[:, 0:1], None, ALU.mult).then_inc(bias_done, 1)
            V.tensor_copy(tri[:], cst[:, C_TRI:C_TRI + P])
            V.tensor_copy(tok[:], cst[:, C_TOK:C_TOK + T8])
            ln1_stats(0, 0)
            ln1_stats(0, 1)
            dve.wait_ge(ln1_step, 1)
            ln1_aggr(0)
            ln1_apply(0, None)
            dve.wait_ge(k_ps, 2 * DC)
            for h in range(H // DC):
                V.tensor_scalar(KBv[:, :, 1, h, :].rearrange("p (a b) k -> p a b k", a=2), keys_in_psum(1),
                                bk_sb[:, 1:2], mask[:, h:h + 1], ALU.add, ALU.mult).then_inc(KB_dve, 1)
            dve.wait_ge(sel_in, 16)
            V.tensor_copy(sel[:], sel_f).then_inc(sel_made, 1)
            dve.wait_ge(wv_in, 32)
            for b in range(B + 2):
                if b < B:
                    dve.wait_ge(v_ps, 2 * b + 2)
                    if b > 1:
                        dve.wait_ge(v_sub, b - 1)
                    V.tensor_tensor(v_f[:, b % 2].rearrange("p (w d) -> p w d", w=2), banks[:, 4 + b, :].rearrange("p (w d) -> p w d", w=2),
                                    bv_bc[:].unsqueeze(1).broadcast_to([P, 2, D]), ALU.add).then_inc(v_add, 1)
                if 0 < b <= B:
                    dve.wait_ge(v_p0, b)
                    if b > 2:
                        dve.wait_ge(v_last, b - 2)
                    V.tensor_tensor(heads(v_r[:, (b - 1) % 2]), heads(v_f[:, (b - 1) % 2]), part(b - 1, 0), ALU.subtract).then_inc(v_sub, 1)
                if b > 1:
                    dve.wait_ge(v_p1, b - 1)
                    V.tensor_tensor(part(b - 2, 2), heads(v_r[:, b % 2]), part(b - 2, 1), ALU.subtract).then_inc(v_last, 1)
            for c in range(1, CHUNKS, 2):
                dve.wait_ge(vsel_ps, c + 1)
                V.tensor_copy(Vallv[:, :, c * VCOLS:(c + 1) * VCOLS], banks[:, c % 4, 0:B * VCOLS].rearrange("p (b x) -> p b x", b=B)).then_inc(vst_d, 1)
            dve.wait_ge(init_done, 5)
            for p in range(FIRST_BODY):
                body(p, 0)
            with dve.Fori(FIRST_BODY, FIRST_BODY + BATCH_PAIRS - 1) as p:
                body(p, 0)
            with dve.Fori(0, B - 2) as b:
                p = b * BATCH_PAIRS + (FIRST_BODY + BATCH_PAIRS - 1)
                body(p, b, routes=True)
                body(p + 1, b + 1, counts=True)
                with dve.Fori(2, BATCH_PAIRS) as j:
                    body(p + j, b + 1)
            for p in range(LAST_BODY, PAIRS + 2):
                body(p, (p - 2) // BATCH_PAIRS, routes=p in (LAST_BODY, PAIRS + 1), counts=p == LAST_BODY + 1)
            route(B - 1, 4, count=pj_use(PAIRS + 2, B, "count"))

            for u in range(3):
                second_part(u)

            steps = 0

            def link(ins):
                nonlocal steps
                steps += 1
                ins.then_inc(meta_step, 1)
                dve.wait_ge(meta_step, steps)

            row0 = hi[0:1, :].bitcast(F32)
            past = row0[:, 0:TABLE * (E - 1)].rearrange("p (j e) -> p j e", e=E - 1)
            past_n = row0[:, 512:512 + TABLE * (E - 1)].rearrange("p (j e) -> p j e", e=E - 1)
            over = row0[:, 1024:1024 + E * 32].rearrange("p (e m) -> p e m", e=E)
            blocks, ends, unit = (blk[0:1, a, :] for a in range(3))
            expert, start, within = (meta[0:1, a, :] for a in range(3))
            js = cst[0:1, C_J:C_J + TABLE]
            V.memset(unit, 1.0)
            link(V.tensor_tensor(over, cnt[0:1, :].unsqueeze(2).broadcast_to([1, E, 32]),
                                 cst[0:1, C_M:C_M + 32].unsqueeze(1).broadcast_to([1, E, 32]), ALU.is_gt))
            link(V.tensor_reduce(blocks, over, AX.X, ALU.add))
            link(V.tensor_tensor_scan(ends, unit, blocks, 0.0, ALU.mult, ALU.add))
            link(V.tensor_tensor(past, js.unsqueeze(2).broadcast_to([1, TABLE, E - 1]),
                                 ends[:, 0:E - 1].unsqueeze(1).broadcast_to([1, TABLE, E - 1]), ALU.is_ge))
            link(V.tensor_reduce(expert, past, AX.X, ALU.add))
            link(V.tensor_tensor(past_n, past, blocks[:, 0:E - 1].unsqueeze(1).broadcast_to([1, TABLE, E - 1]), ALU.mult))
            link(V.tensor_reduce(start, past_n, AX.X, ALU.add))
            link(V.tensor_scalar(exw[:], expert, float(2 * EW), None, ALU.mult))
            link(V.tensor_tensor(within, js, start, ALU.subtract))
            link(V.tensor_scalar(within, within, float(P), None, ALU.mult))
            link(V.scalar_tensor_tensor(off[:], expert, float(LIST), within, ALU.mult, ALU.add))
            assert steps == META_STEPS

            for u in range(3, len(HALVES)):
                second_part(u)

            def rows_to_gather(t, j, g):
                dve.wait_ge(lst_loaded, 16 * GROUP * (g + 1))
                if not isinstance(g, int) or g > 0:
                    dve.wait_ge(gathered[j], 16 * g)
                V.tensor_scalar(idg[:, j, :], lst[:, bass.ds(t, 1), 0], float(TOKENS - 1), None, ALU.min).then_inc(idg_ready, 1)

            def rows_to_add(t, par):
                if not isinstance(t, int) or t > 1:
                    dve.wait_ge(added, 16 * (t - 1))
                V.tensor_scalar(ids[:, par, :], lst[:, bass.ds(t, 1), 0], 0.0, None, ALU.max).then_inc(ids_ready, 1)

            def take_xgT(t, par):
                dve.wait_ge(xt_hi, t + 1)
                V.scalar_tensor_tensor(xgT[:, par, 1], XTp[:, 0:D].rearrange("p (c k) -> p c k", c=DC), X_SCALE,
                                       xgT[:, par, 0], ALU.mult, ALU.subtract).then_inc(xt_lo, 1)

            def take_hT(t, par):
                for u in range(2):
                    dve.wait_ge(ht_hi, 2 * t + u + 1)
                    of = slice(u * 512, (u + 1) * 512)
                    V.scalar_tensor_tensor(hT[par][:, 1, of], HTp[u], H_SCALE, hT[par][:, 0, of], ALU.mult, ALU.subtract).then_inc(ht_lo, 1)

            def take_y(t, par):
                dve.wait_ge(y_full, t + 1)
                if not isinstance(t, int) or t > 1:
                    dve.wait_ge(added, 16 * (t - 1))
                V.tensor_scalar(y[:, par, :], Y[:, 0:D], lst[:, bass.ds(t, 1), 1], 1 / (H_SCALE * W_SCALE), ALU.mult, ALU.mult).then_inc(y_done, 1)

            for t in range(AHEAD):
                rows_to_gather(t, t, 0)
            take_xgT(0, 0)
            take_xgT(1, 1)

            def group(g):
                for j in range(GROUP):
                    t = g * GROUP + j
                    rows_to_gather(t + AHEAD, (j + AHEAD) % GROUP, g + (j + AHEAD) // GROUP)
                    take_hT(t, j % 2)
                    rows_to_add(t, j % 2)
                    take_xgT(t + 2, j % 2)
                    take_y(t, j % 2)

            group(0)
            with dve.Fori(1, FULL) as g:
                group(g)
            for t in range(FULL * GROUP, BLOCKS):
                take_hT(t, t % 2)
                rows_to_add(t, t % 2)
                if t + 2 < BLOCKS:
                    take_xgT(t + 2, t % 2)
                take_y(t, t % 2)


def kernel(**inputs):
    import numpy as np
    import concourse.bacc as bacc
    from concourse.bass_utils import run_bass_kernel_spmd

    g = {k: np.asarray(v) for k, v in inputs.items()}
    cst = np.zeros((P, C_ALL), np.float32)
    p = np.arange(P)
    cst[:, C_ID:C_ID + P] = np.eye(P)
    cst[:, C_TRI:C_TRI + P] = p[:, None] < p[None, :]
    cst[:, C_HM:C_HM + H // DC] = (p[:, None] // HD == np.arange(H // DC)[None, :]) * -HD ** -0.5
    cst[:, C_DESC:C_DESC + E] = E - np.arange(E)
    cst[:, C_BASE:C_BASE + E] = LIST * np.arange(E)
    cst[:, C_TOK:C_TOK + BATCH_TILES] = P * np.arange(BATCH_TILES)[None, :] + p[:, None]
    cst[:, C_J:C_J + TABLE] = np.arange(TABLE)
    cst[:, C_M:C_M + 32] = P * np.arange(32)
    xs = np.arange(SELW)
    sel = np.zeros((P, 4, SELW), np.float32)
    for kb in range(2):
        for slot in range(2):
            sel[:, 2 * kb + slot] = (kb * KREST + p)[:, None] == xs[None, :] - slot * SK
    sel[:P - KREST, 2:] = 0

    def T(a):
        return np.ascontiguousarray(np.swapaxes(a, -1, -2))

    def cols(v):
        return np.ascontiguousarray(v.reshape(DC, P).T)

    up, dn = T(g["L0_ffn_expert_up"]), T(g["L0_ffn_expert_down"])
    up = up.reshape(E, DC, P, F).transpose(2, 0, 1, 3).reshape(P, E, DC * F)
    dn = dn.reshape(E, F // P, P, D).transpose(2, 0, 1, 3).reshape(P, E, F // P * D)
    experts = np.concatenate([up, dn], axis=2).reshape(P, E * EW)

    arrays = {
        "x": np.ascontiguousarray(g["x"]),
        "ctxT": np.ascontiguousarray(g["ctx_1024"].transpose(2, 0, 1)),
        "wqT": T(g["L0_xattn_Wq"]), "bq": cols(g["L0_xattn_bq"]),
        "wkT": T(g["L0_xattn_Wk"]), "bk": cols(g["L0_xattn_bk"]),
        "wvT": T(g["L0_xattn_Wv"]), "bv": np.ascontiguousarray(g["L0_xattn_bv"]),
        "woT": T(g["L0_xattn_Wo"]), "bo": np.ascontiguousarray(g["L0_xattn_bo"]),
        "wr": np.ascontiguousarray(g["L0_ffn_router_w"]), "br": g["L0_ffn_router_b"].reshape(E, 1).copy(),
        "experts": experts,
        "cst": cst, "sel": sel,
    }
    nc = bacc.Bacc("TRN2", target_bir_lowering=False, num_devices=1)
    args = [nc.dram_tensor(f"{k}_dram", a.shape, mybir.dt.from_np(a.dtype), kind="ExternalInput").ap() for k, a in arrays.items()]
    out = nc.dram_tensor("out_dram", (B, S, D), F32, kind="ExternalOutput").ap()
    bass_xattn_moe(nc, *args, out)
    r = run_bass_kernel_spmd(nc, [{f"{k}_dram": a for k, a in arrays.items()}], core_ids=[0])
    return r.results[0]["out_dram"]
```
